# Optimizing a Trainium2 kernel written in Bass

```python
import numpy as np
import jax
import jax.numpy as jnp

def _softmax(x, axis=-1):
    return jax.nn.softmax(x, axis=axis)

def _gelu(x):
    return jax.nn.gelu(x, approximate=True)

def _silu(x):
    return jax.nn.silu(x)

def _sigmoid(x):
    return jax.nn.sigmoid(x)

def _layernorm(x, axis=-1, eps=1e-05):
    m = jnp.mean(x, axis=axis, keepdims=True)
    v = jnp.var(x, axis=axis, keepdims=True)
    return (x - m) / jnp.sqrt(v + eps)

def _scatter_add(tgt, idx, src, axis=0):
    return tgt.at[idx].add(src)

def _segment_sum(src, seg, n):
    return jax.ops.segment_sum(src, seg, n)
kernel_name = 'mk_xattn_ffn_d2_seqx_r4_a27e50'

def setup_inputs(seed: int=0):
    np.random.seed(seed)
    _w = jnp.asarray

    def _rec_inputs():
        import jax
        import jax.numpy as jnp
        _rk = jax.random.key(seed)
        x = 7.22e-05 + 1 * jax.random.normal(jax.random.fold_in(_rk, 1), (8, 256, 256), jnp.float32)
        _lenS = 256 - jax.random.randint(jax.random.fold_in(_rk, 7), (8,), 0, max(1, 256 // 4) + 1, jnp.int32)
        _lenS2 = 256 - jax.random.randint(jax.random.fold_in(_rk, 8), (8,), 0, max(1, 256 // 4) + 1, jnp.int32)
        _ctx_1024P = jax.random.normal(jax.random.fold_in(_rk, 11), (8, 16, 256), jnp.float32)
        _ctx_1024c = jax.random.dirichlet(jax.random.fold_in(_rk, 511), 0.3 * jnp.ones((16,), jnp.float32), (8, 256))
        _ctx_1024t = jnp.einsum('bsk,bkd->bsd', _ctx_1024c, _ctx_1024P)
        _ctx_1024t = _ctx_1024t * jax.lax.rsqrt(jnp.mean(jnp.square(_ctx_1024t)) + 1e-12) * 0.953939
        ctx_1024 = 4.13588e-05 + 0.999923 * (_ctx_1024t + 0.3 * jax.random.normal(jax.random.fold_in(_rk, 611), (8, 256, 256), jnp.float32))
        _validS = jnp.arange(256)[None, :] < _lenS[:, None]
        _validS2 = jnp.arange(256)[None, :] < _lenS2[:, None]
        _causal = jnp.tril(jnp.ones((256, 256), dtype=bool))
        mask_Bx1xSxS2_bf1 = jnp.ones((8, 1, 256, 256), dtype=bool)
        return (x, ctx_1024, mask_Bx1xSxS2_bf1)
    x, ctx_1024, mask_Bx1xSxS2_bf1 = _rec_inputs()

    def _L0_xattn_setup():
        import jax, jax.numpy as jnp
        import numpy as np
        D_MODEL = 256
        NUM_HEADS = 16
        HEAD_DIM = D_MODEL // NUM_HEADS
        key = jax.random.key(seed)
        ks = jax.random.split(key, 12)
        B, S = (4, 512)
        inp = {'query': jax.random.normal(ks[0], (B, S, D_MODEL), jnp.float32), 'key': jax.random.normal(ks[1], (B, S, D_MODEL), jnp.float32), 'value': jax.random.normal(ks[2], (B, S, D_MODEL), jnp.float32), 'mask': jnp.ones((B, 1, S, S), dtype=bool)}
        sc = 1.0 / np.sqrt(D_MODEL)
        inp['Wq'] = jax.random.normal(ks[3], (D_MODEL, D_MODEL), jnp.float32) * sc
        inp['bq'] = jnp.zeros((D_MODEL,), jnp.float32)
        inp['Wk'] = jax.random.normal(ks[4], (D_MODEL, D_MODEL), jnp.float32) * sc
        inp['bk'] = jnp.zeros((D_MODEL,), jnp.float32)
        inp['Wv'] = jax.random.normal(ks[5], (D_MODEL, D_MODEL), jnp.float32) * sc
        inp['bv'] = jnp.zeros((D_MODEL,), jnp.float32)
        inp['Wo'] = jax.random.normal(ks[6], (D_MODEL, D_MODEL), jnp.float32) * sc
        inp['bo'] = jnp.zeros((D_MODEL,), jnp.float32)
        return inp
    _L0_xattn_all = _L0_xattn_setup()
    _L0_xattn_in = {k: v for k, v in _L0_xattn_all.items() if k in ('Wq', 'bq', 'Wk', 'bk', 'Wv', 'bv', 'Wo', 'bo')}
    del _L0_xattn_all

    def _L0_ffn_setup():
        import jax, jax.numpy as jnp
        import numpy as np
        NUM_EXPERTS = 8
        EXPERT_CAPACITY = 2.0
        key = jax.random.key(seed)
        k1, k2, k3, k4 = jax.random.split(key, 4)
        B, T, C, H, E = (4, 1024, 256, 1024, NUM_EXPERTS)
        x = jax.random.normal(k1, (B, T, C), jnp.float32)
        gate_w = jax.random.normal(k2, (C, E), jnp.float32) * 0.02
        w1 = jax.random.normal(k3, (E, C, H), jnp.float32) * 0.02
        w2 = jax.random.normal(k4, (E, H, C), jnp.float32) * 0.02
        return {'x': x, 'gate_w': gate_w, 'w1': w1, 'w2': w2}
    _L0_ffn_all = _L0_ffn_setup()
    _L0_ffn_in = {k: v for k, v in _L0_ffn_all.items() if k in ('gate_w', 'w1', 'w2')}
    del _L0_ffn_all

    def _L1_xattn_setup():
        import jax, jax.numpy as jnp
        import numpy as np
        D_MODEL = 256
        N_HEADS = 16
        D_K = D_MODEL // N_HEADS
        key = jax.random.key(seed)
        ks = jax.random.split(key, 12)
        B, S, D = (2, 512, D_MODEL)
        lim = 1.0 / np.sqrt(D)

        def lin(k):
            kw, kb = jax.random.split(k)
            W = jax.random.uniform(kw, (D, D), jnp.float32, -lim, lim)
            b = jax.random.uniform(kb, (D,), jnp.float32, -lim, lim)
            return (W, b)
        wq, bq = lin(ks[0])
        wk, bk = lin(ks[1])
        wv, bv = lin(ks[2])
        wo, bo = lin(ks[3])
        return {'query': jax.random.normal(ks[4], (B, S, D), jnp.float32), 'key': jax.random.normal(ks[5], (B, S, D), jnp.float32), 'value': jax.random.normal(ks[6], (B, S, D), jnp.float32), 'wq': wq, 'bq': bq, 'wk': wk, 'bk': bk, 'wv': wv, 'bv': bv, 'wo': wo, 'bo': bo, 'time_decay': jnp.float32(0.1)}
    _L1_xattn_all = _L1_xattn_setup()
    _L1_xattn_in = {k: v for k, v in _L1_xattn_all.items() if k in ('wq', 'bq', 'wk', 'bk', 'wv', 'bv', 'wo', 'bo', 'time_decay')}
    del _L1_xattn_all

    def _L1_ffn_setup():
        import jax, jax.numpy as jnp
        import numpy as np
        D_MODEL = 256
        N_HEADS = 16
        HEAD_DIM = D_MODEL // N_HEADS
        FFN_DIM = 1024
        N_EXPERTS = 8
        CAP_FRAC = 0.25
        MOE_TOKEN_DROPOUT = 0.2
        LN_EPS = 1e-05
        B, S = (4, 128)

        def _layer_norm(x, g, b):
            mu = x.mean(-1, keepdims=True)
            var = ((x - mu) ** 2).mean(-1, keepdims=True)
            return (x - mu) * jax.lax.rsqrt(var + LN_EPS) * g + b

        def _self_attention(x, wq, bq, wk, bk, wv, bv, wo, bo):
            b, s, d = x.shape
            q = ((x @ wq + bq) * HEAD_DIM ** (-0.5)).reshape(b, s, N_HEADS, HEAD_DIM)
            k = (x @ wk + bk).reshape(b, s, N_HEADS, HEAD_DIM)
            v = (x @ wv + bv).reshape(b, s, N_HEADS, HEAD_DIM)
            scores = jnp.einsum('bqhd,bkhd->bhqk', q, k)
            p = jax.nn.softmax(scores, axis=-1)
            o = jnp.einsum('bhqk,bkhd->bqhd', p, v).reshape(b, s, d)
            return o @ wo + bo

        def _moe_ffn(x, wr, w1, b1, w2, b2):
            T, D = x.shape
            C = int(np.ceil(CAP_FRAC * T))
            logits = x @ wr
            probs = jax.nn.softmax(logits, axis=-1)
            top1 = jnp.argmax(probs, axis=-1)
            m1 = jax.nn.one_hot(top1, N_EXPERTS, dtype=x.dtype)
            top2 = jnp.argmax(jnp.where(m1 > 0, -jnp.inf, logits), axis=-1)
            m2 = jax.nn.one_hot(top2, N_EXPERTS, dtype=x.dtype)
            loc1 = jnp.cumsum(m1, axis=0) - 1.0
            loc2 = jnp.cumsum(m2, axis=0) - 1.0 + m1.sum(0, keepdims=True)
            m1 = m1 * (loc1 < C)
            m2 = m2 * (loc2 < C)
            t1 = (probs * m1).sum(-1)
            t2 = (probs * m2).sum(-1)
            denom = jnp.maximum(t1 + t2, jnp.finfo(x.dtype).eps)
            t1, t2 = (t1 / denom, t2 / denom)
            tok = jnp.arange(T)
            s1 = loc1[tok, top1].astype(jnp.int32)
            s2 = loc2[tok, top2].astype(jnp.int32)
            v1 = m1[tok, top1] > 0
            v2 = m2[tok, top2] > 0
            s1 = jnp.where(v1, s1, C)
            s2 = jnp.where(v2, s2, C)
            buf = jnp.zeros((N_EXPERTS, C, D), x.dtype)
            buf = buf.at[top1, s1].set(x, mode='drop')
            buf = buf.at[top2, s2].set(x, mode='drop')
            h = jax.nn.relu(jnp.einsum('ecd,edf->ecf', buf, w1) + b1[:, None, :])
            y = (jnp.einsum('ecf,efd->ecd', h, w2) + b2[:, None, :]) * (1.0 - MOE_TOKEN_DROPOUT)
            y1 = y[top1, jnp.minimum(s1, C - 1)]
            y2 = y[top2, jnp.minimum(s2, C - 1)]
            g1 = t1 * v1
            g2 = t2 * v2
            return g1[:, None] * y1 + g2[:, None] * y2
        key = jax.random.key(seed)
        ks = jax.random.split(key, 20)

        def w(k, shape, scale=0.02):
            return jax.random.normal(k, shape, jnp.float32) * scale
        return {'x': jax.random.normal(ks[0], (B, S, D_MODEL), jnp.float32), 'wq': w(ks[1], (D_MODEL, D_MODEL)), 'bq': w(ks[2], (D_MODEL,)), 'wk': w(ks[3], (D_MODEL, D_MODEL)), 'bk': w(ks[4], (D_MODEL,)), 'wv': w(ks[5], (D_MODEL, D_MODEL)), 'bv': w(ks[6], (D_MODEL,)), 'wo': w(ks[7], (D_MODEL, D_MODEL)), 'bo': w(ks[8], (D_MODEL,)), 'ln1_g': 1.0 + w(ks[9], (D_MODEL,)), 'ln1_b': w(ks[10], (D_MODEL,)), 'ln2_g': 1.0 + w(ks[11], (D_MODEL,)), 'ln2_b': w(ks[12], (D_MODEL,)), 'wr': w(ks[13], (D_MODEL, N_EXPERTS)), 'w1': w(ks[14], (N_EXPERTS, D_MODEL, FFN_DIM)), 'b1': w(ks[15], (N_EXPERTS, FFN_DIM)), 'w2': w(ks[16], (N_EXPERTS, FFN_DIM, D_MODEL)), 'b2': w(ks[17], (N_EXPERTS, D_MODEL))}
    _L1_ffn_all = _L1_ffn_setup()
    _L1_ffn_in = {k: v for k, v in _L1_ffn_all.items() if k in ('wq', 'bq', 'wk', 'bk', 'wv', 'bv', 'wo', 'bo', 'ln1_g', 'ln1_b', 'ln2_g', 'ln2_b', 'wr', 'w1', 'b1', 'w2', 'b2')}
    del _L1_ffn_all
    return {'x': x, 'ctx_1024': ctx_1024, 'mask_Bx1xSxS2_bf1': mask_Bx1xSxS2_bf1, 'L0_xattn_Wq': _L0_xattn_in['Wq'], 'L0_xattn_bq': _L0_xattn_in['bq'], 'L0_xattn_Wk': _L0_xattn_in['Wk'], 'L0_xattn_bk': _L0_xattn_in['bk'], 'L0_xattn_Wv': _L0_xattn_in['Wv'], 'L0_xattn_bv': _L0_xattn_in['bv'], 'L0_xattn_Wo': _L0_xattn_in['Wo'], 'L0_xattn_bo': _L0_xattn_in['bo'], 'L0_ffn_gate_w': _L0_ffn_in['gate_w'], 'L0_ffn_w1': _L0_ffn_in['w1'], 'L0_ffn_w2': _L0_ffn_in['w2'], 'L1_xattn_wq': _L1_xattn_in['wq'], 'L1_xattn_bq': _L1_xattn_in['bq'], 'L1_xattn_wk': _L1_xattn_in['wk'], 'L1_xattn_bk': _L1_xattn_in['bk'], 'L1_xattn_wv': _L1_xattn_in['wv'], 'L1_xattn_bv': _L1_xattn_in['bv'], 'L1_xattn_wo': _L1_xattn_in['wo'], 'L1_xattn_bo': _L1_xattn_in['bo'], 'L1_xattn_time_decay': _L1_xattn_in['time_decay'], 'L1_ffn_wq': _L1_ffn_in['wq'], 'L1_ffn_bq': _L1_ffn_in['bq'], 'L1_ffn_wk': _L1_ffn_in['wk'], 'L1_ffn_bk': _L1_ffn_in['bk'], 'L1_ffn_wv': _L1_ffn_in['wv'], 'L1_ffn_bv': _L1_ffn_in['bv'], 'L1_ffn_wo': _L1_ffn_in['wo'], 'L1_ffn_bo': _L1_ffn_in['bo'], 'L1_ffn_ln1_g': _L1_ffn_in['ln1_g'], 'L1_ffn_ln1_b': _L1_ffn_in['ln1_b'], 'L1_ffn_ln2_g': _L1_ffn_in['ln2_g'], 'L1_ffn_ln2_b': _L1_ffn_in['ln2_b'], 'L1_ffn_wr': _L1_ffn_in['wr'], 'L1_ffn_w1': _L1_ffn_in['w1'], 'L1_ffn_b1': _L1_ffn_in['b1'], 'L1_ffn_w2': _L1_ffn_in['w2'], 'L1_ffn_b2': _L1_ffn_in['b2']}

def reference(x, ctx_1024, mask_Bx1xSxS2_bf1, L0_xattn_Wq, L0_xattn_bq, L0_xattn_Wk, L0_xattn_bk, L0_xattn_Wv, L0_xattn_bv, L0_xattn_Wo, L0_xattn_bo, L0_ffn_gate_w, L0_ffn_w1, L0_ffn_w2, L1_xattn_wq, L1_xattn_bq, L1_xattn_wk, L1_xattn_bk, L1_xattn_wv, L1_xattn_bv, L1_xattn_wo, L1_xattn_bo, L1_xattn_time_decay, L1_ffn_wq, L1_ffn_bq, L1_ffn_wk, L1_ffn_bk, L1_ffn_wv, L1_ffn_bv, L1_ffn_wo, L1_ffn_bo, L1_ffn_ln1_g, L1_ffn_ln1_b, L1_ffn_ln2_g, L1_ffn_ln2_b, L1_ffn_wr, L1_ffn_w1, L1_ffn_b1, L1_ffn_w2, L1_ffn_b2):
    import jax
    import jax.numpy as jnp

    def _L0_xattn_ref(query, key, value, mask, Wq, bq, Wk, bk, Wv, bv, Wo, bo):
        import jax, jax.numpy as jnp
        import numpy as np
        D_MODEL = 256
        NUM_HEADS = 16
        HEAD_DIM = D_MODEL // NUM_HEADS
        B, S, _ = query.shape
        H, hd = (NUM_HEADS, HEAD_DIM)

        def proj(x, W, b):
            return (x @ W + b).reshape(B, S, H, hd).transpose(0, 2, 1, 3)
        q = proj(query, Wq, bq)
        k = proj(key, Wk, bk)
        v = proj(value, Wv, bv)
        scores = jnp.einsum('bhqd,bhkd->bhqk', q, k) / jnp.sqrt(jnp.float32(hd))
        scores = jnp.where(mask, scores, jnp.float32(-jnp.inf))
        attn = jax.nn.softmax(scores, axis=-1)
        ctx = jnp.einsum('bhqk,bhkd->bhqd', attn, v)
        ctx = ctx.transpose(0, 2, 1, 3).reshape(B, S, H * hd)
        return ctx @ Wo + bo

    def _L0_ffn_ref(x, gate_w, w1, w2):
        import jax, jax.numpy as jnp
        import numpy as np
        NUM_EXPERTS = 8
        EXPERT_CAPACITY = 2.0
        B, T, C = x.shape
        E = gate_w.shape[1]
        cap = int(EXPERT_CAPACITY * T / E)
        scores = jnp.einsum('BTC,CE->BTE', x, gate_w)
        probs = jax.nn.softmax(scores, axis=-1)
        probs_et = jnp.transpose(probs, (0, 2, 1))
        top_p, top_idx = jax.lax.top_k(probs_et, cap)
        xin = jnp.take_along_axis(x[:, None, :, :], top_idx[..., None], axis=2)
        h = jax.nn.gelu(jnp.einsum('BElC,ECH->BElH', xin, w1), approximate=False)
        y = jnp.einsum('BElH,EHC->BElC', h, w2)
        y = y * top_p[..., None]
        b_idx = jnp.arange(B)[:, None, None]
        out = jnp.zeros((B, T, C), x.dtype).at[b_idx, top_idx].add(y)
        return out

    def _L1_xattn_ref(query, key, value, wq, bq, wk, bk, wv, bv, wo, bo, time_decay):
        import jax, jax.numpy as jnp
        import numpy as np
        D_MODEL = 256
        N_HEADS = 16
        D_K = D_MODEL // N_HEADS
        B, S, D = query.shape
        H, Dk = (N_HEADS, D_K)

        def proj(x, W, b):
            y = jnp.einsum('bsd,ed->bse', x, W) + b
            return y.reshape(B, S, H, Dk).transpose(0, 2, 1, 3)
        Q = proj(query, wq, bq)
        K = proj(key, wk, bk)
        V = proj(value, wv, bv)
        scores = jnp.einsum('bhqd,bhkd->bhqk', Q, K) / jnp.sqrt(jnp.float32(Dk))
        pos = jnp.arange(S, dtype=jnp.float32)
        decay = -time_decay * jnp.abs(pos[:, None] - pos[None, :])
        scores = scores + decay[None, None, :, :]
        attn = jax.nn.softmax(scores, axis=-1)
        ctx = jnp.einsum('bhqk,bhkd->bhqd', attn, V)
        ctx = ctx.transpose(0, 2, 1, 3).reshape(B, S, D)
        out = jnp.einsum('bsd,ed->bse', ctx, wo) + bo
        return out

    def _L1_ffn_ref(x, wq, bq, wk, bk, wv, bv, wo, bo, ln1_g, ln1_b, ln2_g, ln2_b, wr, w1, b1, w2, b2):
        import jax, jax.numpy as jnp
        import numpy as np
        D_MODEL = 256
        N_HEADS = 16
        HEAD_DIM = D_MODEL // N_HEADS
        FFN_DIM = 1024
        N_EXPERTS = 8
        CAP_FRAC = 0.25
        MOE_TOKEN_DROPOUT = 0.2
        LN_EPS = 1e-05
        B, S = (4, 128)

        def _layer_norm(x, g, b):
            mu = x.mean(-1, keepdims=True)
            var = ((x - mu) ** 2).mean(-1, keepdims=True)
            return (x - mu) * jax.lax.rsqrt(var + LN_EPS) * g + b

        def _self_attention(x, wq, bq, wk, bk, wv, bv, wo, bo):
            b, s, d = x.shape
            q = ((x @ wq + bq) * HEAD_DIM ** (-0.5)).reshape(b, s, N_HEADS, HEAD_DIM)
            k = (x @ wk + bk).reshape(b, s, N_HEADS, HEAD_DIM)
            v = (x @ wv + bv).reshape(b, s, N_HEADS, HEAD_DIM)
            scores = jnp.einsum('bqhd,bkhd->bhqk', q, k)
            p = jax.nn.softmax(scores, axis=-1)
            o = jnp.einsum('bhqk,bkhd->bqhd', p, v).reshape(b, s, d)
            return o @ wo + bo

        def _moe_ffn(x, wr, w1, b1, w2, b2):
            T, D = x.shape
            C = int(np.ceil(CAP_FRAC * T))
            logits = x @ wr
            probs = jax.nn.softmax(logits, axis=-1)
            top1 = jnp.argmax(probs, axis=-1)
            m1 = jax.nn.one_hot(top1, N_EXPERTS, dtype=x.dtype)
            top2 = jnp.argmax(jnp.where(m1 > 0, -jnp.inf, logits), axis=-1)
            m2 = jax.nn.one_hot(top2, N_EXPERTS, dtype=x.dtype)
            loc1 = jnp.cumsum(m1, axis=0) - 1.0
            loc2 = jnp.cumsum(m2, axis=0) - 1.0 + m1.sum(0, keepdims=True)
            m1 = m1 * (loc1 < C)
            m2 = m2 * (loc2 < C)
            t1 = (probs * m1).sum(-1)
            t2 = (probs * m2).sum(-1)
            denom = jnp.maximum(t1 + t2, jnp.finfo(x.dtype).eps)
            t1, t2 = (t1 / denom, t2 / denom)
            tok = jnp.arange(T)
            s1 = loc1[tok, top1].astype(jnp.int32)
            s2 = loc2[tok, top2].astype(jnp.int32)
            v1 = m1[tok, top1] > 0
            v2 = m2[tok, top2] > 0
            s1 = jnp.where(v1, s1, C)
            s2 = jnp.where(v2, s2, C)
            buf = jnp.zeros((N_EXPERTS, C, D), x.dtype)
            buf = buf.at[top1, s1].set(x, mode='drop')
            buf = buf.at[top2, s2].set(x, mode='drop')
            h = jax.nn.relu(jnp.einsum('ecd,edf->ecf', buf, w1) + b1[:, None, :])
            y = (jnp.einsum('ecf,efd->ecd', h, w2) + b2[:, None, :]) * (1.0 - MOE_TOKEN_DROPOUT)
            y1 = y[top1, jnp.minimum(s1, C - 1)]
            y2 = y[top2, jnp.minimum(s2, C - 1)]
            g1 = t1 * v1
            g2 = t2 * v2
            return g1[:, None] * y1 + g2[:, None] * y2
        h = _layer_norm(x, ln1_g, ln1_b)
        h = _self_attention(h, wq, bq, wk, bk, wv, bv, wo, bo)
        x = x + h
        h = _layer_norm(x, ln2_g, ln2_b)
        b, s, d = h.shape
        moe = _moe_ffn(h.reshape(b * s, d), wr, w1, b1, w2, b2).reshape(b, s, d)
        return x + moe
    x = x + _L0_xattn_ref(_layernorm(x, axis=-1), ctx_1024, ctx_1024, mask_Bx1xSxS2_bf1, L0_xattn_Wq, L0_xattn_bq, L0_xattn_Wk, L0_xattn_bk, L0_xattn_Wv, L0_xattn_bv, L0_xattn_Wo, L0_xattn_bo)
    x = x + _L0_ffn_ref(_layernorm(x, axis=-1), L0_ffn_gate_w, L0_ffn_w1, L0_ffn_w2)
    x = x + _L1_xattn_ref(_layernorm(x, axis=-1), ctx_1024, ctx_1024, L1_xattn_wq, L1_xattn_bq, L1_xattn_wk, L1_xattn_bk, L1_xattn_wv, L1_xattn_bv, L1_xattn_wo, L1_xattn_bo, L1_xattn_time_decay)
    x = x + _L1_ffn_ref(_layernorm(x, axis=-1), L1_ffn_wq, L1_ffn_bq, L1_ffn_wk, L1_ffn_bk, L1_ffn_wv, L1_ffn_bv, L1_ffn_wo, L1_ffn_bo, L1_ffn_ln1_g, L1_ffn_ln1_b, L1_ffn_ln2_g, L1_ffn_ln2_b, L1_ffn_wr, L1_ffn_w1, L1_ffn_b1, L1_ffn_w2, L1_ffn_b2)
    return x

_drawn_inputs = setup_inputs


def setup_inputs(seed=0):
    import zlib

    import numpy as np

    out = dict(_drawn_inputs(seed))
    spreads = {'L0_xattn_bq': (0.0, 0.369),
     'L0_xattn_bk': (0.0, 2.0),
     'L0_xattn_bv': (0.0, 0.1),
     'L0_xattn_bo': (0.0, 0.1)}
    factors = {'L1_xattn_bq': 8.0,
     'L1_xattn_bk': 64.0,
     'L1_xattn_bv': 2.82,
     'L1_ffn_wq': 8.0,
     'L1_ffn_bq': 8.0,
     'L1_ffn_wk': 8.0,
     'L1_ffn_bk': 64.0,
     'L1_ffn_bv': 8.0,
     'L1_ffn_bo': 4.856,
     'L1_ffn_ln1_g': 8.0,
     'L1_ffn_ln1_b': 8.0,
     'L1_ffn_ln2_g': 8.0,
     'L1_ffn_ln2_b': 8.0,
     'L1_ffn_b1': 21.732,
     'L1_ffn_b2': 8.0}
    for name, (base, spread) in spreads.items():
        noise = np.random.default_rng([zlib.crc32(name.encode()), seed]).standard_normal(out[name].shape)
        drawn = base * np.exp(spread * noise) if base else spread * noise
        out[name] = jnp.asarray(drawn.astype(out[name].dtype))
    for name, factor in factors.items():
        out[name] = (out[name] * factor).astype(out[name].dtype)
    return out
```

```python
import concourse.bass as bass
from concourse import mybir
from contextlib import ExitStack

F32 = mybir.dt.float32
BF16 = mybir.dt.bfloat16
U8 = mybir.dt.uint8
U32 = mybir.dt.uint32
ALU = mybir.AluOpType
ACT = mybir.ActivationFunctionType
AX = mybir.AxisListType

P = 128
NB = 8
T = 256
C = 256
TT = T // P
CT = C // P
NH = 16
HD = C // NH
NE = 8
FF = 1024
FT = FF // P
CAP0 = 64
SLOT = 512
ST = SLOT // P
NT = NB * TT
TERMS = 6
KSTK = TERMS * HD
NPART = 3
JOBS = 4 + NH
TOPK_STEPS = 6 + 2 * (CAP0 // 8) + 4
PICK_STEPS = 5 + 5 + 6
ROUTE_STEPS = PICK_STEPS + 5 + 6 + 4
BIG = 2.0 ** 100
HUGE = 2.0 ** 120
EPS = 1e-5

Q_TERM = [0, 0, 1, 0, 2, 1]
K_TERM = [0, 1, 0, 2, 0, 1]

CF = {}
_at = 0
for _name, _w in (("ident", P), ("sel", P), ("tri", P), ("iota", CAP0), ("slot", 1), ("rev", NE), ("base", NE),
                  ("keep", 2 * NE * NT)):
    CF[_name] = (_at, _at + _w)
    _at += _w
NCF = _at


def wait(eng, sem, value):
    if isinstance(value, int) and value <= 0:
        return
    eng.wait_ge(sem, value)


def alone(eng):
    eng.nop(nofuse=True)


class Steps:

    def __init__(self, eng, sem, base):
        self.eng, self.sem, self.base, self.k = eng, sem, base, 0

    def step(self, ins, by=1):
        ins.then_inc(self.sem, by)
        self.k += by

    def settle(self):
        self.eng.wait_ge(self.sem, self.base + self.k)


class Turn:

    def __init__(self, m, par):
        self.m, self.par = m, par
        self.n = 2 * m + par

    def next(self, k=1):
        q = self.par + k
        return Turn(self.m + q // 2, q % 2)

    def batch(self, layer):
        return self.n - NB * layer


def before_first(t):
    return isinstance(t.n, int) and t.n < 0


def attention_rounds_0(eng, body):
    body(Turn(-1, 0), 0, None, None, None)
    body(Turn(-1, 1), 0, 0, None, None)
    body(Turn(0, 0), 0, 0, 0, None)
    body(Turn(0, 1), 0, 0, 0, 0)
    with eng.Fori(1, 3) as m:
        body(Turn(m, 0), 0, 0, 0, 0)
        body(Turn(m, 1), 0, 0, 0, 0)
    body(Turn(3, 0), None, 0, 0, 0)
    body(Turn(3, 1), None, None, 0, 0)
    body(Turn(4, 0), None, None, None, 0)


def attention_rounds_12(eng, body):
    body(Turn(3, 0), 1, None, None, None)
    body(Turn(3, 1), 1, 1, None, None)
    with eng.Fori(4, 7) as m:
        body(Turn(m, 0), 1, 1, 1, None)
        body(Turn(m, 1), 1, 1, 1, None)
    body(Turn(7, 0), 2, 1, 1, None)
    body(Turn(7, 1), 2, 2, 1, None)
    body(Turn(8, 0), 2, 2, 2, None)
    body(Turn(8, 1), 2, 2, 2, 2)
    with eng.Fori(9, 11) as m:
        body(Turn(m, 0), 2, 2, 2, 2)
        body(Turn(m, 1), 2, 2, 2, 2)
    body(Turn(11, 0), None, 2, 2, 2)
    body(Turn(11, 1), None, None, 2, 2)
    body(Turn(12, 0), None, None, None, 2)


def finished(layer, n):
    return n if layer == 0 else n - NB


def bass_two_layer_cross_attention_moe(
    nc, x, ctxT, maskp, cf, cb, wqkv, wo, bqk, bv, gates, td, lnp, w1, b1, w2, b2, out,
):
    posd = nc.dram_tensor("slot_of_token", [NB * NE, T], F32, kind="Internal").ap()
    prbd = nc.dram_tensor("prob_of_token", [NB * NE, T], F32, kind="Internal").ap()
    zbuf = nc.dram_tensor("expert_inputs", [NE * SLOT, C], F32, kind="Internal").ap()
    ybuf = nc.dram_tensor("expert_outputs", [NE * SLOT, C], F32, kind="Internal").ap()

    with ExitStack() as ctx:
        def sb(name, shape, dt=F32):
            return ctx.enter_context(nc.sbuf_tensor(name, shape, dt))

        def sem(name):
            return ctx.enter_context(nc.semaphore(name))

        Xall = sb("Xall", [P, NT, C])
        XNall = sb("XNall", [P, NT, C])
        XINT = sb("XINT", [P, CT * NE * SLOT])
        YALL = sb("YALL", [P, NB * (NE // 2) * C])
        STK = sb("STK", [P, 2 * 2 * NH * T], BF16)
        WREG = sb("WREG", [P, 2 * (CT * FF + FT * C)])

        xint = XINT[:, :].rearrange("p (c s) -> p c s", c=CT)
        yall = YALL[:, :].rearrange("p (i c) -> p i c", c=C)
        stk = STK[:, :].rearrange("p (r w h t) -> p r w h t", r=2, w=2, h=NH)
        QS = [stk[:, r, 0] for r in range(2)]
        KS = [stk[:, r, 1] for r in range(2)]
        ht = STK[:, :].bitcast(F32).rearrange("p (r f s) -> p r f s", r=2, f=FT)
        W1 = [WREG[:, r * CT * FF:(r + 1) * CT * FF].rearrange("p (c f) -> p c f", c=CT) for r in range(2)]
        o = 2 * CT * FF
        W2 = [WREG[:, o + r * FT * C:o + (r + 1) * FT * C].rearrange("p (f c) -> p f c", f=FT) for r in range(2)]

        def carve(region, start, *shape, dt=F32):
            size = 1
            for s in shape:
                size *= s
            v = region[:, start:start + (size if dt == F32 else size // (2 if dt == BF16 else 4))]
            if dt != F32:
                v = v.bitcast(dt)
            names = "abcdef"[:len(shape)]
            if len(shape) > 1:
                kw = {names[i]: shape[i] for i in range(1, len(shape))}
                v = v.rearrange(f"p ({' '.join(names)}) -> p {' '.join(names)}", **kw)
            return v

        CTX = [carve(WREG, 512 * r, CT, T) for r in range(2)]
        BPOS = carve(WREG, 1024, NE // 2, T)
        BPRB = carve(WREG, 2048, NE // 2, T)
        WCT = [carve(WREG, 3072 + 1024 * r, NE // 2, T) for r in range(2)]
        XNT = carve(WREG, 5120, CT, T)
        QK32 = carve(WREG, 5632, 2, TT, T)
        XNS = carve(WREG, 6656, TT, C)
        XRS = carve(WREG, 7168, TT, C)
        RC = carve(WREG, 7680, 2 * T)
        MASKU = [carve(YALL, 256 * r, 2, TT, T, dt=U8) for r in range(2)]
        BMK = [carve(YALL, 512 + 512 * r, 2, TT, T, dt=BF16) for r in range(2)]
        GSEL = [carve(YALL, 2048 * (1 + r), TT, NE, CAP0) for r in range(2)]
        XST = [carve(YALL, 6144 + 512 * r, TT, C) for r in range(2)]
        LNP = carve(YALL, 0, 4, C)
        UALL = carve(XINT, 0, NT, C)
        PT = [carve(XINT, 4096 + 1024 * r, 2, TT, T) for r in range(2)]
        OT = carve(XINT, 6144, 4, T)
        XRT = carve(XINT, 7168, CT, T)

        PTK = carve(YALL, 7168, T)[0:NB * NE]
        WORK = carve(YALL, 7424, T)[0:NB * NE]
        CHOSEN = carve(YALL, 7680, T)[0:NB * NE]
        POS = carve(YALL, 7936, T)[0:NB * NE]
        ZS = [carve(YALL, 1024 * r, ST, C) for r in range(2)]
        ZT = [carve(YALL, 2048 + 1024 * r, CT, SLOT) for r in range(2)]
        YS = [carve(YALL, 4096 + 1024 * r, ST, C) for r in range(2)]
        B2B = [carve(YALL, 6144 + 256 * r, C) for r in range(2)]
        B1S = [carve(YALL, 6656 + FT * r, FT) for r in range(2)]
        PRR = carve(XINT, 4096, NT, NE)
        EQ = carve(XINT, 4224, NT, NE)
        PICK = carve(XINT, 4352, 2, NT, NE)
        TOT = carve(XINT, 4608, 2, NE, NT)
        SCN = carve(XINT, 4864, 2, NE, NT)
        EXC = carve(XINT, 5120, 2, NE, NT)
        LOC = carve(XINT, 5376, 2, NT, NE)
        TMP = carve(XINT, 5632, 2, NT, NE)
        GOT = [carve(XINT, 4096 * w, NT, C) for w in range(2)]

        WQKV = [sb(f"WQKV{r}", [P, 3, CT, C]) for r in range(2)]
        WO = [sb(f"WO{r}", [P, 4, C]) for r in range(2)]
        BQK = [sb(f"BQK{r}", [P, 2, CT]) for r in range(2)]
        BQ4 = [sb(f"BQ4{r}", [P, CT]) for r in range(2)]
        BV = [sb(f"BV{r}", [P, C]) for r in range(2)]
        GATE = sb("GATE", [P, 2, CT, NE])
        TD = sb("TD", [P, 1])
        cfs = sb("cfs", [P, NCF])
        cbs = sb("cbs", [P, P + TT * T], BF16)
        TDI = sb("TDI", [P, NPART, P], BF16)
        TDP = sb("TDP", [P, NPART + 2])
        TDB = sb("TDB", [P, NPART], BF16)
        ONES = sb("ONES", [P, P])
        POWH = sb("POWH", [P, TT])

        def cst(name):
            return cfs[:, CF[name][0]:CF[name][1]]

        ident, selb, tri = cst("ident"), cst("sel"), cst("tri")
        identb = cbs[:, 0:P]
        dist = cbs[:, P:].rearrange("p (a t) -> p a t", a=TT)

        QKP = [sb(f"QKP{i}", [P, 2, CT, T], BF16) for i in range(NPART)]
        VA = [sb(f"VA{r}", [P, TT, NH, 32]) for r in range(2)]
        MX = sb("MX", [P, TT, NH])
        NM = sb("NM", [P, 2, TT, NH])
        NMP = sb("NMP", [P, TT, NPART, NH], BF16)
        NMT = sb("NMT", [NPART * NH, T], BF16)
        STATS = sb("STATS", [P, TT, 6])
        MV = sb("MV", [P, TT, 2])
        VE = sb("VE", [P, TT])
        RSTD = sb("RSTD", [P, TT])
        LOG = sb("LOG", [P, NT, NE])
        PR = sb("PR", [P, TT, NB, NE])
        SM = sb("SM", [P, NT])
        SMR = sb("SMR", [P, NT])
        TOP8 = sb("TOP8", [NB * NE, 8])
        ZERO = sb("ZERO", [P, C])
        LS = sb("LS", [P, 2, NT])
        ES = sb("ES", [P, 2, NT])
        FIT = sb("FIT", [P, 2, NT])
        G12 = sb("G12", [P, 2, NT])
        IDXF = sb("IDXF", [P, 2, NT])
        IDX = [sb(f"IDX{w}", [P, 2, NT], U32) for w in range(2)]
        POST = sb("POST", [P, TT, NB * NE])

        PS = [ctx.enter_context(nc.psum_tensor(f"PS{i}", [P, 512], F32)) for i in range(2)]
        PTT = [ctx.enter_context(nc.psum_tensor(f"PTT{i}", [P, 2, 512], F32)) for i in range(2)]
        PO = ctx.enter_context(nc.psum_tensor("PO", [P, 512], F32))
        PM = ctx.enter_context(nc.psum_tensor("PM", [P, 512], F32))
        pm_bf = PM[:, :].bitcast(BF16)

        s_const = sem("const_loaded")
        s_x0 = sem("x_first_loaded")
        s_x = sem("x_loaded")
        s_w = [sem(f"attn_weights_loaded{i}") for i in range(3)]
        s_ctx = [sem(f"ctx_loaded{r}") for r in range(2)]
        s_msk = [sem(f"mask_loaded{r}") for r in range(2)]
        s_stk = [sem(f"stack_loaded{r}") for r in range(2)]
        s_nml = [sem(f"negmax_loaded{r}") for r in range(2)]
        s_bc = sem("slot_rows_loaded")
        s_rows = sem("slot_rows_stored")
        g_const = sem("pool_constants")
        g_mask = sem("mask_converted")
        g_rstd = sem("rstd_ready")
        g_copy = sem("router_input_kept")
        v_const = sem("dve_constants")
        v_bank = sem("score_bank_read")
        v_split = sem("parts_subtracted")
        v_nm = sem("negmax_step")
        v_nmt = sem("negmax_rows_ready")
        v_lnp = sem("prep_norm_step")
        v_lnr = sem("router_norm_step")
        v_xn = sem("attn_input_ready")
        v_xr = sem("router_input_ready")
        v_xrt = sem("router_input_transposed")
        v_log = sem("logits_read")
        v_sel = sem("sums_inverted")
        v_on = sem("heads_normalised")
        v_wct = sem("combine_weights_ready")
        v_comb = sem("combined")
        v_res = sem("residual_added")
        a_split = sem("parts_rounded")
        a_exp = sem("probs_ready")
        a_ot = sem("heads_copied")
        p_s = sem("score_bank_written")
        p_nm = sem("negmax_transposed")
        p_st = sem("shifted_scores_ready")
        p_pv = sem("head_group_done")
        p_sel = sem("sums_spread")
        p_wo = sem("attn_out_ready")
        p_rt = sem("router_input_turned")
        p_log = sem("logits_ready")
        p_comb = sem("combine_ready")
        v_base = sem("output_base_ready")
        v_topk = sem("topk_step")
        a_topk = sem("router_exp_ready")
        p_topk = sem("topk_turned")
        v_gsel = sem("gather_matrix_ready")
        a_xst = sem("token_rows_staged")
        p_disp = sem("expert_inputs_ready")
        v_xi = sem("expert_inputs_read_dve")
        a_xi = sem("expert_inputs_read_act")
        s_ew = [sem(f"expert_weights_loaded{r}") for r in range(2)]
        s_zs = [sem(f"slot_rows_in{r}") for r in range(2)]
        s_b12 = [sem(f"expert_biases_loaded{r}") for r in range(2)]
        p_h = sem("hidden_bank_written")
        a_h = sem("hidden_bank_read")
        p_y = sem("expert_output_written")
        v_y = sem("expert_output_read")
        s_lnp = sem("norm_params_loaded")
        s_zero = sem("expert_inputs_cleared")
        v_rt = sem("routing_step")
        a_rt = sem("routing_exp_ready")
        p_rte = sem("choices_counted")
        s_scat = sem("tokens_scattered")
        s_yst = [sem(f"expert_output_stored{r}") for r in range(2)]
        s_got = [sem(f"outputs_gathered{g}") for g in range(4)]
        v_out = sem("output_rows_ready")
        s_out = sem("output_stored")

        block = ctx.enter_context(nc.Block())

        def nln(layer, n):
            return 5 * n if layer < 2 else 13 * n - (13 - 5) * 2 * NB

        def nrt(k, layer):
            return 5 * k if layer == 0 else 7 * k - 2 * NB

        def expert_rounds(eng, first, step, layer):
            base = NE // 2 * layer
            first()
            step(base, 0, False)
            step(base, 1, False)
            with eng.Fori(base + 1, base + NE // 2 - 1) as m:
                step(m, 0, False)
                step(m, 1, False)
            step(base + NE // 2 - 1, 0, False)
            step(base + NE // 2 - 1, 1, True)

        def uses(layer):
            return FT if layer == 0 else FT + CT

        def use0(layer, e):
            return FT * e if layer == 0 else (FT + CT) * e - CT * NE

        @block.sync
        def _(sp):
            def held(sem, value):
                wait(sp, sem, value)
                alone(sp)

            sp.dma_start(Xall[:, 0:TT, :], x[0].rearrange("(a p) c -> p a c", p=P)).then_inc(s_x0, 16)
            sp.dma_start(cfs[:, :], cf).then_inc(s_const, 16)
            sp.dma_start(cbs[:, :], cb.bitcast(BF16)).then_inc(s_const, 16)
            sp.dma_start(TD[:, :], td.partition_broadcast(P)).then_inc(s_const, 16)
            sp.dma_start(GATE[:, :, :, :], gates.rearrange("l (a p) e -> p l a e", p=P)).then_inc(s_const, 16)

            def load_attn(layer):
                r = layer % 2
                sp.dma_start(WQKV[r][:, :, :, :], wqkv[layer].rearrange("w (a p) c -> p w a c", p=P)).then_inc(s_w[layer], 16)
                sp.dma_start(BQK[r][:, :, :], bqk[layer]).then_inc(s_w[layer], 16)
                sp.dma_start(BV[r][:, :], bv[layer].partition_broadcast(P)).then_inc(s_w[layer], 16)
                sp.dma_start(WO[r][:, :, :], wo[layer]).then_inc(s_w[layer], 16)

            load_attn(0)

            def body(t, lp, la, lc, lr):
                if lp is not None and lp < 2:
                    q = t.next(2)
                    held(p_s, JOBS * (q.n - 2) + 4)
                    sp.dma_start(CTX[q.par], ctxT[q.batch(lp)].rearrange("(a p) t -> p a t", p=P)).then_inc(s_ctx[q.par], 16)
                if lp == 0:
                    held(g_mask, q.n - 1)
                    sp.dma_start(MASKU[q.par], maskp[q.batch(0)].rearrange("w (a p) k -> p w a k", p=P)).then_inc(s_msk[q.par], 16)
                if lp == 1:
                    held(v_wct, q.n - NB)
                    b = q.batch(1)
                    rows = (posd, prbd)
                    for dst, src in ((BPOS, posd), (BPRB, prbd)):
                        v = src.rearrange("(b i h) t -> b h i t", b=NB, h=2)
                        for half in range(2):
                            sp.dma_start(dst[half * 64:half * 64 + 64, :, :], v[b, half].partition_broadcast(64)).then_inc(s_bc, 16)
                if lp == 1 and isinstance(q.n, int) and q.n == NB + 1:
                    held(p_comb, 1)
                    sp.dma_start(LNP, lnp.partition_broadcast(P)).then_inc(s_lnp, 16)
                if lc is not None:
                    held(v_nmt, t.n + 1)
                    sp.dma_start(QS[t.par][KSTK:KSTK + NPART, :, :], NMT[:, :]).then_inc(s_nml[t.par], 16)
                if la is not None:
                    q = t.next()
                    held(v_split, 2 * (q.n + 1))
                    held(a_split, 2 * (q.n + 1))
                    held(p_st, 8 * (q.n - 1))
                    for j in range(TERMS):
                        for dst, w, term in ((QS, 0, Q_TERM), (KS, 1, K_TERM)):
                            sp.dma_start(dst[q.par][j * HD:(j + 1) * HD, :, :], QKP[term[j]][:, w, :, :]).then_inc(s_stk[q.par], 16)

            load_attn(1)
            for i in range(1, NB):
                sp.dma_start(Xall[:, TT * i:TT * i + TT, :], x[i].rearrange("(a p) c -> p a c", p=P)).then_inc(s_x, 16)
            attention_rounds_0(sp, body)
            sp.dma_start(zbuf.rearrange("(p k) c -> p k c", p=P), ZERO[:, :].unsqueeze(1).to_broadcast([P, NE * SLOT // P, C])).then_inc(s_zero, 16)
            held(p_wo, NB)
            load_attn(2)
            held(g_copy, NB)
            held(p_log, NB)

            def load_expert(e, m, par, layer):
                held(p_y, ST * (2 * m + par - 1))
                sp.dma_start(W1[par], w1[layer, e].rearrange("(a p) f -> p a f", p=P)).then_inc(s_ew[par], 16)
                sp.dma_start(W2[par], w2[layer, e].rearrange("(f p) c -> p f c", p=P)).then_inc(s_ew[par], 16)

            load_expert(0, 0, 0, 0)
            load_expert(1, 0, 1, 0)
            held(v_topk, TOPK_STEPS)
            sp.dma_start(posd, POS).then_inc(s_rows, 16)
            sp.dma_start(prbd, PTK).then_inc(s_rows, 16)
            with sp.Fori(1, NE // 2) as m:
                load_expert(2 * m, m, 0, 0)
                load_expert(2 * m + 1, m, 1, 0)
            held(s_rows, 32)
            held(p_y, ST * NE)
            attention_rounds_12(sp, body)

            held(g_copy, 2 * NB)
            held(p_log, 2 * NB)
            half = NE // 2

            def load_expert_1(m, par):
              e = 2 * m + par - NE
              load_expert(e, m, par, 1)
              held(v_y, ST * (2 * m + par - 1))
              sp.dma_start(B1S[par], b1[e]).then_inc(s_b12[par], 16)
              sp.dma_start(B2B[par], b2[e].partition_broadcast(P)).then_inc(s_b12[par], 16)

            def load_slots(m, par):
              e = 2 * m + par - NE
              held(p_h, use0(1, 2 * m + par - 1 - 1) + CT)
              sp.dma_start(ZS[par], zbuf.rearrange("(e a p) c -> e p a c", e=NE, p=P)[e]).then_inc(s_zs[par], 16)

            def store_slots(m, par):
              e = 2 * m + par - NE
              held(v_y, ST * (2 * m + par + 1))
              sp.dma_start(ybuf.rearrange("(e a p) c -> e p a c", e=NE, p=P)[e], YS[par]).then_inc(s_yst[par], 16)

            load_expert_1(half, 0)
            load_expert_1(half, 1)
            held(s_scat, 16 * 2 * NT)
            for par in range(2):
              sp.dma_start(ZS[par], zbuf.rearrange("(e a p) c -> e p a c", e=NE, p=P)[par]).then_inc(s_zs[par], 16)
            with sp.Fori(half + 1, 2 * half) as m:
              for par in range(2):
                  load_slots(m, par)
                  load_expert_1(m, par)
                  store_slots(m - 1, par)
            for par in range(2):
              store_slots(2 * half - 1, par)
            for g in range(4):
              held(v_out, g + 1)
              sp.dma_start(out.rearrange("b (a p) c -> p (b a) c", p=P)[:, 4 * g:4 * g + 4, :], Xall[:, 4 * g:4 * g + 4, :]).then_inc(s_out, 16)
            held(s_out, 64)

        @block.gpsimd
        def _(pool):
            nc.gpsimd.memset(ONES[:, :], 1.0).then_inc(g_const, 1)
            nc.gpsimd.memset(POWH[:, :], -0.5).then_inc(g_const, 1)

            def rstd(sem_ve, value):
                pool.wait_ge(sem_ve, value)
                nc.gpsimd.tensor_tensor(RSTD[:, :], VE[:, :], POWH[:, :], ALU.pow).then_inc(g_rstd, 1)

            pool.wait_ge(g_const, 2)

            def body(t, lp, la, lc, lr):
                if lr is not None:
                    q = t.next(-1)
                    k = finished(lr, q.n)
                    rstd(v_lnr, nrt(k, lr) + 5)
                    pool.wait_ge(v_xr, k + 1)
                    nc.gpsimd.tensor_copy(XNall[:, bass.ts(q.batch(lr), TT), :], XRS).then_inc(g_copy, 1)
                if lp is not None:
                    q = t.next(2)
                    rstd(v_lnp, nln(lp, q.n) + 5)
                    if lp == 2:
                        rstd(v_lnp, nln(lp, q.n) + 11)
                    if lp == 0:
                        pool.wait_ge(s_msk[q.par], 16 * (q.m + 1))
                        wait(pool, p_st, 8 * (q.n - 1))
                        alone(pool)
                        nc.gpsimd.tensor_scalar(BMK[q.par], MASKU[q.par], 1.0, BIG, ALU.subtract, ALU.mult).then_inc(g_mask, 1)

            attention_rounds_0(pool, body)
            attention_rounds_12(pool, body)
            pool.wait_ge(s_zero, 16)
            pool.wait_ge(v_rt, ROUTE_STEPS)
            pool.wait_ge(g_copy, 2 * NB)
            for k in range(2):
                for i in range(NT):
                    nc.gpsimd.indirect_dma_start(
                        out=zbuf, out_offset=bass.IndirectOffsetOnAxis(ap=IDX[0][:, k, i:i + 1], axis=0),
                        in_=XNall[:, i, :], in_offset=None, bounds_check=NE * SLOT - 1, oob_is_err=False).then_inc(s_scat, 16)
            for r in range(2):
                pool.wait_ge(s_yst[r], 16 * NE // 2)
            for i in range(NT):
                for k in range(2):
                    nc.gpsimd.indirect_dma_start(
                        out=GOT[k][:, i, :], out_offset=None, in_=ybuf,
                        in_offset=bass.IndirectOffsetOnAxis(ap=IDX[1][:, k, i:i + 1], axis=0),
                        bounds_check=NE * SLOT - 1, oob_is_err=False).then_inc(s_got[i // 4], 16)

        @block.scalar
        def _(act):
            def body(t, lp, la, lc, lr):
                if la is not None:
                    q = t.next()
                    act.wait_ge(v_bank, JOBS * q.n + 3)
                    if not before_first(t):
                        act.wait_ge(s_stk[t.par], 192 * (t.m + 1))
                    nc.scalar.copy(QKP[0][:, :, :, :], QK32).then_inc(a_split, 1)
                    act.wait_ge(v_split, 2 * q.n + 1)
                    nc.scalar.copy(QKP[1][:, :, :, :], QK32).then_inc(a_split, 1)
                if lc is not None:
                    for pr in range(NH // 2):
                        act.wait_ge(p_st, 8 * t.n + pr + 1)
                        if pr >= 2:
                            act.wait_ge(p_pv, 8 * t.n + pr - 1)
                        else:
                            wait(act, p_pv, 8 * t.n + pr - 1)
                        nc.scalar.activation(PT[pr % 2].rearrange("p h a t -> p (h a t)"),
                                             PTT[pr % 2][:, :, :].rearrange("p h k -> p (h k)"), ACT.Exp).then_inc(a_exp, 1)
                        if pr % 2 == 0 and pr:
                            group_out(t, pr // 2 - 1)
                    group_out(t, 3)

            def group_out(t, g):
                act.wait_ge(p_pv, 8 * t.n + 2 * g + 2)
                wait(act, p_wo, t.n)
                nc.scalar.copy(OT[:, g, :], PO[:, 0:T]).then_inc(a_ot, 1)

            attention_rounds_0(act, body)

            act.wait_ge(v_topk, 2)
            nc.scalar.activation(LOG[:, :, :], LOG[:, :, :], ACT.Exp).then_inc(a_topk, 1)
            act.wait_ge(g_copy, NB)
            with act.Fori(0, NB // 2) as m:
                for par in range(2):
                    b = 2 * m + par
                    act.wait_ge(p_disp, 2 * b)
                    nc.scalar.copy(XST[par], XNall[:, bass.ts(b, TT), :]).then_inc(a_xst, 1)
                    act.wait_ge(p_disp, 2 * b + 1)
                    nc.scalar.copy(xint[:, 0, :].rearrange("p (e b s) -> p e b s", e=NE, b=NB)[:, :, b, :],
                                   PTT[par][:, 0, :].rearrange("p (e s) -> p e s", e=NE)).then_inc(a_xi, 1)

            def hidden(m, par, layer):
                e = 2 * m + par
                wait(act, p_y, ST * (e - 1))
                if layer == 1:
                    act.wait_ge(s_b12[par], 32 * (m - NE // 2 + 1))
                for f in range(FT):
                    k = use0(layer, e) + uses(layer) - FT + f
                    j = (uses(layer) * par + uses(layer) - FT + f) % 4
                    act.wait_ge(p_h, k + 1)
                    src = PTT[j // 2][:, j % 2, :]
                    if layer == 0:
                        ins = nc.scalar.activation(ht[:, par, f, :], src, ACT.Gelu)
                    else:
                        ins = nc.scalar.activation(ht[:, par, f, :], src, ACT.Relu, bias=B1S[par][:, f:f + 1])
                    ins.then_inc(a_h, 1)

            def turned(m, par):
                e = 2 * m + par
                for c in range(CT):
                    j = (uses(1) * par + c) % 4
                    act.wait_ge(p_h, use0(1, e) + c + 1)
                    nc.scalar.copy(ZT[par][:, c, :], PTT[j // 2][:, j % 2, :]).then_inc(a_h, 1)

            def step(layer):
                def go(m, par, last):
                    q = Turn(m, par)
                    if not last:
                        hidden(q.next().m, q.next().par, layer)
                        if layer == 1 and not (isinstance(m, int) and m > NE // 2 and par == 0):
                            turned(q.next(2).m, q.next(2).par)
                return go

            expert_rounds(act, lambda: hidden(0, 0, 0), step(0), 0)
            attention_rounds_12(act, body)
            act.wait_ge(v_rt, 2)
            nc.scalar.activation(PRR, PRR, ACT.Exp).then_inc(a_rt, 1)

            def first():
                turned(NE // 2, 0)
                hidden(NE // 2, 0, 1)
                turned(NE // 2, 1)
            expert_rounds(act, first, step(1), 1)

        @block.vector
        def _(dve):
            nc.vector.memset(ZERO[:, :], 0.0)
            c = Steps(dve, v_const, 0)
            for r in range(2):
                c.step(nc.vector.memset(KS[r][KSTK:KSTK + 32, :, :], 1.0))
                c.step(nc.vector.memset(VA[r][:, :, :, :], 0.0))
            c.settle()
            for r in range(2):
                c.step(nc.vector.memset(VA[r][:, :, :, 0:1], 1.0))
            dve.wait_ge(s_const, 64)
            c.step(nc.vector.tensor_copy(TDB[:, 0:1], TD[:, :]))
            c.settle()
            c.step(nc.vector.tensor_tensor(TDP[:, 3:4], TD[:, :], TDB[:, 0:1], ALU.subtract))
            c.settle()
            c.step(nc.vector.tensor_copy(TDB[:, 1:2], TDP[:, 3:4]))
            c.settle()
            c.step(nc.vector.tensor_tensor(TDP[:, 4:5], TDP[:, 3:4], TDB[:, 1:2], ALU.subtract))
            c.settle()
            c.step(nc.vector.tensor_copy(TDB[:, 2:3], TDP[:, 4:5]))
            c.settle()
            c.step(nc.vector.tensor_scalar(TDP[:, 0:3], TDB[:, :], -1.0, None, ALU.mult))
            c.settle()
            for i in range(NPART):
                c.step(nc.vector.tensor_scalar(TDI[:, i, :], identb, TDP[:, i:i + 1], None, ALU.mult))

            def quarter_bias(layer):
                dve.wait_ge(s_w[layer], 64)
                c.step(nc.vector.tensor_scalar(BQ4[layer % 2][:, :], BQK[layer % 2][:, 0, :], 0.25, None, ALU.mult))
                c.settle()

            quarter_bias(0)

            def norm(src, sem, base, powers):
                s = Steps(dve, sem, base)
                alone(dve)
                for a in range(TT):
                    s.step(nc.vector.bn_stats(STATS[:, a, :], src(a)))
                s.settle()
                alone(dve)
                for a in range(TT):
                    s.step(nc.vector.bn_aggr(MV[:, a, :], STATS[:, a, :]))
                s.settle()
                s.step(nc.vector.tensor_scalar(VE[:, :], MV[:, :, 1], EPS, None, ALU.add))
                dve.wait_ge(g_rstd, powers)
                return s

            def apply_norm(dst, src, s, done, affine):
                for a in range(TT):
                    ins = nc.vector.tensor_scalar(dst[:, a, :], src(a), MV[:, a, 0:1], RSTD[:, a:a + 1], ALU.subtract, ALU.mult)
                if affine is not None or done is None:
                    s.step(ins)
                    s.settle()
                if affine is not None:
                    s.step(nc.vector.tensor_tensor(dst, dst, LNP[:, affine, :].unsqueeze(1).to_broadcast([P, TT, C]), ALU.mult))
                    s.settle()
                    ins = nc.vector.tensor_tensor(dst, dst, LNP[:, affine + 1, :].unsqueeze(1).to_broadcast([P, TT, C]), ALU.add)
                if done is not None:
                    ins.then_inc(done, 1)

            def bank(j):
                return PS[j % 2]

            def body(t, lp, la, lc, lr):
                if lc is not None:
                    s = Steps(dve, v_nm, 6 * t.n)
                    dve.wait_ge(v_bank, JOBS * (t.n + 1))
                    if lc == 0:
                        s.step(nc.vector.tensor_scalar(NM[:, 1], MX[:, :, :], -BIG / 2, HUGE, ALU.is_lt, ALU.mult))
                        s.settle()
                        s.step(nc.vector.tensor_tensor(NM[:, 0], NM[:, 1], MX[:, :, :], ALU.subtract))
                    else:
                        s.step(nc.vector.tensor_scalar(NM[:, 0], MX[:, :, :], -1.0, None, ALU.mult), 2)
                    s.settle()
                    s.step(nc.vector.tensor_copy(NMP[:, :, 0, :], NM[:, 0]))
                    s.settle()
                    s.step(nc.vector.tensor_tensor(NM[:, 1], NM[:, 0], NMP[:, :, 0, :], ALU.subtract))
                    s.settle()
                    s.step(nc.vector.tensor_copy(NMP[:, :, 1, :], NM[:, 1]))
                    s.settle()
                    s.step(nc.vector.tensor_tensor(NMP[:, :, 2, :], NM[:, 1], NMP[:, :, 1, :], ALU.subtract))

                q = t.next()
                r = None if la is None else la % 2

                def job(j):
                    dve.wait_ge(p_s, JOBS * q.n + j + 1)

                if la is not None:
                    if isinstance(q.n, int) and q.n in (NB, 2 * NB):
                        quarter_bias(la)
                    job(0)
                    nc.vector.tensor_copy(XNT.rearrange("p a t -> p (a t)"), bank(0)[:, :]).then_inc(v_bank, 1)
                    job(1)
                    nc.vector.scalar_tensor_tensor(
                        QK32[:, 0], bank(1)[:, :].rearrange("p (a t) -> p a t", a=CT), 0.25,
                        BQ4[r][:, :].unsqueeze(2).to_broadcast([P, CT, T]), ALU.mult, ALU.add).then_inc(v_bank, 1)
                if lc is not None:
                    dve.wait_ge(p_nm, t.n + 1)
                    prev = t.next(-1)
                    if not before_first(prev):
                        dve.wait_ge(s_nml[prev.par], 16 * (prev.m + 1))
                    nc.vector.tensor_copy(NMT[:, :], pm_bf[0:NPART * NH, 0:T]).then_inc(v_nmt, 1)
                if la is not None:
                    job(2)
                    nc.vector.tensor_tensor(
                        QK32[:, 1], bank(2)[:, :].rearrange("p (a t) -> p a t", a=CT),
                        BQK[r][:, 1, :].unsqueeze(2).to_broadcast([P, CT, T]), ALU.add).then_inc(v_bank, 1)
                    job(3)
                    wait(dve, p_pv, 8 * (q.n - 1))
                    nc.vector.tensor_tensor(
                        VA[q.par][:, :, :, 1:1 + HD], bank(3)[:, :].rearrange("p (a h d) -> p a h d", a=TT, h=NH),
                        BV[r][:, :].rearrange("p (h d) -> p h d", h=NH).unsqueeze(1).to_broadcast([P, TT, NH, HD]),
                        ALU.add).then_inc(v_bank, 1)
                    dve.wait_ge(a_split, 2 * q.n + 1)
                    nc.vector.tensor_tensor(QK32, QK32, QKP[0][:, :, :, :], ALU.subtract).then_inc(v_split, 1)
                    dve.wait_ge(a_split, 2 * q.n + 2)
                    nc.vector.tensor_tensor(QKP[2][:, :, :, :], QK32, QKP[1][:, :, :, :], ALU.subtract).then_inc(v_split, 1)

                if lr is not None:
                    z = t.next(-1)
                    k = finished(lr, z.n)
                    b = z.batch(lr)
                    dve.wait_ge(v_res, z.n + 1)
                    wait(dve, g_copy, k)
                    src = Xall if lr == 0 else UALL
                    st = norm(lambda a: src[:, b * TT + a, :], v_lnr, nrt(k, lr), rst(lr, z, True))
                    apply_norm(XRS, lambda a: src[:, b * TT + a, :], st, v_xr, 2 if lr == 2 else None)
                    dve.wait_ge(p_rt, k + 1)
                    nc.vector.tensor_copy(XRT.rearrange("p a t -> p (a t)"), PM[:, :]).then_inc(v_xrt, 1)
                    dve.wait_ge(p_log, k + 1)
                    nc.vector.tensor_copy(LOG[:, bass.ts(b, TT), :],
                                          PM[:, 0:TT * NE].rearrange("p (a e) -> p a e", a=TT)).then_inc(v_log, 1)

                if lp is not None:
                    z = t.next(2)
                    b = z.batch(lp)
                    first = isinstance(z.n, int)
                    if lp == 0:
                        dve.wait_ge(s_x0 if first and z.n == 0 else s_x, 16 if first and z.n == 0 else 112)
                    if lp == 1:
                        dve.wait_ge(s_bc, 64 * (z.n - NB + 1))
                        wait(dve, p_comb, z.n - NB - 1)
                        nc.vector.scalar_tensor_tensor(WCT[z.par].rearrange("p i t -> p (i t)"), BPOS.rearrange("p i t -> p (i t)"),
                                                       cst("slot"), BPRB.rearrange("p i t -> p (i t)"),
                                                       ALU.is_equal, ALU.mult).then_inc(v_wct, 1)
                        dve.wait_ge(p_comb, z.n - NB + 1)
                        xv = Xall[:, bass.ts(b, TT), :]
                        nc.vector.tensor_tensor(xv, xv, PM[:, :].rearrange("p (a c) -> p a c", a=TT), ALU.add).then_inc(v_comb, 1)
                        dve.wait_ge(v_comb, z.n - NB + 1)
                    wait(dve, p_s, JOBS * (z.n - 1) + 1)
                    count = rst(lp, z, False)
                    if lp == 2:
                        dve.wait_ge(v_res, z.n - NB + 1)
                        if first and z.n == 2 * NB:
                            dve.wait_ge(s_lnp, 16)
                    st = norm(lambda a: Xall[:, b * TT + a, :], v_lnp, nln(lp, z.n), count)
                    if lp < 2:
                        apply_norm(XNS, lambda a: Xall[:, b * TT + a, :], st, v_xn, None)
                    else:
                        apply_norm(UALL[:, bass.ts(b, TT), :], lambda a: Xall[:, b * TT + a, :], st, None, None)
                        st = norm(lambda a: UALL[:, b * TT + a, :], v_lnp, nln(lp, z.n) + 6, count + 1)
                        apply_norm(XNS, lambda a: UALL[:, b * TT + a, :], st, v_xn, 0)

                def scores(hp):
                    for a in range(TT):
                        j = 4 + 2 * hp + a
                        job(j)
                        nc.vector.tensor_reduce(MX[:, a, 2 * hp:2 * hp + 2],
                                                bank(j)[:, :].rearrange("p (h k) -> p h k", h=2), AX.X, ALU.max).then_inc(v_bank, 1)

                def normalise(g):
                    dve.wait_ge(p_sel, 2 * t.n + g + 1)
                    wait(dve, v_on, 2 * t.n + g)
                    nc.vector.reciprocal(RC, PM[:, :]).then_inc(v_sel, 1)
                    dve.wait_ge(v_sel, 2 * t.n + g + 1)
                    v = OT[:, 2 * g:2 * g + 2, :].rearrange("p i t -> p (i t)")
                    nc.vector.tensor_tensor(v, v, RC, ALU.mult).then_inc(v_on, 1)

                if lc is not None:
                    normalise(0)
                if la is not None:
                    for hp in range(8):
                        scores(hp)
                if lc is not None:
                    normalise(1)
                    b = t.batch(lc)
                    dve.wait_ge(p_wo, t.n + 1)
                    xv = Xall[:, bass.ts(b, TT), :]
                    pv = PM[:, :].rearrange("p (a c) -> p a c", a=TT)
                    if lc < 2:
                        nc.vector.tensor_tensor(xv, xv, pv, ALU.add).then_inc(v_res, 1)
                    else:
                        uv = UALL[:, bass.ts(b, TT), :]
                        nc.vector.tensor_tensor(uv, uv, pv, ALU.add).then_inc(v_res, 1)
                        dve.wait_ge(v_res, t.n + 1)
                        nc.vector.tensor_tensor(xv, xv, uv, ALU.add).then_inc(v_base, 1)

            def rst(layer, z, router):
                if layer == 0:
                    if router:
                        if isinstance(z.n, int):
                            return min(z.n + 3, NB) + z.n + 1
                        return 2 * z.n + 4
                    if isinstance(z.n, int):
                        return z.n + 1 + max(z.n - 2, 0)
                    return 2 * z.n - 1
                if layer == 1:
                    return z.n + NB + 1
                known = isinstance(z.n, int)
                if router:
                    return 3 * NB + 2 * (min(z.n - 13, NB) if known else z.n - 13) + z.n - 2 * NB + 1
                return 3 * NB + 2 * (z.n - 2 * NB) + 1 + (max(z.n - 18, 0) if known else z.n - 18)

            attention_rounds_0(dve, body)

            def softmax(s, src, dst, a_sem):
                s.step(nc.vector.tensor_reduce(SM[:, :], LOG[:, :, :], AX.X, ALU.max))
                s.settle()
                s.step(nc.vector.tensor_tensor(dst, src, SM[:, :].unsqueeze(2).to_broadcast([P, NT, NE]), ALU.subtract))
                dve.wait_ge(a_sem, 1)
                s.step(nc.vector.tensor_reduce(SMR[:, :], dst, AX.X, ALU.add))
                s.settle()
                s.step(nc.vector.reciprocal(SM[:, :], SMR[:, :]))
                s.settle()

            dve.wait_ge(v_log, NB)
            s = Steps(dve, v_topk, 0)
            softmax(s, LOG[:, :, :], LOG[:, :, :], a_topk)
            s.step(nc.vector.tensor_tensor(
                PR[:, :, :, :].rearrange("p a b e -> p b a e"), LOG[:, :, :].rearrange("p (b a) e -> p b a e", a=TT),
                SM[:, :].rearrange("p (b a) -> p b a", a=TT).unsqueeze(3).to_broadcast([P, NB, TT, NE]), ALU.mult))
            dve.wait_ge(p_topk, 1)
            s.step(nc.vector.tensor_copy(PTK, PM[0:NB * NE, 0:T]))
            s.settle()
            for i in range(CAP0 // 8):
                cur = PTK if i == 0 else WORK
                s.step(nc.vector.max(TOP8[:, :], cur))
                s.settle()
                s.step(nc.vector.match_replace(WORK, TOP8[:, :], cur, -1.0))
                s.settle()
            s.step(nc.vector.tensor_scalar(CHOSEN, WORK, 0.0, None, ALU.is_lt))
            s.settle()
            s.step(nc.vector.tensor_tensor_scan(POS, CHOSEN, CHOSEN, 0.0, ALU.add, ALU.max))
            s.settle()
            s.step(nc.vector.tensor_tensor(POS, POS, CHOSEN, ALU.mult))
            s.settle()
            s.step(nc.vector.tensor_scalar(POS, POS, -1.0, None, ALU.add))
            assert s.k == TOPK_STEPS
            dve.wait_ge(p_topk, 2)
            s.step(nc.vector.tensor_copy(POST[:, :, :], PM[:, 0:TT * NB * NE].rearrange("p (a r) -> p a r", a=TT)))
            s.settle()
            with dve.Fori(0, NB // 2) as m:
                for par in range(2):
                    b = 2 * m + par
                    dve.wait_ge(p_disp, 2 * b)
                    for a in range(TT):
                        nc.vector.tensor_tensor(
                            GSEL[par][:, a], cst("iota").unsqueeze(1).to_broadcast([P, NE, CAP0]),
                            POST[:, a, bass.ts(b, NE)].unsqueeze(2).to_broadcast([P, NE, CAP0]),
                            ALU.is_equal).then_inc(v_gsel, 1)
                    dve.wait_ge(p_disp, 2 * b + 2)
                    nc.vector.tensor_copy(xint[:, 1, :].rearrange("p (e b s) -> p e b s", e=NE, b=NB)[:, :, b, :],
                                          PTT[par][:, 1, :].rearrange("p (e s) -> p e s", e=NE)).then_inc(v_xi, 1)

            def expert_out(layer):
                def go(m, par, last):
                    e = 2 * m + par
                    for st in range(ST):
                        bk = (PS[0], PS[1], PO, PM)[st]
                        dve.wait_ge(p_y, ST * e + st + 1)
                        if layer == 0:
                            for h in range(2):
                                ins = nc.vector.tensor_copy(yall[64 * par:64 * par + 64, (2 * st + h) * (NE // 2) + m, :],
                                                            bk[64 * h:64 * h + 64, 0:C])
                        else:
                            if st == 0:
                                wait(dve, s_yst[par], 16 * (m - NE // 2)) if not (isinstance(m, int) and m == NE // 2) else None
                                dve.wait_ge(s_b12[par], 32 * (m - NE // 2 + 1))
                            ins = nc.vector.tensor_tensor(YS[par][:, st, :], bk[:, 0:C], B2B[par], ALU.add)
                        ins.then_inc(v_y, 1)
                return go

            dve.wait_ge(s_rows, 32)
            expert_rounds(dve, lambda: None, expert_out(0), 0)
            for r in range(2):
                nc.vector.memset(KS[r][KSTK:KSTK + 32, :, :], 1.0)
            attention_rounds_12(dve, body)

            dve.wait_ge(v_log, 2 * NB)
            dve.wait_ge(p_wo, 3 * NB)
            s = Steps(dve, v_rt, 0)
            softmax(s, LOG[:, :, :], PRR, a_rt)
            s.step(nc.vector.tensor_tensor(PRR, PRR, SM[:, :].unsqueeze(2).to_broadcast([P, NT, NE]), ALU.mult))
            s.settle()
            by_expert = lambda v: v.unsqueeze(2).to_broadcast([P, NT, NE])
            for k, src in ((0, PRR), (1, TMP[:, 0])):
                if k:
                    s.step(nc.vector.scalar_tensor_tensor(TMP[:, 0], PICK[:, 0], -BIG, LOG[:, :, :], ALU.mult, ALU.add))
                    s.settle()
                s.step(nc.vector.tensor_reduce(SM[:, :], src, AX.X, ALU.max))
                s.settle()
                s.step(nc.vector.tensor_tensor(EQ, src, by_expert(SM[:, :]), ALU.is_equal))
                s.settle()
                s.step(nc.vector.tensor_tensor(EQ, EQ, cst("rev").unsqueeze(1).to_broadcast([P, NT, NE]), ALU.mult))
                s.settle()
                s.step(nc.vector.tensor_reduce(SMR[:, :], EQ, AX.X, ALU.max))
                s.settle()
                s.step(nc.vector.tensor_tensor(PICK[:, k], EQ, by_expert(SMR[:, :]), ALU.is_equal))
                s.settle()
            assert s.k == PICK_STEPS, s.k
            dve.wait_ge(p_rte, 2)
            s.step(nc.vector.tensor_copy(TOT, PS[1][:, 0:2 * NE * NT].rearrange("p (k i e) -> p k e i", k=2, i=NT)))
            s.settle()
            flat = lambda v: v.rearrange("p k e i -> p (k e i)")
            s.step(nc.vector.tensor_tensor_scan(flat(SCN), cst("keep"), flat(TOT), 0.0, ALU.mult, ALU.add))
            s.settle()
            s.step(nc.vector.tensor_tensor(EXC, SCN, TOT, ALU.subtract))
            s.settle()
            s.step(nc.vector.tensor_tensor(LOC, PS[0][:, 0:2 * NE * NT].rearrange("p (k i e) -> p k i e", k=2, i=NT),
                                           EXC.rearrange("p k e i -> p k i e"), ALU.add))
            s.settle()
            s.step(nc.vector.tensor_tensor(LOC[:, 1], LOC[:, 1], SCN[:, 0, :, NT - 1].unsqueeze(1).to_broadcast([P, NT, NE]), ALU.add))
            s.settle()

            def picked(dst, value):
                s.step(nc.vector.tensor_tensor(TMP, PICK, value, ALU.mult))
                s.settle()
                s.step(nc.vector.tensor_reduce(dst, TMP, AX.X, ALU.add))
                s.settle()

            picked(LS[:, :, :], LOC)
            picked(ES[:, :, :], cst("base").unsqueeze(1).unsqueeze(1).to_broadcast([P, 2, NT, NE]))
            picked(G12[:, :, :], PRR.unsqueeze(1).to_broadcast([P, 2, NT, NE]))
            s.step(nc.vector.tensor_scalar(FIT[:, :, :], LS[:, :, :], float(SLOT), None, ALU.is_le))
            s.settle()
            s.step(nc.vector.scalar_tensor_tensor(IDXF[:, :, :], FIT[:, :, :], -65536.0, ES[:, :, :], ALU.mult, ALU.add))
            s.settle()
            s.step(nc.vector.tensor_tensor(IDXF[:, :, :], IDXF[:, :, :], LS[:, :, :], ALU.add))
            s.settle()
            s.step(nc.vector.tensor_scalar(IDX[0][:, :, :], IDXF[:, :, :], 65535.0, None, ALU.add))
            s.settle()
            assert s.k == ROUTE_STEPS, s.k
            s.step(nc.vector.scalar_tensor_tensor(IDXF[:, :, :], LS[:, :, :], float(SLOT), ES[:, :, :], ALU.min, ALU.add))
            s.settle()
            s.step(nc.vector.tensor_scalar(IDX[1][:, :, :], IDXF[:, :, :], -1.0, None, ALU.add))
            s.step(nc.vector.tensor_tensor(G12[:, :, :], G12[:, :, :], FIT[:, :, :], ALU.mult))
            s.settle()
            s.step(nc.vector.tensor_tensor(SM[:, :], G12[:, 0, :], G12[:, 1, :], ALU.add))
            s.settle()
            s.step(nc.vector.tensor_scalar(SM[:, :], SM[:, :], 2.0 ** -23, None, ALU.max))
            s.settle()
            s.step(nc.vector.reciprocal(SMR[:, :], SM[:, :]))
            s.settle()
            s.step(nc.vector.scalar_tensor_tensor(G12[:, :, :], G12[:, :, :], 0.8, SMR[:, :].unsqueeze(1).to_broadcast([P, 2, NT]), ALU.mult, ALU.mult))
            s.settle()
            expert_rounds(dve, lambda: None, expert_out(1), 1)

            for g in range(4):
                dve.wait_ge(s_got[g], 16 * 8)
                for k in range(2):
                    for i in range(4 * g, 4 * g + 4):
                        ins = nc.vector.scalar_tensor_tensor(Xall[:, i, :], GOT[k][:, i, :], G12[:, k, i:i + 1], Xall[:, i, :], ALU.mult, ALU.add)
                        if k == 0 and i % 4 == 3:
                            s.step(ins)
                            s.settle()
                ins.then_inc(v_out, 1)

        @block.tensor
        def _(pe):
            mm = nc.tensor.matmul
            pe.wait_ge(s_const, 64)
            pe.wait_ge(v_const, 15)

            def job_bank(q, j):
                wait(pe, v_bank, JOBS * q.n + j - 1)
                return PS[j % 2]

            def project(q, la):
                r = la % 2
                if la == 2:
                    kv = XNT
                else:
                    kv = CTX[q.par]
                for j, w in ((1, 0), (2, 1)):
                    if j == 1:
                        pe.wait_ge(v_bank, JOBS * q.n + 1)
                    elif la < 2:
                        pe.wait_ge(s_ctx[q.par], 16 * (q.m + 1))
                    bk = job_bank(q, j)
                    src = XNT if j == 1 else kv
                    for mt in range(CT):
                        for a in range(CT):
                            ins = mm(bk[:, mt * T:(mt + 1) * T], WQKV[r][:, w, a, mt * P:(mt + 1) * P], src[:, a, :],
                                     start=(a == 0), stop=(a == CT - 1))
                    ins.then_inc(p_s, 1)
                    yield
                bk = job_bank(q, 3)
                for tk in range(TT):
                    for a in range(CT):
                        ins = mm(bk[:, tk * C:(tk + 1) * C], kv[:, a, tk * P:(tk + 1) * P], WQKV[r][:, 2, a, :],
                                 start=(a == 0), stop=(a == CT - 1))
                ins.then_inc(p_s, 1)
                yield

            def bias(outv, layer, par, which, tile, n):
                if which == 0:
                    rhs = (BMK[par][:, 0, tile, :] if layer == 0 else dist[:, tile, :]).unsqueeze(1).to_broadcast([P, 2, T])
                else:
                    rhs = BMK[par][:, 1] if layer == 0 else dist
                if layer == 0:
                    mm(outv, identb, rhs, start=True, stop=True, skip_group_check=True)
                elif layer == 1:
                    for i in range(NPART):
                        mm(outv, TDI[:, i, :], rhs, start=(i == 0), stop=True, skip_group_check=True)

            def scores(q, la, hp):
                if hp == 0:
                    pe.wait_ge(s_stk[q.par], 192 * (q.m + 1))
                    if la == 0:
                        pe.wait_ge(g_mask, q.n + 1)
                for a in range(TT):
                    bk = job_bank(q, 4 + 2 * hp + a)
                    bias(bk[:, :].rearrange("p (h k) -> p h k", h=2), la, q.par, 0, a, q.n)
                    for h in range(2):
                        ins = mm(bk[:, h * T:(h + 1) * T], QS[q.par][0:KSTK, 2 * hp + h, a * P:(a + 1) * P],
                                 KS[q.par][0:KSTK, 2 * hp + h, :], start=(la == 2), stop=True, skip_group_check=True)
                    ins.then_inc(p_s, 1)

            def shifted(t, lc, pr):
                wait(pe, a_exp, 8 * t.n + pr - 1)
                for h in range(2):
                    bk = PTT[pr % 2][:, h, :].rearrange("p (a t) -> p a t", a=TT)
                    bias(bk, lc, t.par, 1, None, t.n)
                    for a in range(TT):
                        ins = mm(bk[:, a, :], KS[t.par][0:KSTK + NPART, 2 * pr + h, a * P:(a + 1) * P],
                                 QS[t.par][0:KSTK + NPART, 2 * pr + h, :], start=(lc == 2), stop=True, skip_group_check=True)
                ins.then_inc(p_st, 1)

            def weigh(t, pr):
                pe.wait_ge(a_exp, 8 * t.n + pr + 1)
                if pr % 2 == 0:
                    wait(pe, a_ot, 4 * t.n + pr // 2)
                for h in range(2):
                    g = (2 * pr + h) % 4
                    for a in range(TT):
                        ins = mm(PO[32 * g:32 * g + 32, 0:T], VA[t.par][:, a, 2 * pr + h, :], PT[pr % 2][:, h, a, :],
                                 start=(a == 0), stop=(a == TT - 1))
                ins.then_inc(p_pv, 1)

            def spread(t, g):
                pe.wait_ge(a_ot, 4 * t.n + 2 * g + 2)
                mm(PM[:, :], selb, OT[:, 2 * g:2 * g + 2, :].rearrange("p i t -> p (i t)"), start=True, stop=True).then_inc(p_sel, 1)

            def body(t, lp, la, lc, lr):
                q = t.next()
                if la is not None:
                    if isinstance(q.n, int) and q.n % NB == 0 and q.n < 2 * NB:
                        pe.wait_ge(s_w[la], 64)
                    pe.wait_ge(v_xn, q.n + 1)
                    bk = job_bank(q, 0)
                    for ct in range(CT):
                        for a in range(TT):
                            ins = nc.tensor.transpose(bk[:, ct * T + a * P:ct * T + (a + 1) * P], XNS[:, a, ct * P:(ct + 1) * P], ident)
                    ins.then_inc(p_s, 1)
                    steps = project(q, la)
                    next(steps)
                if lc is not None:
                    pe.wait_ge(v_nm, 6 * (t.n + 1))
                    wait(pe, v_res, t.n)
                    if lc == 1 and la == 1:
                        pe.wait_ge(v_comb, t.n + 2 - NB)
                    alone(pe)
                    for a in range(TT):
                        ins = nc.tensor.transpose(pm_bf[0:NPART * NH, a * P:(a + 1) * P],
                                                  NMP[:, a, :, :].rearrange("p i h -> p (i h)"), identb)
                    ins.then_inc(p_nm, 1)
                if la is not None:
                    next(steps)
                    next(steps)
                if lc is not None:
                    pe.wait_ge(s_nml[t.par], 16 * (t.m + 1))
                    shifted(t, lc, 0)
                    for pr in range(NH // 2):
                        if pr + 1 < NH // 2:
                            shifted(t, lc, pr + 1)
                        weigh(t, pr)
                        if pr == 1 and lr is not None:
                            router_turn(t.next(-1), lr, lc)
                        if pr == 2 and lr is not None:
                            router_logits(t.next(-1), lr)
                        if pr == 2 and lp == 1:
                            pe.wait_ge(v_nmt, t.n + 1)
                            combine(t.next(2))
                        if pr == 4:
                            if lp == 1:
                                wait_bank = (v_comb, t.n + 3 - NB)
                            elif lr is not None:
                                wait_bank = (v_log, finished(lr, t.n - 1) + 1)
                            else:
                                wait_bank = (v_nmt, t.n + 1)
                            pe.wait_ge(*wait_bank)
                            spread(t, 0)
                        if pr >= 4 and la is not None:
                            scores(q, la, 2 * (pr - 4))
                            scores(q, la, 2 * (pr - 4) + 1)
                    pe.wait_ge(v_sel, 2 * t.n + 1)
                    spread(t, 1)
                    pe.wait_ge(v_sel, 2 * t.n + 2)
                    pe.wait_ge(v_on, 2 * t.n + 2)
                    r = lc % 2
                    for a in range(TT):
                        for i in range(4):
                            ins = mm(PM[:, a * C:(a + 1) * C], OT[:, i, a * P:(a + 1) * P], WO[r][:, i, :],
                                     start=(i == 0), stop=(i == 3))
                    ins.then_inc(p_wo, 1)
                else:
                    if lp == 1:
                        wait(pe, v_comb, t.n + 2 - NB)
                        combine(t.next(2))
                    if lr is not None:
                        router_turn(t.next(-1), lr, None)
                        router_logits(t.next(-1), lr)
                    if la is not None:
                        for hp in range(8):
                            scores(q, la, hp)

            def router_turn(z, layer, lc):
                k = finished(layer, z.n)
                pe.wait_ge(v_xr, k + 1)
                if lc is None:
                    pe.wait_ge(v_res, z.n + 1)
                else:
                    pe.wait_ge(v_nmt, z.n + 2)
                for ct in range(CT):
                    for a in range(TT):
                        ins = nc.tensor.transpose(PM[:, ct * T + a * P:ct * T + (a + 1) * P], XRS[:, a, ct * P:(ct + 1) * P], ident)
                ins.then_inc(p_rt, 1)

            def router_logits(z, layer):
                k = finished(layer, z.n)
                pe.wait_ge(v_xrt, k + 1)
                for a in range(TT):
                    for ct in range(CT):
                        ins = mm(PM[:, a * NE:(a + 1) * NE], XRT[:, ct, a * P:(a + 1) * P], GATE[:, layer // 2, ct, :],
                                 start=(ct == 0), stop=(ct == CT - 1))
                ins.then_inc(p_log, 1)

            def combine(z):
                b = z.batch(1)
                pe.wait_ge(v_wct, z.n - NB + 1)
                for a in range(TT):
                    for i in range(NE // 2):
                        ins = mm(PM[:, a * C:(a + 1) * C], WCT[z.par][:, i, a * P:(a + 1) * P], yall[:, b * (NE // 2) + i, :],
                                 start=(i == 0), stop=(i == NE // 2 - 1))
                ins.then_inc(p_comb, 1)

            attention_rounds_0(pe, body)
            pe.wait_ge(v_topk, 5)
            for a in range(TT):
                ins = nc.tensor.transpose(PM[0:NB * NE, a * P:(a + 1) * P], PR[:, a].rearrange("p b e -> p (b e)"), ident)
            ins.then_inc(p_topk, 1)
            pe.wait_ge(v_topk, TOPK_STEPS)
            for a in range(TT):
                ins = nc.tensor.transpose(PM[:, a * NB * NE:(a + 1) * NB * NE], POS[:, a * P:(a + 1) * P], ident[0:NB * NE, 0:NB * NE])
            ins.then_inc(p_topk, 1)
            with pe.Fori(0, NB // 2) as m:
                for par in range(2):
                    b = 2 * m + par
                    pe.wait_ge(a_xst, b + 1)
                    pe.wait_ge(v_gsel, TT * (b + 1))
                    for c in range(CT):
                        pe.wait_ge(a_xi if c == 0 else v_xi, b)
                        for a in range(TT):
                            ins = mm(PTT[par][:, c, :], XST[par][:, a, c * P:(c + 1) * P], GSEL[par][:, a].rearrange("p e s -> p (e s)"),
                                     start=(a == 0), stop=(a == TT - 1))
                        ins.then_inc(p_disp, 1)
            pe.wait_ge(a_xi, NB)
            pe.wait_ge(v_xi, NB)

            def turn_inputs(m, par):
                e = 2 * m + par
                pe.wait_ge(s_zs[par], 16 * (m - NE // 2 + 1))
                for c in range(CT):
                    j = (uses(1) * par + c) % 4
                    wait(pe, a_h, use0(1, e) + c - 3)
                    for st in range(ST):
                        ins = nc.tensor.transpose(PTT[j // 2][:, j % 2, st * P:(st + 1) * P], ZS[par][:, st, c * P:(c + 1) * P], ident)
                    ins.then_inc(p_h, 1)

            def hidden(m, par, layer):
                e = 2 * m + par
                pe.wait_ge(s_ew[par], 32 * (m + 1))
                if layer == 1:
                    pe.wait_ge(a_h, use0(1, e) + CT)
                for f in range(FT):
                    k = use0(layer, e) + uses(layer) - FT + f
                    j = (uses(layer) * par + uses(layer) - FT + f) % 4
                    wait(pe, a_h, k - 3)
                    for c in range(CT):
                        rhs = xint[:, c, bass.ts(e, SLOT)] if layer == 0 else ZT[par][:, c, :]
                        ins = mm(PTT[j // 2][:, j % 2, :], W1[par][:, c, f * P:(f + 1) * P], rhs, start=(c == 0), stop=(c == CT - 1))
                    ins.then_inc(p_h, 1)

            def outputs(m, par, layer, st):
                e = 2 * m + par
                if st == 0:
                    pe.wait_ge(a_h, use0(layer, e + 1))
                bk = (PS[0], PS[1], PO, PM)[st]
                wait(pe, v_y, ST * e + st - 3)
                for f in range(FT):
                    ins = mm(bk[:, 0:C], ht[:, par, f, st * P:(st + 1) * P], W2[par][:, f, :], start=(f == 0), stop=(f == FT - 1))
                ins.then_inc(p_y, 1)

            def step(layer):
                def go(m, par, last):
                    q = Turn(m, par)
                    if not last:
                        hidden(q.next().m, q.next().par, layer)
                    for st in range(ST):
                        outputs(m, par, layer, st)
                        if st == 2 and layer == 1 and not last and not (isinstance(m, int) and m > NE // 2 and par == 0):
                            turn_inputs(q.next(2).m, q.next(2).par)
                return go

            expert_rounds(pe, lambda: hidden(0, 0, 0), step(0), 0)
            attention_rounds_12(pe, body)
            pe.wait_ge(v_rt, PICK_STEPS)
            picks = PICK.rearrange("p k i e -> p (k i e)")
            mm(PS[0][:, 0:2 * NT * NE], tri, picks, start=True, stop=True).then_inc(p_rte, 1)
            mm(PS[1][:, 0:2 * NT * NE], ONES[:, :], picks, start=True, stop=True).then_inc(p_rte, 1)

            def first():
                turn_inputs(NE // 2, 0)
                hidden(NE // 2, 0, 1)
                turn_inputs(NE // 2, 1)
            expert_rounds(pe, first, step(1), 1)


def layout(inputs):
    import numpy as np

    a = {k: np.asarray(v) for k, v in inputs.items()}
    f32 = np.float32

    def heads(w):
        return w.reshape(*w.shape[:-1], NH // 2, CT, HD).swapaxes(-3, -2).swapaxes(-2, -1).reshape(w.shape)

    w3, wo, bqk, bv = [], [], [], []
    for wq, wk, wv, w_o, bq, bk, b_v, bo in (
        [a[f"L0_xattn_{n}"] for n in ("Wq", "Wk", "Wv", "Wo", "bq", "bk", "bv", "bo")],
        [a[f"L1_xattn_{n}"].T for n in ("wq", "wk", "wv", "wo", "bq", "bk", "bv", "bo")],
        [a[f"L1_ffn_{n}"] for n in ("wq", "wk", "wv", "wo", "bq", "bk", "bv", "bo")],
    ):
        w3.append(np.stack([heads(wq), heads(wk), wv]))
        rows = np.zeros((4, 4, 32, C), f32)
        rows[:, :, 1:1 + HD] = w_o.reshape(4, 4, HD, C)
        rows[0, 0, 0] = bo
        wo.append(rows.reshape(4, P, C).swapaxes(0, 1))
        bqk.append(np.stack([heads(bq).reshape(CT, P), heads(bk).reshape(CT, P)]).transpose(2, 0, 1))
        bv.append(b_v)

    cf = np.zeros((P, NCF), f32)
    p = np.arange(P)

    def put(name, value):
        cf[:, CF[name][0]:CF[name][1]] = value

    put("ident", np.eye(P))
    put("sel", p[:, None] == 32 * (p[None, :] // 32))
    put("tri", p[:, None] <= p[None, :])
    put("iota", np.arange(CAP0)[None, :])
    put("slot", (p % CAP0)[:, None])
    put("rev", NE - np.arange(NE)[None, :])
    put("base", SLOT * np.arange(NE)[None, :])
    put("keep", (np.arange(2 * NE * NT) % NT != 0)[None, :])
    k = np.arange(T)
    dist = np.abs((k[:, None] - k[None, :]).reshape(TT, P, T)).transpose(1, 0, 2).reshape(P, TT * T)
    cb = (np.concatenate([np.eye(P), dist], 1).astype(f32).view(np.uint32) >> 16).astype(np.uint16)
    mask = a["mask_Bx1xSxS2_bf1"].reshape(NB, T, T)
    mask = np.stack([mask, mask.swapaxes(1, 2)], 1).view(np.uint8)
    c = np.ascontiguousarray
    return {
        "x": c(a["x"]), "ctxT": c(a["ctx_1024"].swapaxes(1, 2)), "maskp": c(mask), "cf": cf, "cb": cb,
        "wqkv": c(np.stack(w3)), "wo": c(np.stack(wo)), "bqk": c(np.stack(bqk)), "bv": c(np.stack(bv)),
        "gates": c(np.stack([a["L0_ffn_gate_w"], a["L1_ffn_wr"]])), "td": c(a["L1_xattn_time_decay"].reshape(1)),
        "lnp": c(np.stack([a[f"L1_ffn_ln{i}_{n}"] for i in (1, 2) for n in "gb"])),
        "w1": c(np.stack([a["L0_ffn_w1"], a["L1_ffn_w1"]])), "b1": c(a["L1_ffn_b1"].reshape(NE, FT, P).swapaxes(1, 2)),
        "w2": c(np.stack([a["L0_ffn_w2"], a["L1_ffn_w2"]])), "b2": c(a["L1_ffn_b2"]),
    }


def kernel(**inputs):
    import concourse.bacc as bacc
    from concourse.bass_utils import run_bass_kernel_spmd

    arrays = layout(inputs)
    nc = bacc.Bacc("TRN2", target_bir_lowering=False, num_devices=1)
    args = [nc.dram_tensor(f"in_{n}", v.shape, mybir.dt.from_np(v.dtype), kind="ExternalInput").ap() for n, v in arrays.items()]
    args.append(nc.dram_tensor("out_0", (NB, T, C), F32, kind="ExternalOutput").ap())
    bass_two_layer_cross_attention_moe(nc, *args)
    got = run_bass_kernel_spmd(nc, [{f"in_{n}": v for n, v in arrays.items()}], core_ids=[0])
    return got.results[0]["out_0"]
```

```python
import concourse.bass as bass
from concourse import mybir
from contextlib import ExitStack

F32 = mybir.dt.float32
BF16 = mybir.dt.bfloat16
U8 = mybir.dt.uint8
U32 = mybir.dt.uint32
ALU = mybir.AluOpType
ACT = mybir.ActivationFunctionType
AX = mybir.AxisListType

P = 128
NB = 8
T = 256
C = 256
TT = T // P
CT = C // P
NH = 16
HD = C // NH
NE = 8
FF = 1024
FT = FF // P
CAP0 = 64
SLOT = 512
ST = SLOT // P
NT = NB * TT
TERMS = 6
KSTK = TERMS * HD
NPART = 3
TOPK_STEPS = 6 + 2 * (CAP0 // 8) + 4
PICK_STEPS = 5 + 5 + 6
HEAD_STEPS = 2 * (2 + 3)
ROUTE_STEPS = PICK_STEPS + 5 + 6 + 4
BIG = 2.0 ** 100
HUGE = 2.0 ** 120
EPS = 1e-5

Q_TERM = [0, 0, 1, 0, 2, 1]
K_TERM = [0, 1, 0, 2, 0, 1]

CF = {}
_at = 0
for _name, _w in (("ident", P), ("tri", P), ("iota", CAP0), ("slot", 1), ("rev", NE), ("base", NE),
                  ("keep", 2 * NE * NT)):
    CF[_name] = (_at, _at + _w)
    _at += _w
NCF = _at


def wait(eng, sem, value):
    if isinstance(value, int) and value <= 0:
        return
    eng.wait_ge(sem, value)


def alone(eng):
    eng.nop(nofuse=True)


class Steps:

    def __init__(self, eng, sem, base):
        self.eng, self.sem, self.base, self.k = eng, sem, base, 0

    def step(self, ins, by=1):
        ins.then_inc(self.sem, by)
        self.k += by

    def settle(self):
        self.eng.wait_ge(self.sem, self.base + self.k)


class Turn:

    def __init__(self, m, par, phase=0):
        self.m, self.par, self.phase = m, par, phase
        self.n = 2 * m + par

    def next(self, k=1):
        q = self.par + k
        return Turn(self.m + q // 2, q % 2, self.phase)

    def batch(self, layer):
        return self.n - NB * layer

    def done(self, ahead):
        k = self.n + ahead
        if isinstance(k, int):
            k = min(max(k, NB * self.phase), NB if self.phase == 0 else 3 * NB)
        return k


def attention_rounds_0(eng, body):
    body(Turn(-2, 1), 0, None, None, None, None)
    body(Turn(-1, 0), 0, 0, None, None, None)
    body(Turn(-1, 1), 0, 0, 0, None, None)
    body(Turn(0, 0), 0, 0, 0, 0, None)
    with eng.Fori(0, 2) as m:
        body(Turn(m, 1), 0, 0, 0, 0, 0)
        body(Turn(m + 1, 0), 0, 0, 0, 0, 0)
    body(Turn(2, 1), None, 0, 0, 0, 0)
    body(Turn(3, 0), None, None, 0, 0, 0)
    body(Turn(3, 1), None, None, None, 0, 0)
    body(Turn(4, 0), None, None, None, None, 0)


def attention_rounds_12(eng, body):
    body(Turn(2, 1, 1), 1, None, None, None, None)
    body(Turn(3, 0, 1), 1, 1, None, None, None)
    body(Turn(3, 1, 1), 1, 1, 1, None, None)
    body(Turn(4, 0, 1), 1, 1, 1, 1, None)
    with eng.Fori(4, 6) as m:
        body(Turn(m, 1, 1), 1, 1, 1, 1, 1)
        body(Turn(m + 1, 0, 1), 1, 1, 1, 1, 1)
    body(Turn(6, 1, 1), 2, 1, 1, 1, 1)
    body(Turn(7, 0, 1), 2, 2, 1, 1, 1)
    body(Turn(7, 1, 1), 2, 2, 2, 1, 1)
    body(Turn(8, 0, 1), 2, 2, 2, 2, 1)
    with eng.Fori(8, 10) as m:
        body(Turn(m, 1, 1), 2, 2, 2, 2, 2)
        body(Turn(m + 1, 0, 1), 2, 2, 2, 2, 2)
    body(Turn(10, 1, 1), None, 2, 2, 2, 2)
    body(Turn(11, 0, 1), None, None, 2, 2, 2)
    body(Turn(11, 1, 1), None, None, None, 2, 2)
    body(Turn(12, 0, 1), None, None, None, None, 2)


def routed(layer, n):
    return n if layer == 0 else n - NB


def routes(lo):
    return None if lo == 1 else lo


def bass_two_layer_cross_attention_moe(
    nc, x, ctxT, maskp, cf, cb, wqkv, wo, bqk, bv, gates, td, lnp, w1, b1, w2, b2, out,
):
    posd = nc.dram_tensor("slot_of_token", [NB * NE, T], F32, kind="Internal").ap()
    prbd = nc.dram_tensor("prob_of_token", [NB * NE, T], F32, kind="Internal").ap()
    zbuf = nc.dram_tensor("expert_inputs", [NE * SLOT, C], F32, kind="Internal").ap()
    ybuf = nc.dram_tensor("expert_outputs", [NE * SLOT, C], F32, kind="Internal").ap()

    with ExitStack() as ctx:
        def sb(name, shape, dt=F32):
            return ctx.enter_context(nc.sbuf_tensor(name, shape, dt))

        def sem(name):
            return ctx.enter_context(nc.semaphore(name))

        Xall = sb("Xall", [P, NT, C])
        XNall = sb("XNall", [P, NT, C])
        XINT = sb("XINT", [P, CT * NE * SLOT])
        YALL = sb("YALL", [P, NB * (NE // 2) * C])
        STK = sb("STK", [P, 2 * 2 * NH * T], BF16)
        WREG = sb("WREG", [P, 2 * (CT * FF + FT * C)])

        xint = XINT[:, :].rearrange("p (c s) -> p c s", c=CT)
        yall = YALL[:, :].rearrange("p (i c) -> p i c", c=C)
        stk = STK[:, :].rearrange("p (r w h t) -> p r w h t", r=2, w=2, h=NH)
        QS = [stk[:, r, 0] for r in range(2)]
        KS = [stk[:, r, 1] for r in range(2)]
        ht = STK[:, :].bitcast(F32).rearrange("p (r f s) -> p r f s", r=2, f=FT)
        W1 = [WREG[:, r * CT * FF:(r + 1) * CT * FF].rearrange("p (c f) -> p c f", c=CT) for r in range(2)]
        o = 2 * CT * FF
        W2 = [WREG[:, o + r * FT * C:o + (r + 1) * FT * C].rearrange("p (f c) -> p f c", f=FT) for r in range(2)]

        def carve(region, start, *shape, dt=F32):
            size = 1
            for s in shape:
                size *= s
            v = region[:, start:start + (size if dt == F32 else size // (2 if dt == BF16 else 4))]
            if dt != F32:
                v = v.bitcast(dt)
            names = "abcdef"[:len(shape)]
            if len(shape) > 1:
                kw = {names[i]: shape[i] for i in range(1, len(shape))}
                v = v.rearrange(f"p ({' '.join(names)}) -> p {' '.join(names)}", **kw)
            return v

        CTX = [carve(WREG, 512 * r, CT, T) for r in range(2)]
        BPOS = carve(WREG, 1024, NE // 2, T)
        BPRB = carve(WREG, 2048, NE // 2, T)
        WCT = [carve(WREG, 3072 + 1024 * r, NE // 2, T) for r in range(2)]
        XNT = carve(WREG, 5120, CT, T)
        QK32 = carve(WREG, 5632, 2, TT, T)
        XNS = carve(WREG, 6656, TT, C)
        XRS = carve(WREG, 7168, TT, C)
        OQ = carve(WREG, 7680, 2, T)
        MASKU = [carve(YALL, 256 * r, 2, TT, T, dt=U8) for r in range(2)]
        BMK = [carve(YALL, 512 + 512 * r, 2, TT, T, dt=BF16) for r in range(2)]
        GSEL = [carve(YALL, 2048 * (1 + r), TT, NE, CAP0) for r in range(2)]
        XST = [carve(YALL, 6144 + 512 * r, TT, C) for r in range(2)]
        LNP = carve(YALL, 0, 4, C)
        UALL = carve(XINT, 0, NT, C)
        PT = [carve(XINT, 4096 + 1024 * r, 2, TT, T) for r in range(2)]
        OT = carve(XINT, 6144, 4, T)
        XRT = carve(XINT, 7168, CT, T)

        PTK = carve(YALL, 7168, T)[0:NB * NE]
        WORK = carve(YALL, 7424, T)[0:NB * NE]
        CHOSEN = carve(YALL, 7680, T)[0:NB * NE]
        POS = carve(YALL, 7936, T)[0:NB * NE]
        ZS = [carve(YALL, 1024 * r, ST, C) for r in range(2)]
        ZT = [carve(YALL, 2048 + 1024 * r, CT, SLOT) for r in range(2)]
        YS = [carve(YALL, 4096 + 1024 * r, ST, C) for r in range(2)]
        B2B = [carve(YALL, 6144 + 256 * r, C) for r in range(2)]
        B1S = [carve(YALL, 6656 + FT * r, FT) for r in range(2)]
        PRR = carve(XINT, 4096, NT, NE)
        EQ = carve(XINT, 4224, NT, NE)
        PICK = carve(XINT, 4352, 2, NT, NE)
        TOT = carve(XINT, 4608, 2, NE, NT)
        SCN = carve(XINT, 4864, 2, NE, NT)
        EXC = carve(XINT, 5120, 2, NE, NT)
        LOC = carve(XINT, 5376, 2, NT, NE)
        TMP = carve(XINT, 5632, 2, NT, NE)
        GOT = [carve(XINT, 4096 * w, NT, C) for w in range(2)]

        WQKV = [sb(f"WQKV{r}", [P, 3, CT, C]) for r in range(2)]
        WO = [sb(f"WO{r}", [P, 4, C]) for r in range(2)]
        BQK = [sb(f"BQK{r}", [P, 2, CT]) for r in range(2)]
        BQ4 = [sb(f"BQ4{r}", [P, CT]) for r in range(2)]
        BV = [sb(f"BV{r}", [P, C]) for r in range(2)]
        GATE = sb("GATE", [P, 2, CT, NE])
        TD = sb("TD", [P, 1])
        cfs = sb("cfs", [P, NCF])
        cbs = sb("cbs", [P, P + TT * T], BF16)
        TDI = sb("TDI", [P, NPART, P], BF16)
        TDP = sb("TDP", [P, NPART + 2])
        TDB = sb("TDB", [P, NPART], BF16)
        ONES = sb("ONES", [P, P])
        POWH = sb("POWH", [P, TT])

        def cst(name):
            return cfs[:, CF[name][0]:CF[name][1]]

        ident, tri = cst("ident"), cst("tri")
        identb = cbs[:, 0:P]
        dist = cbs[:, P:].rearrange("p (a t) -> p a t", a=TT)

        QKP = [sb(f"QKP{i}", [P, 2, CT, T], BF16) for i in range(NPART)]
        VA = [sb(f"VA{r}", [P, TT, NH, 32]) for r in range(2)]
        RS = sb("RS", [P, 2 * T // 32])
        MX = sb("MX", [P, TT, NH])
        NM = sb("NM", [P, 2, TT, NH])
        NMP = sb("NMP", [P, TT, NPART, NH], BF16)
        NMT = sb("NMT", [NPART * NH, T], BF16)
        STATS = sb("STATS", [P, TT, 6])
        MV = sb("MV", [P, TT, 2])
        VE = sb("VE", [P, TT])
        RSTD = sb("RSTD", [P, TT])
        LOG = sb("LOG", [P, NT, NE])
        PR = sb("PR", [P, TT, NB, NE])
        SM = sb("SM", [P, NT])
        SMR = sb("SMR", [P, NT])
        TOP8 = sb("TOP8", [NB * NE, 8])
        ZERO = sb("ZERO", [P, C])
        LS = sb("LS", [P, 2, NT])
        ES = sb("ES", [P, 2, NT])
        FIT = sb("FIT", [P, 2, NT])
        G12 = sb("G12", [P, 2, NT])
        IDXF = sb("IDXF", [P, 2, NT])
        IDX = [sb(f"IDX{w}", [P, 2, NT], U32) for w in range(2)]
        POST = sb("POST", [P, TT, NB * NE])

        PS = [ctx.enter_context(nc.psum_tensor(f"PS{i}", [P, 512], F32)) for i in range(2)]
        PTT = [ctx.enter_context(nc.psum_tensor(f"PTT{i}", [P, 2, 512], F32)) for i in range(2)]
        PO = ctx.enter_context(nc.psum_tensor("PO", [P, 512], F32))
        PM = ctx.enter_context(nc.psum_tensor("PM", [P, 512], F32))
        nm_bf = PO[:, :].bitcast(BF16)[0:NPART * NH, 2 * T:3 * T]

        s_const = sem("const_loaded")
        s_x0 = sem("x_first_loaded")
        s_x = sem("x_loaded")
        s_w = [sem(f"attn_weights_loaded{i}") for i in range(3)]
        s_ctx = [sem(f"ctx_loaded{r}") for r in range(2)]
        s_msk = [sem(f"mask_loaded{r}") for r in range(2)]
        s_stk = [sem(f"stack_loaded{r}") for r in range(2)]
        s_nml = [sem(f"negmax_loaded{r}") for r in range(2)]
        s_bc = sem("slot_rows_loaded")
        s_rows = sem("slot_rows_stored")
        g_const = sem("pool_constants")
        g_mask = sem("mask_converted")
        g_rstd = sem("rstd_ready")
        g_copy = sem("router_input_kept")
        v_const = sem("dve_constants")
        v_bank = sem("score_bank_read_dve")
        a_bank = sem("score_bank_read_act")
        v_split = sem("parts_subtracted")
        v_nm = sem("negmax_step")
        v_nmt = sem("negmax_rows_ready")
        v_lnp = sem("prep_norm_step")
        v_lnr = sem("router_norm_step")
        v_xn = sem("attn_input_ready")
        v_xr = sem("router_input_ready")
        a_xrt = sem("router_input_transposed")
        v_log = sem("logits_read")
        v_ot = sem("heads_step")
        v_wct = sem("combine_weights_ready")
        v_comb = sem("combined")
        v_res = sem("residual_added")
        a_split = sem("parts_rounded")
        a_exp = sem("probs_ready")
        p_a = sem("projection_written")
        p_s = sem("scores_written")
        p_nm = sem("negmax_transposed")
        p_st = sem("shifted_scores_ready")
        p_pv = sem("head_group_done")
        p_wo = sem("attn_out_ready")
        p_rt = sem("router_input_turned")
        p_log = sem("logits_ready")
        p_comb = sem("combine_ready")
        v_base = sem("output_base_ready")
        v_topk = sem("topk_step")
        a_topk = sem("router_exp_ready")
        p_topk = sem("topk_turned")
        v_gsel = sem("gather_matrix_ready")
        a_xst = sem("token_rows_staged")
        p_disp = sem("expert_inputs_ready")
        v_xi = sem("expert_inputs_read_dve")
        a_xi = sem("expert_inputs_read_act")
        s_ew = [sem(f"expert_weights_loaded{r}") for r in range(2)]
        s_zs = [sem(f"slot_rows_in{r}") for r in range(2)]
        s_b12 = [sem(f"expert_biases_loaded{r}") for r in range(2)]
        p_h = sem("hidden_bank_written")
        a_h = sem("hidden_bank_read")
        p_y = sem("expert_output_written")
        v_y = sem("expert_output_read")
        s_lnp = sem("norm_params_loaded")
        s_zero = sem("expert_inputs_cleared")
        v_rt = sem("routing_step")
        a_rt = sem("routing_exp_ready")
        p_rte = sem("choices_counted")
        s_scat = sem("tokens_scattered")
        s_yst = [sem(f"expert_output_stored{r}") for r in range(2)]
        s_got = [sem(f"outputs_gathered{g}") for g in range(4)]
        v_out = sem("output_rows_ready")
        s_out = sem("output_stored")

        block = ctx.enter_context(nc.Block())

        def nln(layer, n):
            return 5 * n if layer < 2 else 13 * n - (13 - 5) * 2 * NB

        def nrt(k, layer):
            return 5 * k if layer == 0 else 7 * k - 2 * NB

        def expert_rounds(eng, first, step, layer):
            base = NE // 2 * layer
            first()
            step(base, 0, False)
            step(base, 1, False)
            with eng.Fori(base + 1, base + NE // 2 - 1) as m:
                step(m, 0, False)
                step(m, 1, False)
            step(base + NE // 2 - 1, 0, False)
            step(base + NE // 2 - 1, 1, True)

        def uses(layer):
            return FT if layer == 0 else FT + CT

        def use0(layer, e):
            return FT * e if layer == 0 else (FT + CT) * e - CT * NE

        @block.sync
        def _(sp):
            def held(sem, value):
                wait(sp, sem, value)
                alone(sp)

            sp.dma_start(Xall[:, 0:TT, :], x[0].rearrange("(a p) c -> p a c", p=P)).then_inc(s_x0, 16)
            sp.dma_start(cfs[:, :], cf).then_inc(s_const, 16)
            sp.dma_start(cbs[:, :], cb.bitcast(BF16)).then_inc(s_const, 16)
            sp.dma_start(TD[:, :], td.partition_broadcast(P)).then_inc(s_const, 16)
            sp.dma_start(GATE[:, :, :, :], gates.rearrange("l (a p) e -> p l a e", p=P)).then_inc(s_const, 16)

            def load_attn(layer):
                r = layer % 2
                sp.dma_start(WQKV[r][:, :, :, :], wqkv[layer].rearrange("w (a p) c -> p w a c", p=P)).then_inc(s_w[layer], 16)
                sp.dma_start(BQK[r][:, :, :], bqk[layer]).then_inc(s_w[layer], 16)
                sp.dma_start(BV[r][:, :], bv[layer].partition_broadcast(P)).then_inc(s_w[layer], 16)
                sp.dma_start(WO[r][:, :, :], wo[layer]).then_inc(s_w[layer], 16)

            load_attn(0)

            def body(t, lp, la, ls, lc, lo):
                z, q = t.next(3), t.next(2)
                if lc is not None:
                    held(v_nmt, t.n + 1)
                    sp.dma_start(QS[t.par][KSTK:KSTK + NPART, :, :], NMT[:, :]).then_inc(s_nml[t.par], 16)
                if lp is not None and lp < 2:
                    held(p_a, 4 * (z.n - 1))
                    sp.dma_start(CTX[z.par], ctxT[z.batch(lp)].rearrange("(a p) t -> p a t", p=P)).then_inc(s_ctx[z.par], 16)
                if lp == 0:
                    held(g_mask, 2 * (z.n - 1))
                    sp.dma_start(MASKU[z.par], maskp[z.batch(0)].rearrange("w (a p) k -> p w a k", p=P)).then_inc(s_msk[z.par], 16)
                if lp == 1:
                    held(v_wct, z.n - NB)
                    b = z.batch(1)
                    for dst, src in ((BPOS, posd), (BPRB, prbd)):
                        v = src.rearrange("(b i h) t -> b h i t", b=NB, h=2)
                        for half in range(2):
                            sp.dma_start(dst[half * 64:half * 64 + 64, :, :], v[b, half].partition_broadcast(64)).then_inc(s_bc, 16)
                if lp == 1 and isinstance(z.n, int) and z.n == NB + 1:
                    held(p_comb, 1)
                    sp.dma_start(LNP, lnp.partition_broadcast(P)).then_inc(s_lnp, 16)
                if la is not None:
                    held(v_split, 2 * (q.n + 1))
                    held(a_split, 2 * (q.n + 1))
                    held(p_st, 8 * (q.n - 1))
                    for j in range(TERMS):
                        for dst, w, term in ((QS, 0, Q_TERM), (KS, 1, K_TERM)):
                            sp.dma_start(dst[q.par][j * HD:(j + 1) * HD, :, :], QKP[term[j]][:, w, :, :]).then_inc(s_stk[q.par], 16)

            load_attn(1)
            for i in range(1, NB):
                sp.dma_start(Xall[:, TT * i:TT * i + TT, :], x[i].rearrange("(a p) c -> p a c", p=P)).then_inc(s_x, 16)
            attention_rounds_0(sp, body)
            sp.dma_start(zbuf.rearrange("(p k) c -> p k c", p=P), ZERO[:, :].unsqueeze(1).to_broadcast([P, NE * SLOT // P, C])).then_inc(s_zero, 16)
            held(p_wo, NB)
            load_attn(2)
            held(g_copy, NB + 1)
            held(p_log, NB)

            def load_expert(e, m, par, layer):
                held(p_y, ST * (2 * m + par - 1))
                sp.dma_start(W1[par], w1[layer, e].rearrange("(a p) f -> p a f", p=P)).then_inc(s_ew[par], 16)
                sp.dma_start(W2[par], w2[layer, e].rearrange("(f p) c -> p f c", p=P)).then_inc(s_ew[par], 16)

            load_expert(0, 0, 0, 0)
            load_expert(1, 0, 1, 0)
            held(v_topk, TOPK_STEPS)
            sp.dma_start(posd, POS).then_inc(s_rows, 16)
            sp.dma_start(prbd, PTK).then_inc(s_rows, 16)
            with sp.Fori(1, NE // 2) as m:
                load_expert(2 * m, m, 0, 0)
                load_expert(2 * m + 1, m, 1, 0)
            held(s_rows, 32)
            held(p_y, ST * NE)
            attention_rounds_12(sp, body)

            held(g_copy, 2 * NB + 1)
            held(p_log, 2 * NB)
            half = NE // 2

            def load_expert_1(m, par):
                e = 2 * m + par - NE
                load_expert(e, m, par, 1)
                held(v_y, ST * (2 * m + par - 1))
                sp.dma_start(B1S[par], b1[e]).then_inc(s_b12[par], 16)
                sp.dma_start(B2B[par], b2[e].partition_broadcast(P)).then_inc(s_b12[par], 16)

            def load_slots(m, par):
                e = 2 * m + par - NE
                held(p_h, use0(1, 2 * m + par - 1 - 1) + CT)
                sp.dma_start(ZS[par], zbuf.rearrange("(e a p) c -> e p a c", e=NE, p=P)[e]).then_inc(s_zs[par], 16)

            def store_slots(m, par):
                e = 2 * m + par - NE
                held(v_y, ST * (2 * m + par + 1))
                sp.dma_start(ybuf.rearrange("(e a p) c -> e p a c", e=NE, p=P)[e], YS[par]).then_inc(s_yst[par], 16)

            load_expert_1(half, 0)
            load_expert_1(half, 1)
            held(s_scat, 16 * 2 * NT)
            for par in range(2):
                sp.dma_start(ZS[par], zbuf.rearrange("(e a p) c -> e p a c", e=NE, p=P)[par]).then_inc(s_zs[par], 16)
            with sp.Fori(half + 1, 2 * half) as m:
                for par in range(2):
                    load_slots(m, par)
                    load_expert_1(m, par)
                    store_slots(m - 1, par)
            for par in range(2):
                store_slots(2 * half - 1, par)
            for g in range(4):
                held(v_out, g + 1)
                sp.dma_start(out.rearrange("b (a p) c -> p (b a) c", p=P)[:, 4 * g:4 * g + 4, :], Xall[:, 4 * g:4 * g + 4, :]).then_inc(s_out, 16)
            held(s_out, 64)

        @block.gpsimd
        def _(pool):
            nc.gpsimd.memset(ONES[:, :], 1.0).then_inc(g_const, 1)
            nc.gpsimd.memset(POWH[:, :], -0.5).then_inc(g_const, 1)

            def rstd(sem_ve, value):
                pool.wait_ge(sem_ve, value)
                nc.gpsimd.tensor_tensor(RSTD[:, :], VE[:, :], POWH[:, :], ALU.pow).then_inc(g_rstd, 1)

            pool.wait_ge(g_const, 2)
            nc.gpsimd.memset(XNall[:, 0, 0:1], 0.0).then_inc(g_copy, 1)

            def convert_mask(q, which):
                nc.gpsimd.tensor_scalar(BMK[q.par][:, which], MASKU[q.par][:, which], 1.0, BIG, ALU.subtract, ALU.mult).then_inc(g_mask, 1)

            def body(t, lp, la, ls, lc, lo):
                lr = routes(lo)
                z, q = t.next(3), t.next(2)
                if la == 0:
                    pool.wait_ge(s_msk[q.par], 16 * (q.m + 1))
                    wait(pool, p_s, 16 * (q.n - 1))
                    alone(pool)
                    convert_mask(q, 0)
                if lr is not None:
                    y = t.next(-1)
                    k = routed(lr, y.n)
                    rstd(v_lnr, nrt(k, lr) + 5)
                    pool.wait_ge(v_xr, k + 1)
                    nc.gpsimd.tensor_copy(XNall[:, bass.ts(y.batch(lr), TT), :], XRS).then_inc(g_copy, 1)
                if lp is not None:
                    rstd(v_lnp, nln(lp, z.n) + 5)
                    if lp == 2:
                        rstd(v_lnp, nln(lp, z.n) + 11)
                if la == 0:
                    wait(pool, p_st, 8 * (q.n - 1))
                    alone(pool)
                    convert_mask(q, 1)

            attention_rounds_0(pool, body)
            attention_rounds_12(pool, body)
            pool.wait_ge(s_zero, 16)
            pool.wait_ge(v_rt, ROUTE_STEPS)
            pool.wait_ge(g_copy, 2 * NB + 1)
            for k in range(2):
                for i in range(NT):
                    nc.gpsimd.indirect_dma_start(
                        out=zbuf, out_offset=bass.IndirectOffsetOnAxis(ap=IDX[0][:, k, i:i + 1], axis=0),
                        in_=XNall[:, i, :], in_offset=None, bounds_check=NE * SLOT - 1, oob_is_err=False).then_inc(s_scat, 16)
            for r in range(2):
                pool.wait_ge(s_yst[r], 16 * NE // 2)
            for i in range(NT):
                for k in range(2):
                    nc.gpsimd.indirect_dma_start(
                        out=GOT[k][:, i, :], out_offset=None, in_=ybuf,
                        in_offset=bass.IndirectOffsetOnAxis(ap=IDX[1][:, k, i:i + 1], axis=0),
                        bounds_check=NE * SLOT - 1, oob_is_err=False).then_inc(s_got[i // 4], 16)

        @block.scalar
        def _(act):
            def body(t, lp, la, ls, lc, lo):
                lr = routes(lo)
                q = t.next(2)

                def middle_parts():
                    act.wait_ge(v_split, 2 * q.n + 1)
                    nc.scalar.copy(QKP[1][:, :, :, :], QK32).then_inc(a_split, 1)

                if la is not None:
                    r = la % 2
                    if isinstance(q.n, int) and q.n % NB == 0:
                        act.wait_ge(v_const, 16 + q.n // NB)
                        act.wait_ge(s_w[la], 64)
                    act.wait_ge(p_a, 4 * q.n + 1)
                    nc.scalar.copy(XNT.rearrange("p a t -> p (a t)"), PS[0][:, :]).then_inc(a_bank, 1)
                    act.wait_ge(p_a, 4 * q.n + 2)
                    wait(act, v_split, 2 * q.n)
                    for c in range(CT):
                        ins = nc.scalar.activation(QK32[:, 0, c, :], PS[1][:, c * T:(c + 1) * T], ACT.Identity, bias=BQ4[r][:, c:c + 1], scale=0.25)
                    ins.then_inc(a_bank, 1)
                    act.wait_ge(p_a, 4 * q.n + 3)
                    for c in range(CT):
                        ins = nc.scalar.activation(QK32[:, 1, c, :], PS[0][:, c * T:(c + 1) * T], ACT.Identity, bias=BQK[r][:, 1, c:c + 1])
                    ins.then_inc(a_bank, 1)
                    act.wait_ge(a_bank, 3 * q.n + 3)
                    prev = q.next(-1)
                    if not (isinstance(prev.n, int) and prev.n < 0):
                        act.wait_ge(s_stk[prev.par], 192 * (prev.m + 1))
                    nc.scalar.copy(QKP[0][:, :, :, :], QK32).then_inc(a_split, 1)
                    if lc is None:
                        middle_parts()
                if lc is not None:
                    for pr in range(NH // 2):
                        act.wait_ge(p_st, 8 * t.n + pr + 1)
                        wait(act, p_pv, 8 * t.n + pr - 1)
                        nc.scalar.activation(PT[pr % 2].rearrange("p h a t -> p (h a t)"),
                                             PTT[pr % 2][:, :, :].rearrange("p h k -> p (h k)"), ACT.Exp).then_inc(a_exp, 1)
                        if pr == 1 and la is not None:
                            middle_parts()
                        if pr == 4 and lr is not None:
                            router_input(routed(lr, t.n - 1))
                elif lr is not None:
                    router_input(routed(lr, t.n - 1))

            def router_input(k):
                act.wait_ge(p_rt, k + 1)
                nc.scalar.copy(XRT.rearrange("p a t -> p (a t)"), PM[:, :]).then_inc(a_xrt, 1)

            attention_rounds_0(act, body)

            act.wait_ge(v_topk, 2)
            nc.scalar.activation(LOG[:, :, :], LOG[:, :, :], ACT.Exp).then_inc(a_topk, 1)
            act.wait_ge(g_copy, NB + 1)
            with act.Fori(0, NB // 2) as m:
                for par in range(2):
                    b = 2 * m + par
                    act.wait_ge(p_disp, 2 * b)
                    nc.scalar.copy(XST[par], XNall[:, bass.ts(b, TT), :]).then_inc(a_xst, 1)
                    act.wait_ge(p_disp, 2 * b + 1)
                    nc.scalar.copy(xint[:, 0, :].rearrange("p (e b s) -> p e b s", e=NE, b=NB)[:, :, b, :],
                                   PTT[par][:, 0, :].rearrange("p (e s) -> p e s", e=NE)).then_inc(a_xi, 1)

            def hidden(m, par, layer):
                e = 2 * m + par
                wait(act, p_y, ST * (e - 1))
                if layer == 1:
                    act.wait_ge(s_b12[par], 32 * (m - NE // 2 + 1))
                for f in range(FT):
                    k = use0(layer, e) + uses(layer) - FT + f
                    j = (uses(layer) * par + uses(layer) - FT + f) % 4
                    act.wait_ge(p_h, k + 1)
                    src = PTT[j // 2][:, j % 2, :]
                    if layer == 0:
                        ins = nc.scalar.activation(ht[:, par, f, :], src, ACT.Gelu)
                    else:
                        ins = nc.scalar.activation(ht[:, par, f, :], src, ACT.Relu, bias=B1S[par][:, f:f + 1])
                    ins.then_inc(a_h, 1)

            def turned(m, par):
                e = 2 * m + par
                for c in range(CT):
                    j = (uses(1) * par + c) % 4
                    act.wait_ge(p_h, use0(1, e) + c + 1)
                    nc.scalar.copy(ZT[par][:, c, :], PTT[j // 2][:, j % 2, :]).then_inc(a_h, 1)

            def step(layer):
                def go(m, par, last):
                    q = Turn(m, par)
                    if not last:
                        hidden(q.next().m, q.next().par, layer)
                        if layer == 1 and not (isinstance(m, int) and m > NE // 2 and par == 0):
                            turned(q.next(2).m, q.next(2).par)
                return go

            expert_rounds(act, lambda: hidden(0, 0, 0), step(0), 0)
            attention_rounds_12(act, body)
            act.wait_ge(v_rt, 2)
            nc.scalar.activation(PRR, PRR, ACT.Exp).then_inc(a_rt, 1)

            def first():
                turned(NE // 2, 0)
                hidden(NE // 2, 0, 1)
                turned(NE // 2, 1)
            expert_rounds(act, first, step(1), 1)

        @block.vector
        def _(dve):
            nc.vector.memset(ZERO[:, :], 0.0)
            c = Steps(dve, v_const, 0)
            for r in range(2):
                c.step(nc.vector.memset(KS[r][KSTK:KSTK + 32, :, :], 1.0))
                c.step(nc.vector.memset(VA[r][:, :, :, :], 0.0))
            c.settle()
            for r in range(2):
                c.step(nc.vector.memset(VA[r][:, :, :, 0:1], 1.0))
            dve.wait_ge(s_const, 64)
            c.step(nc.vector.tensor_copy(TDB[:, 0:1], TD[:, :]))
            c.settle()
            c.step(nc.vector.tensor_tensor(TDP[:, 3:4], TD[:, :], TDB[:, 0:1], ALU.subtract))
            c.settle()
            c.step(nc.vector.tensor_copy(TDB[:, 1:2], TDP[:, 3:4]))
            c.settle()
            c.step(nc.vector.tensor_tensor(TDP[:, 4:5], TDP[:, 3:4], TDB[:, 1:2], ALU.subtract))
            c.settle()
            c.step(nc.vector.tensor_copy(TDB[:, 2:3], TDP[:, 4:5]))
            c.settle()
            c.step(nc.vector.tensor_scalar(TDP[:, 0:3], TDB[:, :], -1.0, None, ALU.mult))
            c.settle()
            for i in range(NPART):
                c.step(nc.vector.tensor_scalar(TDI[:, i, :], identb, TDP[:, i:i + 1], None, ALU.mult))

            def quarter_bias(layer):
                dve.wait_ge(s_w[layer], 64)
                c.step(nc.vector.tensor_scalar(BQ4[layer % 2][:, :], BQK[layer % 2][:, 0, :], 0.25, None, ALU.mult))
                c.settle()

            quarter_bias(0)

            def norm_begin(src, sem, base):
                s = Steps(dve, sem, base)
                alone(dve)
                for a in range(TT):
                    s.step(nc.vector.bn_stats(STATS[:, a, :], src(a)))
                s.settle()
                alone(dve)
                for a in range(TT):
                    s.step(nc.vector.bn_aggr(MV[:, a, :], STATS[:, a, :]))
                s.settle()
                s.step(nc.vector.tensor_scalar(VE[:, :], MV[:, :, 1], EPS, None, ALU.add))
                return s

            def norm_end(dst, src, s, powers, done, affine):
                dve.wait_ge(g_rstd, powers)
                for a in range(TT):
                    ins = nc.vector.tensor_scalar(dst[:, a, :], src(a), MV[:, a, 0:1], RSTD[:, a:a + 1], ALU.subtract, ALU.mult)
                if affine is not None or done is None:
                    s.step(ins)
                    s.settle()
                if affine is not None:
                    s.step(nc.vector.tensor_tensor(dst, dst, LNP[:, affine, :].unsqueeze(1).to_broadcast([P, TT, C]), ALU.mult))
                    s.settle()
                    ins = nc.vector.tensor_tensor(dst, dst, LNP[:, affine + 1, :].unsqueeze(1).to_broadcast([P, TT, C]), ALU.add)
                if done is not None:
                    ins.then_inc(done, 1)

            def powers_before(t, lo):
                if not isinstance(t.n, int):
                    return (2 * t.n + 2, t.n + NB + 3, 3 * t.n - 19)[lo]
                p = t.done(3)
                return p + max(0, p - 2 * NB) + (min(max(t.n - 1, 0), NB) if t.phase == 0 else NB + max(0, t.n - 1 - 2 * NB))

            def body(t, lp, la, ls, lc, lo):
                lr = routes(lo)
                z, q, y = t.next(3), t.next(2), t.next(-1)
                r = None if la is None else la % 2
                before = t.done(2) + 16 * t.done(1)
                powers = powers_before(t, lo)
                first = isinstance(t.n, int)

                if la is not None and first and q.n in (NB, 2 * NB):
                    quarter_bias(la)

                if lc is not None:
                    s = Steps(dve, v_nm, 6 * t.n)
                    dve.wait_ge(v_bank, before)
                    if lc == 0:
                        s.step(nc.vector.tensor_scalar(NM[:, 1], MX[:, :, :], -BIG / 2, HUGE, ALU.is_lt, ALU.mult))
                        s.settle()
                        s.step(nc.vector.tensor_tensor(NM[:, 0], NM[:, 1], MX[:, :, :], ALU.subtract))
                    else:
                        s.step(nc.vector.tensor_scalar(NM[:, 0], MX[:, :, :], -1.0, None, ALU.mult), 2)
                    s.settle()
                    s.step(nc.vector.tensor_copy(NMP[:, :, 0, :], NM[:, 0]))
                    s.settle()
                    s.step(nc.vector.tensor_tensor(NM[:, 1], NM[:, 0], NMP[:, :, 0, :], ALU.subtract))
                    s.settle()
                    s.step(nc.vector.tensor_copy(NMP[:, :, 1, :], NM[:, 1]))
                    s.settle()
                    s.step(nc.vector.tensor_tensor(NMP[:, :, 2, :], NM[:, 1], NMP[:, :, 1, :], ALU.subtract))

                def turn_group(g):
                    dve.wait_ge(p_pv, 8 * t.n + 2 * g + 2)
                    if g == 0:
                        wait(dve, v_ot, HEAD_STEPS * t.n)
                    elif g == 2:
                        dve.wait_ge(v_ot, HEAD_STEPS * t.n + 5)
                    nc.vector.transpose(OQ[:, g % 2, :], PO[:, 0:T]).then_inc(v_ot, 1)

                def normalise(u, pair):
                    s = Steps(dve, v_ot, HEAD_STEPS * u.n + 5 * pair + 2)
                    s.settle()
                    blocks = OQ.rearrange("p i (b d) -> p (i b) d", d=32)
                    s.step(nc.vector.reciprocal(RS[:, :], blocks[:, :, 0]))
                    s.settle()
                    s.step(nc.vector.tensor_tensor(blocks, blocks, RS[:, :].unsqueeze(2).to_broadcast([P, 2 * T // 32, 32]), ALU.mult))
                    s.settle()
                    if pair == 0:
                        wait(dve, p_wo, u.n)
                    s.step(nc.vector.transpose(OT[:, 2 * pair:2 * pair + 2, :].rearrange("p i t -> p (i t)"), OQ.rearrange("p i t -> p (i t)")))

                if lo is not None:
                    normalise(y, 1)
                if lc is not None:
                    dve.wait_ge(p_nm, t.n + 1)
                    if not (first and t.n == 0):
                        dve.wait_ge(s_nml[y.par], 16 * (y.m + 1))
                    nc.vector.tensor_copy(NMT[:, :], nm_bf).then_inc(v_nmt, 1)
                if lo is not None:
                    b = y.batch(lo)
                    dve.wait_ge(p_wo, t.n)
                    xv = Xall[:, bass.ts(b, TT), :]
                    pv = PM[:, :].rearrange("p (a c) -> p a c", a=TT)
                    if lo < 2:
                        nc.vector.tensor_tensor(xv, xv, pv, ALU.add).then_inc(v_res, 1)
                    else:
                        uv = UALL[:, bass.ts(b, TT), :]
                        nc.vector.tensor_tensor(uv, uv, pv, ALU.add).then_inc(v_res, 1)
                        dve.wait_ge(v_res, t.n)
                        nc.vector.tensor_tensor(xv, xv, uv, ALU.add).then_inc(v_base, 1)
                if la is not None:
                    dve.wait_ge(a_split, 2 * q.n + 1)
                    nc.vector.tensor_tensor(QK32, QK32, QKP[0][:, :, :, :], ALU.subtract).then_inc(v_split, 1)

                def scores(hp):
                    if ls is None:
                        return
                    for a in range(TT):
                        k = 2 * hp + a
                        dve.wait_ge(p_s, 16 * t.next().n + k + 1)
                        nc.vector.tensor_reduce(MX[:, a, 2 * hp:2 * hp + 2],
                                                PS[(k + 1) % 2][:, :].rearrange("p (h k) -> p h k", h=2), AX.X, ALU.max).then_inc(v_bank, 1)

                scores(0)
                if lr is not None:
                    k = routed(lr, y.n)
                    b = y.batch(lr)
                    dve.wait_ge(v_res, t.n)
                    src = Xall if lr == 0 else UALL
                    rows = lambda a: src[:, b * TT + a, :]
                    st = norm_begin(rows, v_lnr, nrt(k, lr))
                if lp == 1:
                    dve.wait_ge(s_bc, 64 * (z.n - NB + 1))
                    wait(dve, p_comb, z.n - NB - 1)
                    nc.vector.scalar_tensor_tensor(WCT[z.par].rearrange("p i t -> p (i t)"), BPOS.rearrange("p i t -> p (i t)"),
                                                   cst("slot"), BPRB.rearrange("p i t -> p (i t)"),
                                                   ALU.is_equal, ALU.mult).then_inc(v_wct, 1)
                scores(1)
                if lc is not None:
                    turn_group(0)
                if lr is not None:
                    dve.wait_ge(g_copy, k + 1)
                    powers = powers + 1
                    norm_end(XRS, rows, st, powers, v_xr, 2 if lr == 2 else None)
                scores(2)
                if la is not None:
                    dve.wait_ge(a_split, 2 * q.n + 2)
                    nc.vector.tensor_tensor(QKP[2][:, :, :, :], QK32, QKP[1][:, :, :, :], ALU.subtract).then_inc(v_split, 1)
                scores(3)
                if lc is not None:
                    turn_group(1)
                    normalise(t, 0)
                if lp == 1:
                    dve.wait_ge(p_comb, z.n - NB + 1)
                    xv = Xall[:, bass.ts(z.batch(1), TT), :]
                    nc.vector.tensor_tensor(xv, xv, PM[:, :].rearrange("p (a c) -> p a c", a=TT), ALU.add).then_inc(v_comb, 1)
                    dve.wait_ge(v_comb, z.n - NB + 1)
                scores(4)
                if lp is not None:
                    zb = z.batch(lp)
                    if lp == 0:
                        dve.wait_ge(s_x0 if first and z.n == 0 else s_x, 16 if first and z.n == 0 else 112)
                    if lp == 2:
                        dve.wait_ge(v_res, z.n - NB + 1)
                        if first and z.n == 2 * NB:
                            dve.wait_ge(s_lnp, 16)
                    zrows = lambda a: Xall[:, zb * TT + a, :]
                    st = norm_begin(zrows, v_lnp, nln(lp, z.n))
                scores(5)
                if lc is not None:
                    turn_group(2)
                if lp is not None:
                    wait(dve, p_a, 4 * (z.n - 1) + 1)
                    powers = powers + 1
                    if lp < 2:
                        norm_end(XNS, zrows, st, powers, v_xn, None)
                    else:
                        norm_end(UALL[:, bass.ts(zb, TT), :], zrows, st, powers, None, None)
                        urows = lambda a: UALL[:, zb * TT + a, :]
                        st = norm_begin(urows, v_lnp, nln(lp, z.n) + 6)
                scores(6)
                if lr is not None:
                    dve.wait_ge(p_log, k + 1)
                    nc.vector.tensor_copy(LOG[:, bass.ts(b, TT), :],
                                          PM[:, 0:TT * NE].rearrange("p (a e) -> p a e", a=TT)).then_inc(v_log, 1)
                scores(7)
                if lc is not None:
                    turn_group(3)
                if lp == 2:
                    norm_end(XNS, urows, st, powers + 1, v_xn, 0)
                if la is not None:
                    dve.wait_ge(p_a, 4 * q.n + 4)
                    wait(dve, p_pv, 8 * (q.n - 1))
                    nc.vector.tensor_tensor(
                        VA[q.par][:, :, :, 1:1 + HD], PS[1][:, :].rearrange("p (a h d) -> p a h d", a=TT, h=NH),
                        BV[r][:, :].rearrange("p (h d) -> p h d", h=NH).unsqueeze(1).to_broadcast([P, TT, NH, HD]),
                        ALU.add).then_inc(v_bank, 1)

            attention_rounds_0(dve, body)

            def softmax(s, src, dst, a_sem):
                s.step(nc.vector.tensor_reduce(SM[:, :], LOG[:, :, :], AX.X, ALU.max))
                s.settle()
                s.step(nc.vector.tensor_tensor(dst, src, SM[:, :].unsqueeze(2).to_broadcast([P, NT, NE]), ALU.subtract))
                dve.wait_ge(a_sem, 1)
                s.step(nc.vector.tensor_reduce(SMR[:, :], dst, AX.X, ALU.add))
                s.settle()
                s.step(nc.vector.reciprocal(SM[:, :], SMR[:, :]))
                s.settle()

            dve.wait_ge(v_log, NB)
            s = Steps(dve, v_topk, 0)
            softmax(s, LOG[:, :, :], LOG[:, :, :], a_topk)
            s.step(nc.vector.tensor_tensor(
                PR[:, :, :, :].rearrange("p a b e -> p b a e"), LOG[:, :, :].rearrange("p (b a) e -> p b a e", a=TT),
                SM[:, :].rearrange("p (b a) -> p b a", a=TT).unsqueeze(3).to_broadcast([P, NB, TT, NE]), ALU.mult))
            dve.wait_ge(p_topk, 1)
            s.step(nc.vector.tensor_copy(PTK, PM[0:NB * NE, 0:T]))
            s.settle()
            for i in range(CAP0 // 8):
                cur = PTK if i == 0 else WORK
                s.step(nc.vector.max(TOP8[:, :], cur))
                s.settle()
                s.step(nc.vector.match_replace(WORK, TOP8[:, :], cur, -1.0))
                s.settle()
            s.step(nc.vector.tensor_scalar(CHOSEN, WORK, 0.0, None, ALU.is_lt))
            s.settle()
            s.step(nc.vector.tensor_tensor_scan(POS, CHOSEN, CHOSEN, 0.0, ALU.add, ALU.max))
            s.settle()
            s.step(nc.vector.tensor_tensor(POS, POS, CHOSEN, ALU.mult))
            s.settle()
            s.step(nc.vector.tensor_scalar(POS, POS, -1.0, None, ALU.add))
            assert s.k == TOPK_STEPS
            dve.wait_ge(p_topk, 2)
            s.step(nc.vector.tensor_copy(POST[:, :, :], PM[:, 0:TT * NB * NE].rearrange("p (a r) -> p a r", a=TT)))
            s.settle()
            with dve.Fori(0, NB // 2) as m:
                for par in range(2):
                    b = 2 * m + par
                    dve.wait_ge(p_disp, 2 * b)
                    for a in range(TT):
                        nc.vector.tensor_tensor(
                            GSEL[par][:, a], cst("iota").unsqueeze(1).to_broadcast([P, NE, CAP0]),
                            POST[:, a, bass.ts(b, NE)].unsqueeze(2).to_broadcast([P, NE, CAP0]),
                            ALU.is_equal).then_inc(v_gsel, 1)
                    dve.wait_ge(p_disp, 2 * b + 2)
                    nc.vector.tensor_copy(xint[:, 1, :].rearrange("p (e b s) -> p e b s", e=NE, b=NB)[:, :, b, :],
                                          PTT[par][:, 1, :].rearrange("p (e s) -> p e s", e=NE)).then_inc(v_xi, 1)

            def expert_out(layer):
                def go(m, par, last):
                    e = 2 * m + par
                    for st in range(ST):
                        bk = (PS[0], PS[1], PO, PM)[st]
                        dve.wait_ge(p_y, ST * e + st + 1)
                        if layer == 0:
                            for h in range(2):
                                ins = nc.vector.tensor_copy(yall[64 * par:64 * par + 64, (2 * st + h) * (NE // 2) + m, :],
                                                            bk[64 * h:64 * h + 64, 0:C])
                        else:
                            if st == 0:
                                wait(dve, s_yst[par], 16 * (m - NE // 2)) if not (isinstance(m, int) and m == NE // 2) else None
                                dve.wait_ge(s_b12[par], 32 * (m - NE // 2 + 1))
                            ins = nc.vector.tensor_tensor(YS[par][:, st, :], bk[:, 0:C], B2B[par], ALU.add)
                        ins.then_inc(v_y, 1)
                return go

            dve.wait_ge(s_rows, 32)
            expert_rounds(dve, lambda: None, expert_out(0), 0)
            for r in range(2):
                nc.vector.memset(KS[r][KSTK:KSTK + 32, :, :], 1.0)
            attention_rounds_12(dve, body)

            dve.wait_ge(v_log, 2 * NB)
            dve.wait_ge(p_wo, 3 * NB)
            s = Steps(dve, v_rt, 0)
            softmax(s, LOG[:, :, :], PRR, a_rt)
            s.step(nc.vector.tensor_tensor(PRR, PRR, SM[:, :].unsqueeze(2).to_broadcast([P, NT, NE]), ALU.mult))
            s.settle()
            by_expert = lambda v: v.unsqueeze(2).to_broadcast([P, NT, NE])
            for k, src in ((0, PRR), (1, TMP[:, 0])):
                if k:
                    s.step(nc.vector.scalar_tensor_tensor(TMP[:, 0], PICK[:, 0], -BIG, LOG[:, :, :], ALU.mult, ALU.add))
                    s.settle()
                s.step(nc.vector.tensor_reduce(SM[:, :], src, AX.X, ALU.max))
                s.settle()
                s.step(nc.vector.tensor_tensor(EQ, src, by_expert(SM[:, :]), ALU.is_equal))
                s.settle()
                s.step(nc.vector.tensor_tensor(EQ, EQ, cst("rev").unsqueeze(1).to_broadcast([P, NT, NE]), ALU.mult))
                s.settle()
                s.step(nc.vector.tensor_reduce(SMR[:, :], EQ, AX.X, ALU.max))
                s.settle()
                s.step(nc.vector.tensor_tensor(PICK[:, k], EQ, by_expert(SMR[:, :]), ALU.is_equal))
                s.settle()
            assert s.k == PICK_STEPS, s.k
            dve.wait_ge(p_rte, 2)
            s.step(nc.vector.tensor_copy(TOT, PS[1][:, 0:2 * NE * NT].rearrange("p (k i e) -> p k e i", k=2, i=NT)))
            s.settle()
            flat = lambda v: v.rearrange("p k e i -> p (k e i)")
            s.step(nc.vector.tensor_tensor_scan(flat(SCN), cst("keep"), flat(TOT), 0.0, ALU.mult, ALU.add))
            s.settle()
            s.step(nc.vector.tensor_tensor(EXC, SCN, TOT, ALU.subtract))
            s.settle()
            s.step(nc.vector.tensor_tensor(LOC, PS[0][:, 0:2 * NE * NT].rearrange("p (k i e) -> p k i e", k=2, i=NT),
                                           EXC.rearrange("p k e i -> p k i e"), ALU.add))
            s.settle()
            s.step(nc.vector.tensor_tensor(LOC[:, 1], LOC[:, 1], SCN[:, 0, :, NT - 1].unsqueeze(1).to_broadcast([P, NT, NE]), ALU.add))
            s.settle()

            def picked(dst, value):
                s.step(nc.vector.tensor_tensor(TMP, PICK, value, ALU.mult))
                s.settle()
                s.step(nc.vector.tensor_reduce(dst, TMP, AX.X, ALU.add))
                s.settle()

            picked(LS[:, :, :], LOC)
            picked(ES[:, :, :], cst("base").unsqueeze(1).unsqueeze(1).to_broadcast([P, 2, NT, NE]))
            picked(G12[:, :, :], PRR.unsqueeze(1).to_broadcast([P, 2, NT, NE]))
            s.step(nc.vector.tensor_scalar(FIT[:, :, :], LS[:, :, :], float(SLOT), None, ALU.is_le))
            s.settle()
            s.step(nc.vector.scalar_tensor_tensor(IDXF[:, :, :], FIT[:, :, :], -65536.0, ES[:, :, :], ALU.mult, ALU.add))
            s.settle()
            s.step(nc.vector.tensor_tensor(IDXF[:, :, :], IDXF[:, :, :], LS[:, :, :], ALU.add))
            s.settle()
            s.step(nc.vector.tensor_scalar(IDX[0][:, :, :], IDXF[:, :, :], 65535.0, None, ALU.add))
            s.settle()
            assert s.k == ROUTE_STEPS, s.k
            s.step(nc.vector.scalar_tensor_tensor(IDXF[:, :, :], LS[:, :, :], float(SLOT), ES[:, :, :], ALU.min, ALU.add))
            s.settle()
            s.step(nc.vector.tensor_scalar(IDX[1][:, :, :], IDXF[:, :, :], -1.0, None, ALU.add))
            s.step(nc.vector.tensor_tensor(G12[:, :, :], G12[:, :, :], FIT[:, :, :], ALU.mult))
            s.settle()
            s.step(nc.vector.tensor_tensor(SM[:, :], G12[:, 0, :], G12[:, 1, :], ALU.add))
            s.settle()
            s.step(nc.vector.tensor_scalar(SM[:, :], SM[:, :], 2.0 ** -23, None, ALU.max))
            s.settle()
            s.step(nc.vector.reciprocal(SMR[:, :], SM[:, :]))
            s.settle()
            s.step(nc.vector.scalar_tensor_tensor(G12[:, :, :], G12[:, :, :], 0.8, SMR[:, :].unsqueeze(1).to_broadcast([P, 2, NT]), ALU.mult, ALU.mult))
            s.settle()
            expert_rounds(dve, lambda: None, expert_out(1), 1)

            for g in range(4):
                dve.wait_ge(s_got[g], 16 * 8)
                for k in range(2):
                    for i in range(4 * g, 4 * g + 4):
                        ins = nc.vector.scalar_tensor_tensor(Xall[:, i, :], GOT[k][:, i, :], G12[:, k, i:i + 1], Xall[:, i, :], ALU.mult, ALU.add)
                        if k == 0 and i % 4 == 3:
                            s.step(ins)
                            s.settle()
                ins.then_inc(v_out, 1)

        @block.tensor
        def _(pe):
            mm = nc.tensor.matmul
            pe.wait_ge(s_const, 64)
            pe.wait_ge(v_const, 15)

            def project(q, la, w):
                r = la % 2
                if w == 0:
                    pe.wait_ge(a_bank, 3 * q.n + 1)
                    src = XNT
                elif la < 2:
                    pe.wait_ge(s_ctx[q.par], 16 * (q.m + 1))
                    src = CTX[q.par]
                else:
                    src = XNT
                bk = PS[1 - w]
                for mt in range(CT):
                    for a in range(CT):
                        ins = mm(bk[:, mt * T:(mt + 1) * T], WQKV[r][:, w, a, mt * P:(mt + 1) * P], src[:, a, :],
                                 start=(a == 0), stop=(a == CT - 1))
                ins.then_inc(p_a, 1)

            def values(q, la):
                kv = XNT if la == 2 else CTX[q.par]
                for tk in range(TT):
                    for a in range(CT):
                        ins = mm(PS[1][:, tk * C:(tk + 1) * C], kv[:, a, tk * P:(tk + 1) * P], WQKV[la % 2][:, 2, a, :],
                                 start=(a == 0), stop=(a == CT - 1))
                ins.then_inc(p_a, 1)

            def bias(outv, layer, par, which, tile):
                if which == 0:
                    rhs = (BMK[par][:, 0, tile, :] if layer == 0 else dist[:, tile, :]).unsqueeze(1).to_broadcast([P, 2, T])
                else:
                    rhs = BMK[par][:, 1] if layer == 0 else dist
                if layer == 0:
                    mm(outv, identb, rhs, start=True, stop=True, skip_group_check=True)
                elif layer == 1:
                    for i in range(NPART):
                        mm(outv, TDI[:, i, :], rhs, start=(i == 0), stop=True, skip_group_check=True)

            def scores(q, la, hp, before, projected):
                if hp == 0:
                    pe.wait_ge(s_stk[q.par], 192 * (q.m + 1))
                    if la == 0:
                        pe.wait_ge(g_mask, 2 * q.n + 1)
                for a in range(TT):
                    k = 2 * hp + a
                    bk = PS[(k + 1) % 2]
                    if k < 2 and projected is not None:
                        pe.wait_ge(a_bank, projected + 2 + k)
                    else:
                        pe.wait_ge(v_bank, before + max(k - 1, 0))
                    bias(bk[:, :].rearrange("p (h k) -> p h k", h=2), la, q.par, 0, a)
                    for h in range(2):
                        ins = mm(bk[:, h * T:(h + 1) * T], QS[q.par][0:KSTK, 2 * hp + h, a * P:(a + 1) * P],
                                 KS[q.par][0:KSTK, 2 * hp + h, :], start=(la == 2), stop=True, skip_group_check=True)
                    ins.then_inc(p_s, 1)

            def shifted(t, lc, pr):
                if pr == 0 and lc == 0:
                    pe.wait_ge(g_mask, 2 * (t.n + 1))
                wait(pe, a_exp, 8 * t.n + pr - 1)
                for h in range(2):
                    bk = PTT[pr % 2][:, h, :].rearrange("p (a t) -> p a t", a=TT)
                    bias(bk, lc, t.par, 1, None)
                    for a in range(TT):
                        ins = mm(bk[:, a, :], KS[t.par][0:KSTK + NPART, 2 * pr + h, a * P:(a + 1) * P],
                                 QS[t.par][0:KSTK + NPART, 2 * pr + h, :], start=(lc == 2), stop=True, skip_group_check=True)
                ins.then_inc(p_st, 1)

            def weigh(t, pr):
                pe.wait_ge(a_exp, 8 * t.n + pr + 1)
                if pr % 2 == 0:
                    wait(pe, v_ot, HEAD_STEPS * t.n + (-3, 1, 2, 6)[pr // 2])
                for h in range(2):
                    g = (2 * pr + h) % 4
                    for a in range(TT):
                        ins = mm(PO[32 * g:32 * g + 32, 0:T], VA[t.par][:, a, 2 * pr + h, :], PT[pr % 2][:, h, a, :],
                                 start=(a == 0), stop=(a == TT - 1))
                ins.then_inc(p_pv, 1)

            def body(t, lp, la, ls, lc, lo):
                lr = routes(lo)
                z, q, y = t.next(3), t.next(2), t.next(-1)
                before = t.done(2) + 16 * t.done(1)
                projected = None if la is None else 3 * q.n
                if la is not None:
                    if isinstance(q.n, int) and q.n % NB == 0 and q.n < 2 * NB:
                        pe.wait_ge(s_w[la], 64)
                    pe.wait_ge(v_xn, q.n + 1)
                    wait(pe, v_bank, before)
                    wait(pe, a_bank, projected)
                    alone(pe)
                    for ct in range(CT):
                        for a in range(TT):
                            ins = nc.tensor.transpose(PS[0][:, ct * T + a * P:ct * T + (a + 1) * P], XNS[:, a, ct * P:(ct + 1) * P], ident)
                    ins.then_inc(p_a, 1)
                    project(q, la, 0)
                if lc is not None:
                    pe.wait_ge(v_nm, 6 * (t.n + 1))
                    alone(pe)
                    for a in range(TT):
                        ins = nc.tensor.transpose(nm_bf[:, a * P:(a + 1) * P],
                                                  NMP[:, a, :, :].rearrange("p i h -> p (i h)"), identb)
                    ins.then_inc(p_nm, 1)
                if la is not None:
                    project(q, la, 1)
                if lo is not None:
                    pe.wait_ge(v_ot, HEAD_STEPS * t.n)
                    for a in range(TT):
                        for i in range(4):
                            ins = mm(PM[:, a * C:(a + 1) * C], OT[:, i, a * P:(a + 1) * P], WO[lo % 2][:, i, :],
                                     start=(i == 0), stop=(i == 3))
                    ins.then_inc(p_wo, 1)
                if lc is not None:
                    pe.wait_ge(s_nml[t.par], 16 * (t.m + 1))
                    shifted(t, lc, 0)
                    for pr in range(NH // 2):
                        if pr + 1 < NH // 2:
                            shifted(t, lc, pr + 1)
                        if ls is not None:
                            scores(t.next(), ls, pr, before, projected)
                        weigh(t, pr)
                        if pr == 2 and lp == 1:
                            combine(z, t, lo)
                        if pr == 3 and lr is not None:
                            router_turn(y, lr)
                        if pr == 5 and lr is not None:
                            router_logits(y, lr)
                else:
                    for hp in range(8):
                        if ls is not None:
                            scores(t.next(), ls, hp, before, projected)
                        if hp == 2 and lp == 1:
                            combine(z, t, lo)
                    if lr is not None:
                        router_turn(y, lr)
                        router_logits(y, lr)
                if la is not None:
                    if ls is None:
                        pe.wait_ge(a_bank, projected + 2)
                    else:
                        pe.wait_ge(v_bank, before + 15)
                    values(q, la)
                if lp == 1:
                    pe.wait_ge(v_comb, z.n - NB + 1)
                elif lr is not None:
                    pe.wait_ge(v_log, routed(lr, y.n) + 1)

            def router_turn(z, layer):
                k = routed(layer, z.n)
                pe.wait_ge(v_xr, k + 1)
                pe.wait_ge(v_res, z.n + 1)
                for ct in range(CT):
                    for a in range(TT):
                        ins = nc.tensor.transpose(PM[:, ct * T + a * P:ct * T + (a + 1) * P], XRS[:, a, ct * P:(ct + 1) * P], ident)
                ins.then_inc(p_rt, 1)

            def router_logits(z, layer):
                k = routed(layer, z.n)
                pe.wait_ge(a_xrt, k + 1)
                for a in range(TT):
                    for ct in range(CT):
                        ins = mm(PM[:, a * NE:(a + 1) * NE], XRT[:, ct, a * P:(a + 1) * P], GATE[:, layer // 2, ct, :],
                                 start=(ct == 0), stop=(ct == CT - 1))
                ins.then_inc(p_log, 1)

            def combine(z, t, lo):
                b = z.batch(1)
                if lo is not None:
                    pe.wait_ge(v_res, t.n)
                pe.wait_ge(v_wct, z.n - NB + 1)
                for a in range(TT):
                    for i in range(NE // 2):
                        ins = mm(PM[:, a * C:(a + 1) * C], WCT[z.par][:, i, a * P:(a + 1) * P], yall[:, b * (NE // 2) + i, :],
                                 start=(i == 0), stop=(i == NE // 2 - 1))
                ins.then_inc(p_comb, 1)

            attention_rounds_0(pe, body)
            pe.wait_ge(v_topk, 5)
            for a in range(TT):
                ins = nc.tensor.transpose(PM[0:NB * NE, a * P:(a + 1) * P], PR[:, a].rearrange("p b e -> p (b e)"), ident)
            ins.then_inc(p_topk, 1)
            pe.wait_ge(v_topk, TOPK_STEPS)
            for a in range(TT):
                ins = nc.tensor.transpose(PM[:, a * NB * NE:(a + 1) * NB * NE], POS[:, a * P:(a + 1) * P], ident[0:NB * NE, 0:NB * NE])
            ins.then_inc(p_topk, 1)
            with pe.Fori(0, NB // 2) as m:
                for par in range(2):
                    b = 2 * m + par
                    pe.wait_ge(a_xst, b + 1)
                    pe.wait_ge(v_gsel, TT * (b + 1))
                    for c in range(CT):
                        pe.wait_ge(a_xi if c == 0 else v_xi, b)
                        for a in range(TT):
                            ins = mm(PTT[par][:, c, :], XST[par][:, a, c * P:(c + 1) * P], GSEL[par][:, a].rearrange("p e s -> p (e s)"),
                                     start=(a == 0), stop=(a == TT - 1))
                        ins.then_inc(p_disp, 1)
            pe.wait_ge(a_xi, NB)
            pe.wait_ge(v_xi, NB)

            def turn_inputs(m, par):
                e = 2 * m + par
                pe.wait_ge(s_zs[par], 16 * (m - NE // 2 + 1))
                for c in range(CT):
                    j = (uses(1) * par + c) % 4
                    wait(pe, a_h, use0(1, e) + c - 3)
                    for st in range(ST):
                        ins = nc.tensor.transpose(PTT[j // 2][:, j % 2, st * P:(st + 1) * P], ZS[par][:, st, c * P:(c + 1) * P], ident)
                    ins.then_inc(p_h, 1)

            def hidden(m, par, layer):
                e = 2 * m + par
                pe.wait_ge(s_ew[par], 32 * (m + 1))
                if layer == 1:
                    pe.wait_ge(a_h, use0(1, e) + CT)
                for f in range(FT):
                    k = use0(layer, e) + uses(layer) - FT + f
                    j = (uses(layer) * par + uses(layer) - FT + f) % 4
                    wait(pe, a_h, k - 3)
                    for c in range(CT):
                        rhs = xint[:, c, bass.ts(e, SLOT)] if layer == 0 else ZT[par][:, c, :]
                        ins = mm(PTT[j // 2][:, j % 2, :], W1[par][:, c, f * P:(f + 1) * P], rhs, start=(c == 0), stop=(c == CT - 1))
                    ins.then_inc(p_h, 1)

            def outputs(m, par, layer, st):
                e = 2 * m + par
                if st == 0:
                    pe.wait_ge(a_h, use0(layer, e + 1))
                bk = (PS[0], PS[1], PO, PM)[st]
                wait(pe, v_y, ST * e + st - 3)
                for f in range(FT):
                    ins = mm(bk[:, 0:C], ht[:, par, f, st * P:(st + 1) * P], W2[par][:, f, :], start=(f == 0), stop=(f == FT - 1))
                ins.then_inc(p_y, 1)

            def step(layer):
                def go(m, par, last):
                    q = Turn(m, par)
                    if not last:
                        hidden(q.next().m, q.next().par, layer)
                    for st in range(ST):
                        outputs(m, par, layer, st)
                        if st == 2 and layer == 1 and not last and not (isinstance(m, int) and m > NE // 2 and par == 0):
                            turn_inputs(q.next(2).m, q.next(2).par)
                return go

            expert_rounds(pe, lambda: hidden(0, 0, 0), step(0), 0)
            attention_rounds_12(pe, body)
            pe.wait_ge(v_rt, PICK_STEPS)
            picks = PICK.rearrange("p k i e -> p (k i e)")
            mm(PS[0][:, 0:2 * NT * NE], tri, picks, start=True, stop=True).then_inc(p_rte, 1)
            mm(PS[1][:, 0:2 * NT * NE], ONES[:, :], picks, start=True, stop=True).then_inc(p_rte, 1)

            def first():
                turn_inputs(NE // 2, 0)
                hidden(NE // 2, 0, 1)
                turn_inputs(NE // 2, 1)
            expert_rounds(pe, first, step(1), 1)


def layout(inputs):
    import numpy as np

    a = {k: np.asarray(v) for k, v in inputs.items()}
    f32 = np.float32

    def heads(w):
        return w.reshape(*w.shape[:-1], NH // 2, CT, HD).swapaxes(-3, -2).swapaxes(-2, -1).reshape(w.shape)

    w3, wo, bqk, bv = [], [], [], []
    for wq, wk, wv, w_o, bq, bk, b_v, bo in (
        [a[f"L0_xattn_{n}"] for n in ("Wq", "Wk", "Wv", "Wo", "bq", "bk", "bv", "bo")],
        [a[f"L1_xattn_{n}"].T for n in ("wq", "wk", "wv", "wo", "bq", "bk", "bv", "bo")],
        [a[f"L1_ffn_{n}"] for n in ("wq", "wk", "wv", "wo", "bq", "bk", "bv", "bo")],
    ):
        w3.append(np.stack([heads(wq), heads(wk), wv]))
        rows = np.zeros((4, 4, 32, C), f32)
        rows[:, :, 1:1 + HD] = w_o.reshape(4, 4, HD, C)
        rows[0, 0, 0] = bo
        wo.append(rows.reshape(4, P, C).swapaxes(0, 1))
        bqk.append(np.stack([heads(bq).reshape(CT, P), heads(bk).reshape(CT, P)]).transpose(2, 0, 1))
        bv.append(b_v)

    cf = np.zeros((P, NCF), f32)
    p = np.arange(P)

    def put(name, value):
        cf[:, CF[name][0]:CF[name][1]] = value

    put("ident", np.eye(P))
    put("tri", p[:, None] <= p[None, :])
    put("iota", np.arange(CAP0)[None, :])
    put("slot", (p % CAP0)[:, None])
    put("rev", NE - np.arange(NE)[None, :])
    put("base", SLOT * np.arange(NE)[None, :])
    put("keep", (np.arange(2 * NE * NT) % NT != 0)[None, :])
    k = np.arange(T)
    dist = np.abs((k[:, None] - k[None, :]).reshape(TT, P, T)).transpose(1, 0, 2).reshape(P, TT * T)
    cb = (np.concatenate([np.eye(P), dist], 1).astype(f32).view(np.uint32) >> 16).astype(np.uint16)
    mask = a["mask_Bx1xSxS2_bf1"].reshape(NB, T, T)
    mask = np.stack([mask, mask.swapaxes(1, 2)], 1).view(np.uint8)
    c = np.ascontiguousarray
    return {
        "x": c(a["x"]), "ctxT": c(a["ctx_1024"].swapaxes(1, 2)), "maskp": c(mask), "cf": cf, "cb": cb,
        "wqkv": c(np.stack(w3)), "wo": c(np.stack(wo)), "bqk": c(np.stack(bqk)), "bv": c(np.stack(bv)),
        "gates": c(np.stack([a["L0_ffn_gate_w"], a["L1_ffn_wr"]])), "td": c(a["L1_xattn_time_decay"].reshape(1)),
        "lnp": c(np.stack([a[f"L1_ffn_ln{i}_{n}"] for i in (1, 2) for n in "gb"])),
        "w1": c(np.stack([a["L0_ffn_w1"], a["L1_ffn_w1"]])), "b1": c(a["L1_ffn_b1"].reshape(NE, FT, P).swapaxes(1, 2)),
        "w2": c(np.stack([a["L0_ffn_w2"], a["L1_ffn_w2"]])), "b2": c(a["L1_ffn_b2"]),
    }


def kernel(**inputs):
    import concourse.bacc as bacc
    from concourse.bass_utils import run_bass_kernel_spmd

    arrays = layout(inputs)
    nc = bacc.Bacc("TRN2", target_bir_lowering=False, num_devices=1)
    args = [nc.dram_tensor(f"in_{n}", v.shape, mybir.dt.from_np(v.dtype), kind="ExternalInput").ap() for n, v in arrays.items()]
    args.append(nc.dram_tensor("out_0", (NB, T, C), F32, kind="ExternalOutput").ap())
    bass_two_layer_cross_attention_moe(nc, *args)
    got = run_bass_kernel_spmd(nc, [{f"in_{n}": v for n, v in arrays.items()}], core_ids=[0])
    return got.results[0]["out_0"]
```

```python
import concourse.bass as bass
from concourse import mybir
from contextlib import ExitStack

F32 = mybir.dt.float32
BF16 = mybir.dt.bfloat16
U8 = mybir.dt.uint8
U32 = mybir.dt.uint32
ALU = mybir.AluOpType
ACT = mybir.ActivationFunctionType
AX = mybir.AxisListType

P = 128
NB = 8
T = 256
C = 256
TT = T // P
CT = C // P
NH = 16
HD = C // NH
NE = 8
FF = 1024
FT = FF // P
CAP0 = 64
SLOT = 512
ST = SLOT // P
NT = NB * TT
TERMS = 6
KSTK = TERMS * HD
NPART = 3
KDEC = 2 * NPART
PAIRS = NH // 8
TOPK_STEPS = 6 + 2 * (CAP0 // 8) + 4
PICK_STEPS = 5 + 5 + 6
DECAY_STEPS = 4 + 6 + NPART + 2
DST_STEPS = 4
HEAD_STEPS = 2 * (2 + 3)
FIRST_STEPS = PICK_STEPS + 4 + 4 + 6
ROUTE_STEPS = FIRST_STEPS + 1 + 6
BIG = 2.0 ** 100
HUGE = 2.0 ** 120
EPS = 1e-5

Q_TERM = [0, 0, 1, 0, 2, 1]
K_TERM = [0, 1, 0, 2, 0, 1]

CF = {}
_at = 0
for _name, _w in (("ident", P), ("tri", P), ("iota", CAP0), ("slot", 1), ("rev", NE), ("base", NE), ("part", NPART), ("token", NT), ("place", ST),
                  ("keep", 2 * NE * NT)):
    CF[_name] = (_at, _at + _w)
    _at += _w
NCF = _at


def wait(eng, sem, value):
    if isinstance(value, int) and value <= 0:
        return
    eng.wait_ge(sem, value)


def alone(eng):
    eng.nop(nofuse=True)


class Steps:

    def __init__(self, eng, sem, base):
        self.eng, self.sem, self.base, self.k = eng, sem, base, 0

    def step(self, ins, by=1):
        ins.then_inc(self.sem, by)
        self.k += by

    def settle(self):
        self.eng.wait_ge(self.sem, self.base + self.k)


class Turn:

    def __init__(self, m, par, phase=0):
        self.m, self.par, self.phase = m, par, phase
        self.n = 2 * m + par

    def next(self, k=1):
        q = self.par + k
        return Turn(self.m + q // 2, q % 2, self.phase)

    def batch(self, layer):
        return self.n - NB * layer

    def done(self, ahead):
        k = self.n + ahead
        if isinstance(k, int):
            k = min(max(k, NB * self.phase), NB if self.phase == 0 else 3 * NB)
        return k


def attention_rounds_0(eng, body):
    body(Turn(-2, 1), 0, None, None, None, None)
    body(Turn(-1, 0), 0, 0, None, None, None)
    body(Turn(-1, 1), 0, 0, 0, None, None)
    body(Turn(0, 0), 0, 0, 0, 0, None)
    with eng.Fori(0, 2) as m:
        body(Turn(m, 1), 0, 0, 0, 0, 0)
        body(Turn(m + 1, 0), 0, 0, 0, 0, 0)
    body(Turn(2, 1), None, 0, 0, 0, 0)
    body(Turn(3, 0), None, None, 0, 0, 0)
    body(Turn(3, 1), None, None, None, 0, 0)
    body(Turn(4, 0), None, None, None, None, 0)


def attention_rounds_12(eng, body):
    body(Turn(2, 1, 1), 1, None, None, None, None)
    body(Turn(3, 0, 1), 1, 1, None, None, None)
    body(Turn(3, 1, 1), 1, 1, 1, None, None)
    body(Turn(4, 0, 1), 1, 1, 1, 1, None)
    with eng.Fori(4, 6) as m:
        body(Turn(m, 1, 1), 1, 1, 1, 1, 1)
        body(Turn(m + 1, 0, 1), 1, 1, 1, 1, 1)
    body(Turn(6, 1, 1), 2, 1, 1, 1, 1)
    body(Turn(7, 0, 1), 2, 2, 1, 1, 1)
    body(Turn(7, 1, 1), 2, 2, 2, 1, 1)
    body(Turn(8, 0, 1), 2, 2, 2, 2, 1)
    with eng.Fori(8, 10) as m:
        body(Turn(m, 1, 1), 2, 2, 2, 2, 2)
        body(Turn(m + 1, 0, 1), 2, 2, 2, 2, 2)
    body(Turn(10, 1, 1), None, 2, 2, 2, 2)
    body(Turn(11, 0, 1), None, None, 2, 2, 2)
    body(Turn(11, 1, 1), None, None, None, 2, 2)
    body(Turn(12, 0, 1), None, None, None, None, 2)


def routed(layer, n):
    return n if layer == 0 else n - NB


def gather_rounds(eng, body):
    body(0, 0)
    body(0, 1)
    with eng.Fori(1, NB // 2 - 1) as m:
        body(m, 0)
        body(m, 1)
    body(NB // 2 - 1, 0)
    body(NB // 2 - 1, 1)


def projections(la):
    return (0, 1) if la == 2 else (1, 0)


def routes(lo):
    return None if lo == 1 else lo


def bass_two_layer_cross_attention_moe(
    nc, x, ctxT, maskp, cf, cb, cd, wqkv, wo, bo, bqk, bv, gates, td, lnp, w1, b1, w2, b2, out,
):
    posd = nc.dram_tensor("slot_of_token", [NB * NE, T], F32, kind="Internal").ap()
    prbd = nc.dram_tensor("prob_of_token", [NB * NE, T], F32, kind="Internal").ap()
    zbuf = nc.dram_tensor("expert_inputs", [NE * SLOT, C + 1], F32, kind="Internal").ap()
    decay_rows = nc.dram_tensor("decay_rows", [KDEC, 2, T], BF16, kind="Internal").ap()
    gbuf = nc.dram_tensor("outputs_by_token", [2 * NB * T, C], F32, kind="Internal").ap()

    with ExitStack() as ctx:
        def sb(name, shape, dt=F32):
            return ctx.enter_context(nc.sbuf_tensor(name, shape, dt))

        def sem(name):
            return ctx.enter_context(nc.semaphore(name))

        Xall = sb("Xall", [P, NT, C])
        XNall = sb("XNall", [P, NT, C + 1])
        XINT = sb("XINT", [P, CT * NE * SLOT])
        YALL = sb("YALL", [P, NB * (NE // 2) * C])
        STK = sb("STK", [P, 2 * 2 * NH * T], BF16)
        WREG = sb("WREG", [P, 2 * (CT * FF + FT * C)])

        xint = XINT[:, :].rearrange("p (c s) -> p c s", c=CT)
        yall = YALL[:, :].rearrange("p (i c) -> p i c", c=C)
        stk = STK[:, :].rearrange("p (r w h t) -> p r w h t", r=2, w=2, h=NH)
        QS = [stk[:, r, 0] for r in range(2)]
        KS = [stk[:, r, 1] for r in range(2)]
        ht = STK[:, :].bitcast(F32).rearrange("p (r f s) -> p r f s", r=2, f=FT)
        W1 = [WREG[:, r * CT * FF:(r + 1) * CT * FF].rearrange("p (c f) -> p c f", c=CT) for r in range(2)]
        o = 2 * CT * FF
        W2 = [WREG[:, o + r * FT * C:o + (r + 1) * FT * C].rearrange("p (f c) -> p f c", f=FT) for r in range(2)]

        def carve(region, start, *shape, dt=F32):
            size = 1
            for s in shape:
                size *= s
            v = region[:, start:start + (size if dt == F32 else size // (2 if dt == BF16 else 4))]
            if dt != F32:
                v = v.bitcast(dt)
            names = "abcdef"[:len(shape)]
            if len(shape) > 1:
                kw = {names[i]: shape[i] for i in range(1, len(shape))}
                v = v.rearrange(f"p ({' '.join(names)}) -> p {' '.join(names)}", **kw)
            return v

        CTX = [carve(WREG, 512 * r, CT, T) for r in range(2)]
        BPOS = carve(WREG, 1024, NE // 2, T)
        BPRB = carve(WREG, 2048, NE // 2, T)
        WCT = [carve(WREG, 3072 + 1024 * r, NE // 2, T) for r in range(2)]
        CD = carve(WREG, 3072, 2, 2, T, dt=BF16)
        DROW = carve(WREG, 3584, 2, T, dt=BF16)
        XNT = carve(WREG, 5120, CT, T)
        QK32 = carve(WREG, 5632, 2, TT, T)
        XNS = carve(WREG, 6656, TT, C)
        XRS = carve(WREG, 7168, TT, C)
        OQ = carve(WREG, 7680, 2, T)
        MASKU = [carve(YALL, 256 * r, 2, TT, T, dt=U8) for r in range(2)]
        BMK = [carve(YALL, 512 + 512 * r, 2, TT, T, dt=BF16) for r in range(2)]
        GSEL = [carve(YALL, 2048 * (1 + r), TT, NE, CAP0) for r in range(2)]
        XST = [carve(YALL, 6144 + 512 * r, TT, C) for r in range(2)]
        LNP = carve(YALL, 0, 4, C)
        UALL = carve(XINT, 0, NT, C)
        PT = [carve(XINT, 4096 + 1024 * r, 2, TT, T) for r in range(2)]
        OT = carve(XINT, 6144, PAIRS, T)
        OC = carve(XINT, 6656, T // 32, 2, HD)
        DECAY = carve(XINT, 7680, TT, T)
        XRT = carve(XINT, 7168, CT, T)

        PTK = carve(YALL, 7168, T)[0:NB * NE]
        WORK = carve(YALL, 7424, T)[0:NB * NE]
        CHOSEN = carve(YALL, 7680, T)[0:NB * NE]
        POS = carve(YALL, 7936, T)[0:NB * NE]
        ZS = [carve(YALL, 1536 * r, ST, C + 1) for r in range(2)]
        ZT = [carve(YALL, 3072 + 1024 * r, CT, SLOT) for r in range(2)]
        YS = [carve(YALL, 5120 + 1024 * r, ST, C) for r in range(2)]
        B2B = [carve(YALL, 7168 + 256 * r, C) for r in range(2)]
        B1S = [carve(YALL, 7680 + FT * r, FT) for r in range(2)]
        PRR = carve(XINT, 4096, NT, NE)
        EQ = carve(XINT, 4224, NT, NE)
        PICK = carve(XINT, 4352, 2, NT, NE)
        TOT = carve(XINT, 4608, 2, NE, NT)
        SCN = carve(XINT, 4864, 2, NE, NT)
        EXC = carve(XINT, 5120, 2, NE, NT)
        LOC = carve(XINT, 5376, 2, NT, NE)
        TMP = carve(XINT, 5632, 2, NT, NE)
        GOT = [carve(XINT, 4096 * w, NT, C) for w in range(2)]

        WQKV = [sb(f"WQKV{r}", [P, 3, CT, C]) for r in range(2)]
        WO = [sb(f"WO{r}", [P, PAIRS, C]) for r in range(2)]
        BO = [sb(f"BO{r}", [P, C]) for r in range(2)]
        BQK = [sb(f"BQK{r}", [P, 2, CT]) for r in range(2)]
        BQ4 = [sb(f"BQ4{r}", [P, CT]) for r in range(2)]
        BV = [sb(f"BV{r}", [P, C]) for r in range(2)]
        GATE = sb("GATE", [P, 2, CT, NE])
        TD = sb("TD", [P, 1])
        cfs = sb("cfs", [P, NCF])
        cbs = sb("cbs", [P, P + TT * T + TT * P], BF16)
        TDI = sb("TDI", [P, NPART, P], BF16)
        TDP = sb("TDP", [P, NPART + 2])
        TDB = sb("TDB", [P, NPART], BF16)
        ONES = sb("ONES", [P, P])
        POWH = sb("POWH", [P, TT])

        def cst(name):
            return cfs[:, CF[name][0]:CF[name][1]]

        ident, tri = cst("ident"), cst("tri")
        identb = cbs[:, 0:P]
        dist = cbs[:, P:P + TT * T].rearrange("p (a t) -> p a t", a=TT)
        corr = cbs[:, P + TT * T:].rearrange("p (a t) -> p a t", a=TT)

        QKP = [sb(f"QKP{i}", [P, 2, CT, T], BF16) for i in range(NPART)]
        VA = [sb(f"VA{r}", [P, TT, NH, 32]) for r in range(2)]
        RS = sb("RS", [P, 2, T // 32])
        JUNK = sb("JUNK", [P, TT, 2, T], BF16)
        PSEL = sb("PSEL", [KDEC, 1])
        TDP6 = sb("TDP6", [KDEC, NPART])
        MX = sb("MX", [P, TT, NH])
        NM = sb("NM", [P, 2, TT, NH])
        NMP = sb("NMP", [P, TT, NPART, NH], BF16)
        NMT = sb("NMT", [NPART * NH, T], BF16)
        STATS = sb("STATS", [P, TT, 6])
        MV = sb("MV", [P, TT, 2])
        VE = sb("VE", [P, TT])
        RSTD = sb("RSTD", [P, TT])
        LOG = sb("LOG", [P, NT, NE])
        PR = sb("PR", [P, TT, NB, NE])
        SM = sb("SM", [P, NT])
        SMR = sb("SMR", [P, NT])
        TOP8 = sb("TOP8", [NB * NE, 8])
        ZERO = sb("ZERO", [P, C + 1])
        LS = sb("LS", [P, 2, NT])
        ES = sb("ES", [P, 2, NT])
        FIT = sb("FIT", [P, 2, NT])
        G12 = sb("G12", [P, 2, NT])
        IDXF = sb("IDXF", [P, 2, NT])
        IDX = sb("IDX", [P, 2, NT], U32)
        FIRSTS = sb("FIRSTS", [P, NE])
        DST = sb("DST", [P, 2, ST])
        DSTI = [sb(f"DSTI{r}", [P, ST], U32) for r in range(2)]
        POST = sb("POST", [P, TT, NB * NE])

        PS = [ctx.enter_context(nc.psum_tensor(f"PS{i}", [P, 512], F32)) for i in range(2)]
        PTT = [ctx.enter_context(nc.psum_tensor(f"PTT{i}", [P, 2, 512], F32)) for i in range(2)]
        PO = ctx.enter_context(nc.psum_tensor("PO", [P, 512], F32))
        PM = ctx.enter_context(nc.psum_tensor("PM", [P, 512], F32))
        nm_bf = PO[:, :].bitcast(BF16)[0:NPART * NH, 2 * T:3 * T]

        s_const = sem("const_loaded")
        s_x0 = sem("x_first_loaded")
        s_x1 = sem("x_second_loaded")
        s_gate = sem("gates_loaded")
        s_x = sem("x_loaded")
        s_w = [sem(f"attn_weights_loaded{i}") for i in range(3)]
        s_ctx = [sem(f"ctx_loaded{r}") for r in range(2)]
        s_msk = [sem(f"mask_loaded{r}") for r in range(2)]
        s_stk = [sem(f"stack_loaded{r}") for r in range(2)]
        s_nml = [sem(f"negmax_loaded{r}") for r in range(2)]
        s_bc = sem("slot_rows_loaded")
        s_rows = sem("slot_rows_stored")
        g_const = sem("pool_constants")
        g_mask = sem("mask_converted")
        g_rstd = sem("rstd_ready")
        g_copy = sem("router_input_kept")
        v_const = sem("dve_constants")
        v_q4 = sem("query_bias_quartered")
        v_bank = sem("score_bank_read_dve")
        a_bank = sem("score_bank_read_act")
        g_split = sem("parts_subtracted")
        g_aff = sem("scaled")
        g_xn = sem("attn_input_scaled")
        g_xr = sem("router_input_scaled")
        g_bo = sem("output_bias_added")
        g_base = sem("output_base_ready")
        v_decay = sem("decay_rows_ready")
        s_dec = sem("decay_rows_stored")
        s_drow = sem("decay_rows_loaded")
        s_ones = sem("ones_rows_loaded")
        v_nm = sem("negmax_step")
        v_nmt = sem("negmax_rows_ready")
        v_lnp = sem("prep_norm_step")
        v_lnr = sem("router_norm_step")
        v_xn = sem("attn_input_ready")
        v_xr = sem("router_input_ready")
        a_xrt = sem("router_input_transposed")
        v_log = sem("logits_read")
        v_ot = sem("heads_step")
        v_wct = sem("combine_weights_ready")
        v_comb = sem("combined")
        v_res = sem("residual_added")
        a_split = sem("parts_rounded")
        a_exp = sem("probs_ready")
        p_a = sem("projection_written")
        p_s = sem("scores_written")
        p_nm = sem("negmax_transposed")
        p_st = sem("shifted_scores_ready")
        p_pv = sem("head_group_done")
        p_wo = sem("attn_out_ready")
        p_rt = sem("router_input_turned")
        p_log = sem("logits_ready")
        p_comb = sem("combine_ready")
        v_topk = sem("topk_step")
        a_topk = sem("router_exp_ready")
        p_topk = sem("topk_turned")
        v_gsel = sem("gather_matrix_ready")
        a_xst = sem("token_rows_staged")
        p_disp = sem("expert_inputs_ready")
        v_xi = sem("expert_inputs_read_dve")
        a_xi = sem("expert_inputs_read_act")
        s_w1 = [sem(f"expert_w1_loaded{r}") for r in range(2)]
        s_w2 = [sem(f"expert_w2_loaded{r}") for r in range(2)]
        s_zs = [sem(f"slot_rows_in{r}") for r in range(2)]
        s_b12 = [sem(f"expert_biases_loaded{r}") for r in range(2)]
        p_h = sem("hidden_bank_written")
        a_h = sem("hidden_bank_read")
        p_y = sem("expert_output_written")
        v_y = sem("expert_output_read")
        s_lnp = sem("norm_params_loaded")
        s_zero = sem("expert_inputs_cleared")
        v_rt = sem("routing_step")
        a_rt = sem("routing_exp_ready")
        p_rte = sem("choices_counted")
        s_scat = sem("tokens_scattered")
        s_gzero = sem("outputs_by_token_cleared")
        v_dst = sem("destination_step")
        s_ysc = [sem(f"expert_output_scattered{r}") for r in range(2)]
        s_got = [sem(f"outputs_loaded{g}") for g in range(4)]
        v_out = sem("output_rows_ready")
        s_out = sem("output_stored")

        block = ctx.enter_context(nc.Block())

        def nln(layer, n):
            return 5 * n if layer < 2 else 11 * n - (11 - 5) * 2 * NB

        def expert_rounds(eng, first, step, layer):
            base = NE // 2 * layer
            first()
            step(base, 0, False)
            step(base, 1, False)
            with eng.Fori(base + 1, base + NE // 2 - 1) as m:
                step(m, 0, False)
                step(m, 1, False)
            step(base + NE // 2 - 1, 0, False)
            step(base + NE // 2 - 1, 1, True)

        def uses(layer):
            return FT if layer == 0 else FT + CT

        def use0(layer, e):
            return FT * e if layer == 0 else (FT + CT) * e - CT * NE

        @block.sync
        def _(sp):
            def held(sem, value):
                wait(sp, sem, value)
                alone(sp)

            sp.dma_start(Xall[:, 0:TT, :], x[0].rearrange("(a p) c -> p a c", p=P)).then_inc(s_x0, 16)
            sp.dma_start(cfs[:, :], cf).then_inc(s_const, 16)
            sp.dma_start(cbs[:, :], cb.bitcast(BF16)).then_inc(s_const, 16)
            sp.dma_start(TD[:, :], td.partition_broadcast(P)).then_inc(s_const, 16)
            sp.dma_start(CD[0:KDEC], cd.bitcast(BF16)).then_inc(s_const, 16)

            def load_attn(layer):
                r = layer % 2
                sp.dma_start(WQKV[r][:, :, :, :], wqkv[layer].rearrange("w (a p) c -> p w a c", p=P)).then_inc(s_w[layer], 16)
                sp.dma_start(BQK[r][:, :, :], bqk[layer]).then_inc(s_w[layer], 16)
                sp.dma_start(BV[r][:, :], bv[layer].partition_broadcast(P)).then_inc(s_w[layer], 16)
                sp.dma_start(WO[r][:, :, :], wo[layer]).then_inc(s_w[layer], 16)
                sp.dma_start(BO[r][:, :], bo[layer].partition_broadcast(P)).then_inc(s_w[layer], 16)

            def load_ones():
                for r in range(2):
                    sp.dma_start(KS[r][KSTK:KSTK + NPART, :, :],
                                 cd.bitcast(BF16)[0:NPART, 0, 1].unsqueeze(1).to_broadcast([NPART, NH, T])).then_inc(s_ones, 16)

            def load_slot_rows(b):
                for dst, src in ((BPOS, posd), (BPRB, prbd)):
                    v = src.rearrange("(b i h) t -> b h i t", b=NB, h=2)
                    for half in range(2):
                        sp.dma_start(dst[half * 64:half * 64 + 64, :, :], v[b, half].partition_broadcast(64)).then_inc(s_bc, 16)

            def body(t, lp, la, ls, lc, lo):
                z, q = t.next(3), t.next(2)
                if lc is not None:
                    held(v_nmt, t.n + 1)
                    sp.dma_start(QS[t.par][KSTK:KSTK + NPART, :, :], NMT[:, :]).then_inc(s_nml[t.par], 16)
                if lp is not None and lp < 2:
                    held(p_a, 4 * (z.n - 1))
                    sp.dma_start(CTX[z.par], ctxT[z.batch(lp)].rearrange("(a p) t -> p a t", p=P)).then_inc(s_ctx[z.par], 16)
                if lp == 0:
                    held(g_mask, 2 * (z.n - 1))
                    sp.dma_start(MASKU[z.par], maskp[z.batch(0)].rearrange("w (a p) k -> p w a k", p=P)).then_inc(s_msk[z.par], 16)
                if lp == 1 and not (isinstance(z.n, int) and z.n == NB):
                    held(v_wct, z.n - NB)
                    load_slot_rows(z.batch(1))
                if lp == 1 and isinstance(z.n, int) and z.n == NB + 1:
                    held(p_comb, 1)
                    sp.dma_start(LNP, lnp.partition_broadcast(P)).then_inc(s_lnp, 16)
                if la is not None:
                    held(g_split, 2 * (q.n + 1))
                    held(a_split, 2 * (q.n + 1))
                    held(p_st, 8 * (q.n - 1))
                    for j in range(TERMS):
                        for dst, w, term in ((QS, 0, Q_TERM), (KS, 1, K_TERM)):
                            sp.dma_start(dst[q.par][j * HD:(j + 1) * HD, :, :], QKP[term[j]][:, w, :, :]).then_inc(s_stk[q.par], 16)

            def load_later():
                sp.dma_start(GATE[:, :, :, :], gates.rearrange("l (a p) e -> p l a e", p=P)).then_inc(s_gate, 16)

            def body_0(t, *layers):
                body(t, *layers)
                if isinstance(t.n, int) and t.n == -3:
                    load_attn(0)
                    sp.dma_start(Xall[:, TT:2 * TT, :], x[1].rearrange("(a p) c -> p a c", p=P)).then_inc(s_x1, 16)
                    load_ones()
                    for i in range(2, NB):
                        sp.dma_start(Xall[:, TT * i:TT * i + TT, :], x[i].rearrange("(a p) c -> p a c", p=P)).then_inc(s_x, 16)
                if isinstance(t.n, int) and t.n == -2:
                    load_later()
                if isinstance(t.n, int) and t.n == -1:
                    load_attn(1)
                    held(v_decay, 1)
                    sp.dma_start(decay_rows, DROW[0:KDEC]).then_inc(s_dec, 16)

            attention_rounds_0(sp, body_0)
            held(p_wo, NB)
            held(g_bo, NB)
            load_attn(2)
            held(g_copy, NB + 1)
            held(p_log, NB)

            def load_expert(e, m, par, layer):
                first = isinstance(m, int) and m == NE // 2 * layer
                if not first:
                    held(p_h, use0(layer, 2 * m + par - 1))
                sp.dma_start(W1[par], w1[layer, e].rearrange("(a p) f -> p a f", p=P)).then_inc(s_w1[par], 16)
                if not first:
                    held(p_y, ST * (2 * m + par - 1))
                sp.dma_start(W2[par], w2[layer, e].rearrange("(f p) c -> p f c", p=P)).then_inc(s_w2[par], 16)

            load_expert(0, 0, 0, 0)
            load_expert(1, 0, 1, 0)
            held(v_topk, TOPK_STEPS)
            sp.dma_start(posd, POS).then_inc(s_rows, 16)
            sp.dma_start(prbd, PTK).then_inc(s_rows, 16)
            sp.dma_start(zbuf.rearrange("(p k) c -> p k c", p=P), ZERO[:, :].unsqueeze(1).to_broadcast([P, NE * SLOT // P, C + 1])).then_inc(s_zero, 16)
            with sp.Fori(1, NE // 2) as m:
                load_expert(2 * m, m, 0, 0)
                load_expert(2 * m + 1, m, 1, 0)
            sp.dma_start(gbuf.rearrange("(p k) c -> p k c", p=P), ZERO[:, 0:C].unsqueeze(1).to_broadcast([P, 2 * NT, C])).then_inc(s_gzero, 16)
            held(s_rows, 32)
            held(p_h, use0(0, NE))
            load_slot_rows(0)
            held(p_y, ST * NE)
            held(s_dec, 16)
            load_ones()
            for r in range(2):
                for w, dst in ((0, QS), (1, KS)):
                    sp.dma_start(dst[r][KSTK + NPART:KSTK + NPART + KDEC, :, :],
                                 decay_rows[:, w].unsqueeze(1).to_broadcast([KDEC, NH, T])).then_inc(s_drow, 16)
            attention_rounds_12(sp, body)

            held(g_copy, 2 * NB + 1)
            held(p_log, 2 * NB)
            half = NE // 2

            def load_expert_1(m, par):
                e = 2 * m + par - NE
                load_expert(e, m, par, 1)
                held(v_y, ST * (2 * m + par - 1))
                sp.dma_start(B1S[par], b1[e]).then_inc(s_b12[par], 16)
                sp.dma_start(B2B[par], b2[e].partition_broadcast(P)).then_inc(s_b12[par], 16)

            def load_slots(m, par):
                e = 2 * m + par - NE
                held(p_h, use0(1, 2 * m + par - 1 - 1) + CT)
                held(v_dst, DST_STEPS * (2 * m + par - 1 - NE))
                sp.dma_start(ZS[par], zbuf.rearrange("(e a p) c -> e p a c", e=NE, p=P)[e]).then_inc(s_zs[par], 16)

            load_expert_1(half, 0)
            load_expert_1(half, 1)
            held(s_scat, 16 * 2 * NT)
            for par in range(2):
                sp.dma_start(ZS[par], zbuf.rearrange("(e a p) c -> e p a c", e=NE, p=P)[par]).then_inc(s_zs[par], 16)
            with sp.Fori(half + 1, 2 * half) as m:
                for par in range(2):
                    load_slots(m, par)
                    load_expert_1(m, par)
            for r in range(2):
                held(s_ysc[r], 16 * ST * half)
            for g in range(4):
                for k in range(2):
                    sp.dma_start(GOT[k][:, 4 * g:4 * g + 4, :],
                                 gbuf.rearrange("(k i p) c -> k p i c", k=2, p=P)[k][:, 4 * g:4 * g + 4, :]).then_inc(s_got[g], 16)
            for g in range(4):
                held(v_out, g + 1)
                sp.dma_start(out.rearrange("b (a p) c -> p (b a) c", p=P)[:, 4 * g:4 * g + 4, :], Xall[:, 4 * g:4 * g + 4, :]).then_inc(s_out, 16)
            held(s_out, 64)

        @block.gpsimd
        def _(pool):
            nc.gpsimd.memset(ONES[:, :], 1.0).then_inc(g_const, 1)
            nc.gpsimd.memset(POWH[:, :], -0.5).then_inc(g_const, 1)

            def rstd(sem_ve, value):
                pool.wait_ge(sem_ve, value)
                nc.gpsimd.tensor_tensor(RSTD[:, :], VE[:, :], POWH[:, :], ALU.pow).then_inc(g_rstd, 1)

            pool.wait_ge(g_const, 2)
            pool.wait_ge(s_const, 64)
            nc.gpsimd.tensor_copy(XNall[:, :, C], cst("token")).then_inc(g_copy, 1)

            def convert_mask(q, which):
                nc.gpsimd.tensor_scalar(BMK[q.par][:, which], MASKU[q.par][:, which], 1.0, BIG, ALU.subtract, ALU.mult).then_inc(g_mask, 1)

            def affine(x, rows, before, done, count):
                for i, op, sem in ((0, ALU.mult, g_aff), (1, ALU.add, done)):
                    par = LNP[:, rows + i, :].unsqueeze(1).to_broadcast([P, TT, C])
                    if i == 0:
                        pool.wait_ge(*before)
                    else:
                        pool.wait_ge(g_aff, count + 1)
                    nc.gpsimd.tensor_tensor(x, x, par, op).then_inc(sem, 1)

            def affines_before(t):
                if isinstance(t.n, int):
                    return t.done(3) - 2 * NB + max(0, t.done(-1) - 2 * NB)
                return 2 * t.n + 2 - 4 * NB

            def add_output_bias(z, lp):
                if isinstance(z.n, int) and z.n % NB == 0:
                    pool.wait_ge(s_w[lp], 80)
                if lp == 2:
                    pool.wait_ge(v_xn, z.n + 1)
                v = (UALL if lp == 2 else Xall)[:, bass.ts(z.batch(lp), TT), :]
                if lp < 2:
                    pool.wait_ge(v_xn, z.n + 1)
                nc.gpsimd.tensor_tensor(v, v, BO[lp % 2][:, :].unsqueeze(1).to_broadcast([P, TT, C]), ALU.add).then_inc(g_bo, 1)

            def body(t, lp, la, ls, lc, lo):
                lr = routes(lo)
                z, q, y = t.next(3), t.next(2), t.next(-1)
                aff = affines_before(t)

                def maxima_mask():
                    pool.wait_ge(s_msk[q.par], 16 * (q.m + 1))
                    wait(pool, v_bank, t.done(2) + 16 * t.done(1))
                    alone(pool)
                    convert_mask(q, 0)

                if la == 0 and isinstance(t.n, int) and t.n < 0:
                    maxima_mask()
                if lp in (0, 2):
                    rstd(v_lnp, nln(lp, z.n) + 5)
                    if lp == 0:
                        add_output_bias(z, lp)
                if la is not None:
                    pool.wait_ge(a_split, 2 * q.n + 1)
                    nc.gpsimd.tensor_tensor(QK32, QK32, QKP[0][:, :, :, :], ALU.subtract).then_inc(g_split, 1)
                if la == 0 and not (isinstance(t.n, int) and t.n < 0):
                    maxima_mask()
                if lr is not None:
                    k = routed(lr, y.n)
                    rstd(v_lnr, 5 * k + 5)
                if la is not None:
                    pool.wait_ge(a_split, 2 * q.n + 2)
                    nc.gpsimd.tensor_tensor(QKP[2][:, :, :, :], QK32, QKP[1][:, :, :, :], ALU.subtract).then_inc(g_split, 1)
                if lr is not None:
                    if lr == 2:
                        affine(XRS, 2, (v_xr, k + 1), g_xr, aff)
                        aff = aff + 1
                if lp == 2:
                    rstd(v_lnp, nln(lp, z.n) + 11)
                if lr is not None:
                    if lr == 2:
                        pool.wait_ge(g_xr, k + 1 - NB)
                    else:
                        pool.wait_ge(v_xr, k + 1)
                    nc.gpsimd.tensor_copy(XNall[:, bass.ts(y.batch(lr), TT), 0:C], XRS).then_inc(g_copy, 1)
                if lp == 2:
                    affine(XNS, 0, (v_xn, z.n + 1), g_xn, aff)
                    add_output_bias(z, lp)
                if lo == 2:
                    xv = Xall[:, bass.ts(y.batch(2), TT), :]
                    nc.gpsimd.tensor_tensor(xv, xv, UALL[:, bass.ts(y.batch(2), TT), :], ALU.add).then_inc(g_base, 1)
                if lp == 1:
                    rstd(v_lnp, nln(lp, z.n) + 5)
                    add_output_bias(z, lp)
                if la == 0:
                    wait(pool, p_st, 8 * (q.n - 1))
                    alone(pool)
                    convert_mask(q, 1)

            attention_rounds_0(pool, body)
            attention_rounds_12(pool, body)
            pool.wait_ge(s_zero, 16)
            pool.wait_ge(g_base, NB)
            pool.wait_ge(g_copy, 2 * NB + 1)
            for k in range(2):
                pool.wait_ge(v_rt, (FIRST_STEPS, ROUTE_STEPS)[k])
                for i in range(NT):
                    nc.gpsimd.indirect_dma_start(
                        out=zbuf, out_offset=bass.IndirectOffsetOnAxis(ap=IDX[:, k, i:i + 1], axis=0),
                        in_=XNall[:, i, :], in_offset=None, bounds_check=NE * SLOT - 1, oob_is_err=False).then_inc(s_scat, 16)
            pool.wait_ge(s_gzero, 16)
            with pool.Fori(NE // 2, NE) as m:
                for par in range(2):
                    pool.wait_ge(v_dst, DST_STEPS * (2 * m + par + 1 - NE))
                    for st in range(ST):
                        pool.wait_ge(v_y, ST * (2 * m + par) + st + 1)
                        alone(pool)
                        nc.gpsimd.indirect_dma_start(
                            out=gbuf, out_offset=bass.IndirectOffsetOnAxis(ap=DSTI[par][:, st:st + 1], axis=0),
                            in_=YS[par][:, st, :], in_offset=None,
                            bounds_check=2 * NB * T - 1, oob_is_err=False).then_inc(s_ysc[par], 16)

        @block.scalar
        def _(act):
            def body(t, lp, la, ls, lc, lo):
                lr = routes(lo)
                q = t.next(2)

                def high_parts():
                    act.wait_ge(a_bank, 3 * q.n + 3)
                    prev = q.next(-1)
                    if not (isinstance(prev.n, int) and prev.n < 0):
                        act.wait_ge(s_stk[prev.par], 192 * (prev.m + 1))
                    nc.scalar.copy(QKP[0][:, :, :, :], QK32).then_inc(a_split, 1)

                def middle_parts():
                    act.wait_ge(g_split, 2 * q.n + 1)
                    nc.scalar.copy(QKP[1][:, :, :, :], QK32).then_inc(a_split, 1)

                if la is not None:
                    r = la % 2
                    if isinstance(q.n, int) and q.n % NB == 0:
                        act.wait_ge(v_q4, 1 + q.n // NB)
                        act.wait_ge(s_w[la], 80)
                    act.wait_ge(p_a, 4 * q.n + 1)
                    nc.scalar.copy(XNT.rearrange("p a t -> p (a t)"), PS[0][:, :]).then_inc(a_bank, 1)
                    act.wait_ge(p_a, 4 * q.n + 2)
                    wait(act, g_split, 2 * q.n)
                    for i, w in enumerate(projections(la)):
                        if i == 1:
                            act.wait_ge(p_a, 4 * q.n + 3)
                        bias = BQ4[r] if w == 0 else BQK[r][:, 1]
                        for c in range(CT):
                            ins = nc.scalar.activation(QK32[:, w, c, :], PS[1 - i][:, c * T:(c + 1) * T], ACT.Identity,
                                                       bias=bias[:, c:c + 1], scale=0.25 if w == 0 else 1.0)
                        ins.then_inc(a_bank, 1)
                    if lc is None:
                        high_parts()
                        middle_parts()
                if lc is not None:
                    for pr in range(NH // 2):
                        act.wait_ge(p_st, 8 * t.n + pr + 1)
                        wait(act, p_pv, 8 * t.n + pr - 1)
                        nc.scalar.activation(PT[pr % 2].rearrange("p h a t -> p (h a t)"),
                                             PTT[pr % 2][:, :, :].rearrange("p h k -> p (h k)"), ACT.Exp).then_inc(a_exp, 1)
                        if pr == 0 and la is not None:
                            high_parts()
                        if pr == 2 and la is not None:
                            middle_parts()
                        if lr is not None and pr == (6 if lr == 0 else 7):
                            router_input(routed(lr, t.n - 1))
                elif lr is not None:
                    router_input(routed(lr, t.n - 1))

            def router_input(k):
                act.wait_ge(p_rt, k + 1)
                nc.scalar.copy(XRT.rearrange("p a t -> p (a t)"), PM[:, :]).then_inc(a_xrt, 1)

            attention_rounds_0(act, body)

            act.wait_ge(v_topk, 2)
            nc.scalar.activation(LOG[:, :, :], LOG[:, :, :], ACT.Exp).then_inc(a_topk, 1)
            act.wait_ge(g_copy, NB + 1)
            def stage_rows(b, par):
                wait(act, p_disp, CT * (b - 1))
                nc.scalar.copy(XST[par], XNall[:, bass.ts(b, TT), 0:C]).then_inc(a_xst, 1)

            def gather(m, par):
                b = 2 * m + par
                if not (isinstance(b, int) and b == NB - 1):
                    stage_rows(b + 1, 1 - par)
                act.wait_ge(p_disp, CT * b + 1)
                nc.scalar.copy(xint[:, 0, :].rearrange("p (e b s) -> p e b s", e=NE, b=NB)[:, :, b, :],
                               PTT[par][:, 0, :].rearrange("p (e s) -> p e s", e=NE)).then_inc(a_xi, 1)

            stage_rows(0, 0)
            gather_rounds(act, gather)

            def hidden(m, par, layer):
                e = 2 * m + par
                wait(act, p_y, ST * (e - 1))
                if layer == 1:
                    act.wait_ge(s_b12[par], 32 * (m - NE // 2 + 1))
                for f in range(FT):
                    k = use0(layer, e) + uses(layer) - FT + f
                    j = (uses(layer) * par + uses(layer) - FT + f) % 4
                    act.wait_ge(p_h, k + 1)
                    src = PTT[j // 2][:, j % 2, :]
                    if layer == 0:
                        ins = nc.scalar.activation(ht[:, par, f, :], src, ACT.Gelu)
                    else:
                        ins = nc.scalar.activation(ht[:, par, f, :], src, ACT.Relu, bias=B1S[par][:, f:f + 1])
                    ins.then_inc(a_h, 1)

            def turned(m, par):
                e = 2 * m + par
                for c in range(CT):
                    j = (uses(1) * par + c) % 4
                    act.wait_ge(p_h, use0(1, e) + c + 1)
                    nc.scalar.copy(ZT[par][:, c, :], PTT[j // 2][:, j % 2, :]).then_inc(a_h, 1)

            def step(layer):
                def go(m, par, last):
                    q = Turn(m, par)
                    if not last:
                        hidden(q.next().m, q.next().par, layer)
                        if layer == 1 and not (isinstance(m, int) and m > NE // 2 and par == 0):
                            turned(q.next(2).m, q.next(2).par)
                return go

            expert_rounds(act, lambda: hidden(0, 0, 0), step(0), 0)
            attention_rounds_12(act, body)
            act.wait_ge(v_rt, 2)
            nc.scalar.activation(PRR, PRR, ACT.Exp).then_inc(a_rt, 1)

            def first():
                turned(NE // 2, 0)
                hidden(NE // 2, 0, 1)
                turned(NE // 2, 1)
            expert_rounds(act, first, step(1), 1)

        @block.vector
        def _(dve):
            nc.vector.memset(ZERO[:, :], 0.0)
            c = Steps(dve, v_const, 0)
            for r in range(2):
                c.step(nc.vector.memset(VA[r][:, :, :, :], 0.0))
            c.settle()
            for r in range(2):
                c.step(nc.vector.memset(VA[r][:, :, :, 0:1], 1.0))

            def make_decay():
                dve.wait_ge(s_const, 64)
                c.step(nc.vector.tensor_copy(TDB[:, 0:1], TD[:, :]))
                c.settle()
                c.step(nc.vector.tensor_tensor(TDP[:, 3:4], TD[:, :], TDB[:, 0:1], ALU.subtract))
                c.settle()
                c.step(nc.vector.tensor_copy(TDB[:, 1:2], TDP[:, 3:4]))
                c.settle()
                c.step(nc.vector.tensor_tensor(TDP[:, 4:5], TDP[:, 3:4], TDB[:, 1:2], ALU.subtract))
                c.settle()
                c.step(nc.vector.tensor_copy(TDB[:, 2:3], TDP[:, 4:5]))
                c.settle()
                c.step(nc.vector.tensor_scalar(TDP[:, 0:3], TDB[:, :], -1.0, None, ALU.mult))
                c.settle()
                for i in range(NPART):
                    c.step(nc.vector.tensor_scalar(TDI[:, i, :], identb, TDP[:, i:i + 1], None, ALU.mult))

                part = CF["part"][0]
                c.step(nc.vector.tensor_tensor(TDP6[:, :], TDP[0:KDEC, 0:NPART], cfs[0:KDEC, part:part + NPART], ALU.mult))
                c.settle()
                c.step(nc.vector.tensor_reduce(PSEL[:, :], TDP6[:, :], AX.X, ALU.add))
                c.settle()
                nc.vector.scalar_tensor_tensor(DROW[0:KDEC], CD[0:KDEC, 0], PSEL[:, :], CD[0:KDEC, 1], ALU.mult, ALU.add).then_inc(v_decay, 1)

            def quarter_bias(layer):
                dve.wait_ge(s_w[layer], 80)
                nc.vector.tensor_scalar(BQ4[layer % 2][:, :], BQK[layer % 2][:, 0, :], 0.25, None, ALU.mult).then_inc(v_q4, 1)


            def norm_stats(s, src, a):
                alone(dve)
                s.step(nc.vector.bn_stats(STATS[:, a, :], src(a)))

            def norm_spread(s):
                s.settle()
                alone(dve)
                for a in range(TT):
                    s.step(nc.vector.bn_aggr(MV[:, a, :], STATS[:, a, :]))
                s.settle()
                s.step(nc.vector.tensor_scalar(VE[:, :], MV[:, :, 1], EPS, None, ALU.add))

            def norm_apply(s, dst, src, a, powers, done):
                dve.wait_ge(g_rstd, powers)
                ins = nc.vector.tensor_scalar(dst[:, a, :], src(a), MV[:, a, 0:1], RSTD[:, a:a + 1], ALU.subtract, ALU.mult)
                if a == TT - 1:
                    if done is None:
                        s.step(ins)
                    else:
                        ins.then_inc(done, 1)

            def powers_before(t, lo):
                if not isinstance(t.n, int):
                    return (2 * t.n + 2, t.n + NB + 3, 3 * t.n - 19)[lo]
                p = t.done(3)
                return p + max(0, p - 2 * NB) + (min(max(t.n - 1, 0), NB) if t.phase == 0 else NB + max(0, t.n - 1 - 2 * NB))

            def combine_weights(z):
                dve.wait_ge(s_bc, 64 * (z.n - NB + 1))
                wait(dve, p_comb, z.n - NB - 1)
                nc.vector.scalar_tensor_tensor(WCT[z.par].rearrange("p i t -> p (i t)"), BPOS.rearrange("p i t -> p (i t)"),
                                               cst("slot"), BPRB.rearrange("p i t -> p (i t)"),
                                               ALU.is_equal, ALU.mult).then_inc(v_wct, 1)

            def body(t, lp, la, ls, lc, lo):
                lr = routes(lo)
                z, q, y = t.next(3), t.next(2), t.next(-1)
                r = None if la is None else la % 2
                before = t.done(2) + 16 * t.done(1)
                powers = powers_before(t, lo)
                first = isinstance(t.n, int)

                if la is not None and first and q.n % NB == 0 and q.n < 3 * NB:
                    quarter_bias(la)

                def turn_group(g):
                    dve.wait_ge(p_pv, 8 * t.n + 2 * g + 2)
                    if g == 0:
                        wait(dve, v_ot, HEAD_STEPS * t.n)
                    elif g == 2:
                        dve.wait_ge(v_ot, HEAD_STEPS * t.n + 5)
                    nc.vector.transpose(OQ[:, g % 2, :], PO[:, 0:T]).then_inc(v_ot, 1)

                blocks = OQ.rearrange("p i (b d) -> p i b d", d=32)

                def invert(s):
                    s.settle()
                    s.step(nc.vector.reciprocal(RS[:, :, :], blocks[:, :, :, 0]))

                def scale(s):
                    s.settle()
                    s.step(nc.vector.tensor_tensor(OC.rearrange("p b i d -> p i b d"), blocks[:, :, :, 1:1 + HD],
                                                   RS[:, :, :].unsqueeze(3).to_broadcast([P, 2, T // 32, HD]), ALU.mult))

                def turn_back(s, u, pair):
                    s.settle()
                    if pair == 0:
                        wait(dve, p_wo, u.n)
                    s.step(nc.vector.transpose(OT[:, pair, :], OC.rearrange("p b i d -> p (b i d)")))

                if lo is not None:
                    h = Steps(dve, v_ot, HEAD_STEPS * y.n + 7)
                if lc is not None:
                    s = Steps(dve, v_nm, 6 * t.n)
                    dve.wait_ge(v_bank, before)
                    if lc == 0:
                        s.step(nc.vector.tensor_scalar(NM[:, 1], MX[:, :, :], -BIG / 2, HUGE, ALU.is_lt, ALU.mult))
                        s.settle()
                        s.step(nc.vector.tensor_tensor(NM[:, 0], NM[:, 1], MX[:, :, :], ALU.subtract))
                    else:
                        s.step(nc.vector.tensor_scalar(NM[:, 0], MX[:, :, :], -1.0, None, ALU.mult), 2)
                if lo is not None:
                    invert(h)
                if lc is not None:
                    s.settle()
                    s.step(nc.vector.tensor_copy(NMP[:, :, 0, :], NM[:, 0]))
                    s.settle()
                    s.step(nc.vector.tensor_tensor(NM[:, 1], NM[:, 0], NMP[:, :, 0, :], ALU.subtract))
                if lo is not None:
                    scale(h)
                if lc is not None:
                    s.settle()
                    s.step(nc.vector.tensor_copy(NMP[:, :, 1, :], NM[:, 1]))
                    s.settle()
                    s.step(nc.vector.tensor_tensor(NMP[:, :, 2, :], NM[:, 1], NMP[:, :, 1, :], ALU.subtract))
                if lo is not None:
                    turn_back(h, y, 1)
                if lc is not None:
                    dve.wait_ge(p_nm, t.n + 1)
                    if not (first and t.n == 0):
                        dve.wait_ge(s_nml[y.par], 16 * (y.m + 1))
                    nc.vector.tensor_copy(NMT[:, :], nm_bf).then_inc(v_nmt, 1)
                def prepared_rows(a):
                    return Xall[:, z.batch(lp) * TT + a, :]

                if lp in (0, 2):
                    if lp == 0:
                        if first and z.n < 2:
                            dve.wait_ge((s_x0, s_x1)[z.n], 16)
                        else:
                            dve.wait_ge(s_x, 16 * (NB - 2))
                    else:
                        dve.wait_ge(v_res, z.n - NB + 1)
                        if first and z.n == 2 * NB:
                            dve.wait_ge(s_lnp, 16)
                    st = Steps(dve, v_lnp, nln(lp, z.n))
                    for a in range(TT):
                        norm_stats(st, prepared_rows, a)
                    norm_spread(st)
                    powers = powers + 1
                    if lp == 0:
                        wait(dve, p_a, 4 * (z.n - 1) + 1)
                    for a in range(TT):
                        if lp == 0:
                            norm_apply(st, XNS, prepared_rows, a, powers, v_xn)
                        else:
                            norm_apply(st, UALL[:, bass.ts(z.batch(lp), TT), :], prepared_rows, a, powers, None)
                            normed_rows = lambda a: UALL[:, z.batch(lp) * TT + a, :]
                if lo is not None:
                    b = y.batch(lo)
                    dve.wait_ge(p_wo, t.n)
                    dve.wait_ge(g_bo, t.n)
                    xv = Xall[:, bass.ts(b, TT), :]
                    pv = PM[:, :].rearrange("p (a c) -> p a c", a=TT)
                    if lo < 2:
                        nc.vector.tensor_tensor(xv, xv, pv, ALU.add).then_inc(v_res, 1)
                    else:
                        uv = UALL[:, bass.ts(b, TT), :]
                        nc.vector.tensor_tensor(uv, uv, pv, ALU.add).then_inc(v_res, 1)

                def score(hp, a):
                    if ls is None:
                        return
                    k = 2 * hp + a
                    if k == 0 and ls == 0:
                        dve.wait_ge(g_mask, 2 * t.next().n + 1)
                    dve.wait_ge(p_s, 16 * t.next().n + k + 1)
                    bank = PS[(k + 1) % 2][:, :].rearrange("p (h k) -> p h k", h=2)
                    if ls == 2:
                        ins = nc.vector.tensor_reduce(MX[:, a, 2 * hp:2 * hp + 2], bank, AX.X, ALU.max)
                    else:
                        wait(dve, v_bank, before + max(k - 1, 0))
                        alone(dve)
                        for h in range(2):
                            ins = nc.vector.tensor_tensor_reduce(
                                out=JUNK[:, a, h], in0=bank[:, h, :], in1=BMK[t.next().par][:, 0, a, :] if ls == 0 else DECAY[:, a, :],
                                scale=1.0, scalar=-3e38, op0=ALU.add, op1=ALU.max, accum_out=MX[:, a, 2 * hp + h:2 * hp + h + 1])
                    ins.then_inc(v_bank, 1)

                if lp == 1 and not (first and z.n == NB):
                    combine_weights(z)
                score(0, 0)
                if lr is not None:
                    k = routed(lr, y.n)
                    b = y.batch(lr)
                    dve.wait_ge(v_res, t.n)
                    src = Xall if lr == 0 else UALL
                    rows = lambda a: src[:, b * TT + a, :]
                    rn = Steps(dve, v_lnr, 5 * k)
                    norm_stats(rn, rows, 0)
                score(0, 1)
                if lr is not None:
                    norm_stats(rn, rows, 1)
                score(1, 0)
                if lc is not None:
                    turn_group(0)
                if lr is not None:
                    norm_spread(rn)
                    powers = powers + 1
                score(1, 1)
                score(2, 0)
                score(2, 1)
                if lr is not None:
                    dve.wait_ge(g_copy, k + 1)
                    norm_apply(rn, XRS, rows, 0, powers, v_xr)
                score(3, 0)
                if lc is not None:
                    turn_group(1)
                score(3, 1)
                if lc is not None:
                    h = Steps(dve, v_ot, HEAD_STEPS * t.n + 2)
                    invert(h)
                if lr is not None:
                    norm_apply(rn, XRS, rows, 1, powers, v_xr)
                if lp == 1:
                    dve.wait_ge(p_comb, z.n - NB + 1)
                    xv = Xall[:, bass.ts(z.batch(1), TT), :]
                    nc.vector.tensor_tensor(xv, xv, PM[:, :].rearrange("p (a c) -> p a c", a=TT), ALU.add).then_inc(v_comb, 1)
                score(4, 0)
                if lc is not None:
                    scale(h)
                if lp == 1:
                    dve.wait_ge(v_comb, z.n - NB + 1)
                    rows = prepared_rows
                    st = Steps(dve, v_lnp, nln(lp, z.n))
                    norm_stats(st, rows, 0)
                elif lp == 2:
                    rows = normed_rows
                    st = Steps(dve, v_lnp, nln(lp, z.n) + 6)
                    st.settle()
                    norm_stats(st, rows, 0)
                score(4, 1)
                if lc is not None:
                    turn_back(h, t, 0)
                if lp in (1, 2):
                    norm_stats(st, rows, 1)
                score(5, 0)
                if lc is not None:
                    turn_group(2)
                if lp in (1, 2):
                    norm_spread(st)
                score(5, 1)
                score(6, 0)
                if lp in (1, 2):
                    dve.wait_ge(p_a, 4 * (z.n - 1) + 1)
                    norm_apply(st, XNS, rows, 0, powers + 1, v_xn)
                score(6, 1)
                if lp in (1, 2):
                    norm_apply(st, XNS, rows, 1, powers + 1, v_xn)
                score(7, 0)
                if lc is not None:
                    turn_group(3)
                score(7, 1)
                if lr is not None:
                    dve.wait_ge(p_log, k + 1)
                    nc.vector.tensor_copy(LOG[:, bass.ts(y.batch(lr), TT), :],
                                          PM[:, 0:TT * NE].rearrange("p (a e) -> p a e", a=TT)).then_inc(v_log, 1)
                if la is not None:
                    dve.wait_ge(p_a, 4 * q.n + 4)
                    wait(dve, p_pv, 8 * (q.n - 1))
                    nc.vector.tensor_tensor(
                        VA[q.par][:, :, :, 1:1 + HD], PS[1][:, :].rearrange("p (a h d) -> p a h d", a=TT, h=NH),
                        BV[r][:, :].rearrange("p (h d) -> p h d", h=NH).unsqueeze(1).to_broadcast([P, TT, NH, HD]),
                        ALU.add).then_inc(v_bank, 1)

            def body_0(t, *layers):
                body(t, *layers)
                if isinstance(t.n, int) and t.n == -2:
                    make_decay()

            attention_rounds_0(dve, body_0)

            def softmax(s, src, dst, a_sem):
                s.step(nc.vector.tensor_reduce(SM[:, :], LOG[:, :, :], AX.X, ALU.max))
                s.settle()
                s.step(nc.vector.tensor_tensor(dst, src, SM[:, :].unsqueeze(2).to_broadcast([P, NT, NE]), ALU.subtract))
                dve.wait_ge(a_sem, 1)
                s.step(nc.vector.tensor_reduce(SMR[:, :], dst, AX.X, ALU.add))
                s.settle()
                s.step(nc.vector.reciprocal(SM[:, :], SMR[:, :]))
                s.settle()

            dve.wait_ge(v_log, NB)
            s = Steps(dve, v_topk, 0)
            softmax(s, LOG[:, :, :], LOG[:, :, :], a_topk)
            s.step(nc.vector.tensor_tensor(
                PR[:, :, :, :].rearrange("p a b e -> p b a e"), LOG[:, :, :].rearrange("p (b a) e -> p b a e", a=TT),
                SM[:, :].rearrange("p (b a) -> p b a", a=TT).unsqueeze(3).to_broadcast([P, NB, TT, NE]), ALU.mult))
            dve.wait_ge(p_topk, 1)
            s.step(nc.vector.tensor_copy(PTK, PM[0:NB * NE, 0:T]))
            s.settle()
            for i in range(CAP0 // 8):
                cur = PTK if i == 0 else WORK
                s.step(nc.vector.max(TOP8[:, :], cur))
                s.settle()
                s.step(nc.vector.match_replace(WORK, TOP8[:, :], cur, -1.0))
                s.settle()
            s.step(nc.vector.tensor_scalar(CHOSEN, WORK, 0.0, None, ALU.is_lt))
            s.settle()
            s.step(nc.vector.tensor_tensor_scan(POS, CHOSEN, CHOSEN, 0.0, ALU.add, ALU.max))
            s.settle()
            s.step(nc.vector.tensor_tensor(POS, POS, CHOSEN, ALU.mult))
            s.settle()
            s.step(nc.vector.tensor_scalar(POS, POS, -1.0, None, ALU.add))
            assert s.k == TOPK_STEPS
            dve.wait_ge(p_topk, 2)
            s.step(nc.vector.tensor_copy(POST[:, :, :], PM[:, 0:TT * NB * NE].rearrange("p (a r) -> p a r", a=TT)))
            s.settle()
            def gather_matrix(b, par):
                wait(dve, p_disp, CT * (b - 1))
                for a in range(TT):
                    nc.vector.tensor_tensor(
                        GSEL[par][:, a], cst("iota").unsqueeze(1).to_broadcast([P, NE, CAP0]),
                        POST[:, a, bass.ts(b, NE)].unsqueeze(2).to_broadcast([P, NE, CAP0]),
                        ALU.is_equal).then_inc(v_gsel, 1)

            def gather(m, par):
                b = 2 * m + par
                if not (isinstance(b, int) and b == NB - 1):
                    gather_matrix(b + 1, 1 - par)
                dve.wait_ge(p_disp, CT * b + 2)
                nc.vector.tensor_copy(xint[:, 1, :].rearrange("p (e b s) -> p e b s", e=NE, b=NB)[:, :, b, :],
                                      PTT[par][:, 1, :].rearrange("p (e s) -> p e s", e=NE)).then_inc(v_xi, 1)

            gather_matrix(0, 0)
            gather_rounds(dve, gather)

            def destinations(m, par):
                e = 2 * m + par - NE
                ids = ZS[par][:, :, C]
                s = Steps(dve, v_dst, DST_STEPS * e)
                dve.wait_ge(s_zs[par], 16 * (m - NE // 2 + 1))
                if not isinstance(e, int) or e > 0:
                    s.settle()
                alone(dve)
                s.step(nc.vector.tensor_scalar(DST[:, 0, :], cst("place"), FIRSTS[:, bass.ds(e, 1)], float(NB * T), ALU.is_ge, ALU.mult))
                s.step(nc.vector.tensor_scalar(DST[:, 1, :], ids, 0.5, 65536.0, ALU.is_lt, ALU.mult))
                s.settle()
                s.step(nc.vector.tensor_tensor(DST[:, 0, :], DST[:, 0, :], DST[:, 1, :], ALU.add))
                s.settle()
                s.step(nc.vector.scalar_tensor_tensor(DSTI[par][:, :], DST[:, 0, :], -1.0, ids, ALU.add, ALU.add))

            def expert_out(layer):
                def go(m, par, last):
                    e = 2 * m + par
                    if last and layer == 0:
                        combine_weights(Turn(NB // 2, 0, 1))
                    for st in range(ST):
                        bk = (PS[0], PS[1], PO, PM)[st]
                        dve.wait_ge(p_y, ST * e + st + 1)
                        if layer == 0:
                            for h in range(2):
                                ins = nc.vector.tensor_copy(yall[64 * par:64 * par + 64, (2 * st + h) * (NE // 2) + m, :],
                                                            bk[64 * h:64 * h + 64, 0:C])
                        else:
                            if st == 0:
                                if not (isinstance(m, int) and m == NE // 2):
                                    dve.wait_ge(s_ysc[par], 16 * ST * (m - NE // 2))
                                destinations(m, par)
                                dve.wait_ge(s_b12[par], 32 * (m - NE // 2 + 1))
                            ins = nc.vector.tensor_tensor(YS[par][:, st, :], bk[:, 0:C], B2B[par], ALU.add)
                        ins.then_inc(v_y, 1)
                return go

            dve.wait_ge(s_rows, 32)
            expert_rounds(dve, lambda: None, expert_out(0), 0)
            nc.vector.tensor_scalar(DECAY, dist, TD[:, :], -1.0, ALU.mult, ALU.mult).then_inc(v_decay, 1)
            dve.wait_ge(v_decay, 2)
            attention_rounds_12(dve, body)

            dve.wait_ge(v_log, 2 * NB)
            dve.wait_ge(p_wo, 3 * NB)
            s = Steps(dve, v_rt, 0)
            softmax(s, LOG[:, :, :], PRR, a_rt)
            s.step(nc.vector.tensor_tensor(PRR, PRR, SM[:, :].unsqueeze(2).to_broadcast([P, NT, NE]), ALU.mult))
            s.settle()
            by_expert = lambda v: v.unsqueeze(2).to_broadcast([P, NT, NE])
            for k, src in ((0, PRR), (1, TMP[:, 0])):
                if k:
                    s.step(nc.vector.scalar_tensor_tensor(TMP[:, 0], PICK[:, 0], -BIG, LOG[:, :, :], ALU.mult, ALU.add))
                    s.settle()
                s.step(nc.vector.tensor_reduce(SM[:, :], src, AX.X, ALU.max))
                s.settle()
                s.step(nc.vector.tensor_tensor(EQ, src, by_expert(SM[:, :]), ALU.is_equal))
                s.settle()
                s.step(nc.vector.tensor_tensor(EQ, EQ, cst("rev").unsqueeze(1).to_broadcast([P, NT, NE]), ALU.mult))
                s.settle()
                s.step(nc.vector.tensor_reduce(SMR[:, :], EQ, AX.X, ALU.max))
                s.settle()
                s.step(nc.vector.tensor_tensor(PICK[:, k], EQ, by_expert(SMR[:, :]), ALU.is_equal))
                s.settle()
            assert s.k == PICK_STEPS, s.k
            def picked(dst, pick, value):
                tmp = TMP if pick is PICK else TMP[:, 0]
                s.step(nc.vector.tensor_tensor(tmp, pick, value, ALU.mult))
                s.settle()
                s.step(nc.vector.tensor_reduce(dst, tmp, AX.X, ALU.add))
                s.settle()

            picked(ES[:, :, :], PICK, cst("base").unsqueeze(1).unsqueeze(1).to_broadcast([P, 2, NT, NE]))
            picked(G12[:, :, :], PICK, PRR.unsqueeze(1).to_broadcast([P, 2, NT, NE]))
            dve.wait_ge(p_rte, 2)
            s.step(nc.vector.tensor_copy(TOT, PS[1][:, 0:2 * NE * NT].rearrange("p (k i e) -> p k e i", k=2, i=NT)))
            s.settle()
            flat = lambda v: v.rearrange("p k e i -> p (k e i)")
            s.step(nc.vector.tensor_tensor_scan(flat(SCN), cst("keep"), flat(TOT), 0.0, ALU.mult, ALU.add))
            s.settle()
            s.step(nc.vector.tensor_tensor(EXC, SCN, TOT, ALU.subtract))
            s.settle()
            s.step(nc.vector.tensor_tensor(LOC, PS[0][:, 0:2 * NE * NT].rearrange("p (k i e) -> p k i e", k=2, i=NT),
                                           EXC.rearrange("p k e i -> p k i e"), ALU.add))
            s.settle()
            for k in range(2):
                if k == 1:
                    s.step(nc.vector.tensor_tensor(LOC[:, 1], LOC[:, 1], SCN[:, 0, :, NT - 1].unsqueeze(1).to_broadcast([P, NT, NE]), ALU.add))
                    s.settle()
                picked(LS[:, k], PICK[:, k], LOC[:, k])
                s.step(nc.vector.tensor_scalar(FIT[:, k], LS[:, k], float(SLOT), None, ALU.is_le))
                s.settle()
                s.step(nc.vector.scalar_tensor_tensor(IDXF[:, k], FIT[:, k], -65536.0, ES[:, k], ALU.mult, ALU.add))
                s.settle()
                s.step(nc.vector.tensor_tensor(IDXF[:, k], IDXF[:, k], LS[:, k], ALU.add))
                s.settle()
                s.step(nc.vector.tensor_scalar(IDX[:, k], IDXF[:, k], 65535.0, None, ALU.add))
                s.settle()
                if k == 0:
                    assert s.k == FIRST_STEPS, s.k
            assert s.k == ROUTE_STEPS, s.k
            s.step(nc.vector.tensor_copy(FIRSTS[:, :], SCN[:, 0, :, NT - 1]))
            s.step(nc.vector.tensor_tensor(G12[:, :, :], G12[:, :, :], FIT[:, :, :], ALU.mult))
            s.settle()
            s.step(nc.vector.tensor_tensor(SM[:, :], G12[:, 0, :], G12[:, 1, :], ALU.add))
            s.settle()
            s.step(nc.vector.tensor_scalar(SM[:, :], SM[:, :], 2.0 ** -23, None, ALU.max))
            s.settle()
            s.step(nc.vector.reciprocal(SMR[:, :], SM[:, :]))
            s.settle()
            s.step(nc.vector.scalar_tensor_tensor(G12[:, :, :], G12[:, :, :], 0.8, SMR[:, :].unsqueeze(1).to_broadcast([P, 2, NT]), ALU.mult, ALU.mult))
            s.settle()
            expert_rounds(dve, lambda: None, expert_out(1), 1)

            for g in range(4):
                dve.wait_ge(s_got[g], 16 * 2)
                for k in range(2):
                    for i in range(4 * g, 4 * g + 4):
                        ins = nc.vector.scalar_tensor_tensor(Xall[:, i, :], GOT[k][:, i, :], G12[:, k, i:i + 1], Xall[:, i, :], ALU.mult, ALU.add)
                        if k == 0 and i % 4 == 3:
                            s.step(ins)
                            s.settle()
                ins.then_inc(v_out, 1)

        @block.tensor
        def _(pe):
            mm = nc.tensor.matmul
            pe.wait_ge(s_const, 64)

            def project(q, la, i):
                r = la % 2
                w = projections(la)[i]
                if w == 0 or la == 2:
                    pe.wait_ge(a_bank, 3 * q.n + 1)
                    src = XNT
                else:
                    pe.wait_ge(s_ctx[q.par], 16 * (q.m + 1))
                    src = CTX[q.par]
                if i == 1:
                    pe.wait_ge(a_bank, 3 * q.n + 1)
                bk = PS[1 - i]
                for mt in range(CT):
                    for a in range(CT):
                        ins = mm(bk[:, mt * T:(mt + 1) * T], WQKV[r][:, w, a, mt * P:(mt + 1) * P], src[:, a, :],
                                 start=(a == 0), stop=(a == CT - 1))
                ins.then_inc(p_a, 1)

            def values(q, la):
                kv = XNT if la == 2 else CTX[q.par]
                for tk in range(TT):
                    for a in range(CT):
                        ins = mm(PS[1][:, tk * C:(tk + 1) * C], kv[:, a, tk * P:(tk + 1) * P], WQKV[la % 2][:, 2, a, :],
                                 start=(a == 0), stop=(a == CT - 1))
                ins.then_inc(p_a, 1)

            def scores(q, hp, a, before, projected):
                k = 2 * hp + a
                if k == 0:
                    pe.wait_ge(s_stk[q.par], 192 * (q.m + 1))
                bk = PS[(k + 1) % 2]
                if k < 2 and projected is not None:
                    pe.wait_ge(a_bank, projected + 2 + k)
                else:
                    pe.wait_ge(v_bank, before + max(k - 1, 0))
                for h in range(2):
                    ins = mm(bk[:, h * T:(h + 1) * T], QS[q.par][0:KSTK, 2 * hp + h, a * P:(a + 1) * P],
                             KS[q.par][0:KSTK, 2 * hp + h, :], start=True, stop=True)
                ins.then_inc(p_s, 1)

            def shifted(t, lc, pr):
                if pr == 0 and lc == 0:
                    pe.wait_ge(g_mask, 2 * (t.n + 1))
                if pr == 0 and isinstance(t.n, int) and t.n % NB == 0 and t.n < 2 * NB:
                    pe.wait_ge(s_ones, 32 * (lc + 1))
                if pr == 0 and lc == 1 and isinstance(t.n, int) and t.n == NB:
                    pe.wait_ge(v_const, DECAY_STEPS)
                    pe.wait_ge(s_drow, 64)
                rows = KSTK + NPART + (KDEC if lc == 1 else 0)
                wait(pe, a_exp, 8 * t.n + pr - 1)
                for h in range(2):
                    flat = PTT[pr % 2][:, h, :]
                    bk = flat.rearrange("p (a t) -> p a t", a=TT)
                    if lc == 0:
                        mm(bk, identb, BMK[t.par][:, 1], start=True, stop=True, skip_group_check=True)
                    for a in range(TT):
                        ins = mm(bk[:, a, :], KS[t.par][0:rows, 2 * pr + h, a * P:(a + 1) * P],
                                 QS[t.par][0:rows, 2 * pr + h, :],
                                 start=(lc == 2 or (lc == 1 and a == 0)), stop=True, skip_group_check=True)
                    if lc == 1:
                        for i in range(NPART):
                            ins = mm(flat.rearrange("p (x t) -> p x t", t=P)[:, 0:4:3, :], TDI[:, i, :], corr,
                                     start=False, stop=True, skip_group_check=True)
                ins.then_inc(p_st, 1)

            def weigh(t, pr):
                pe.wait_ge(a_exp, 8 * t.n + pr + 1)
                if pr % 2 == 0:
                    wait(pe, v_ot, HEAD_STEPS * t.n + (-3, 1, 2, 6)[pr // 2])
                for h in range(2):
                    g = (2 * pr + h) % 4
                    for a in range(TT):
                        ins = mm(PO[32 * g:32 * g + 32, 0:T], VA[t.par][:, a, 2 * pr + h, :], PT[pr % 2][:, h, a, :],
                                 start=(a == 0), stop=(a == TT - 1))
                ins.then_inc(p_pv, 1)

            def body(t, lp, la, ls, lc, lo):
                lr = routes(lo)
                z, q, y = t.next(3), t.next(2), t.next(-1)
                before = t.done(2) + 16 * t.done(1)
                projected = None if la is None else 3 * q.n
                if la is not None:
                    if isinstance(q.n, int) and q.n % NB == 0 and q.n < 2 * NB:
                        pe.wait_ge(s_w[la], 80)
                    if la == 2:
                        pe.wait_ge(g_xn, q.n - 2 * NB + 1)
                    else:
                        pe.wait_ge(v_xn, q.n + 1)
                    wait(pe, v_bank, before if isinstance(q.n, int) and q.n % NB == 0 and q.n < 2 * NB else before - 1)
                    wait(pe, a_bank, projected)
                    alone(pe)
                    for ct in range(CT):
                        for a in range(TT):
                            ins = nc.tensor.transpose(PS[0][:, ct * T + a * P:ct * T + (a + 1) * P], XNS[:, a, ct * P:(ct + 1) * P], ident)
                    ins.then_inc(p_a, 1)
                    wait(pe, v_bank, before)
                    project(q, la, 0)
                if lc is not None:
                    pe.wait_ge(v_nm, 6 * (t.n + 1))
                    alone(pe)
                    for a in range(TT):
                        ins = nc.tensor.transpose(nm_bf[:, a * P:(a + 1) * P],
                                                  NMP[:, a, :, :].rearrange("p i h -> p (i h)"), identb)
                    ins.then_inc(p_nm, 1)
                if la is not None:
                    project(q, la, 1)
                if lo is not None:
                    pe.wait_ge(v_ot, HEAD_STEPS * t.n)
                    for a in range(TT):
                        for i in range(PAIRS):
                            ins = mm(PM[:, a * C:(a + 1) * C], OT[:, i, a * P:(a + 1) * P], WO[lo % 2][:, i, :],
                                     start=(i == 0), stop=(i == PAIRS - 1))
                    ins.then_inc(p_wo, 1)
                if lc is not None:
                    pe.wait_ge(s_nml[t.par], 16 * (t.m + 1))
                    shifted(t, lc, 0)
                    for pr in range(NH // 2):
                        if pr + 1 < NH // 2:
                            shifted(t, lc, pr + 1)
                        if ls is not None:
                            scores(t.next(), pr, 0, before, projected)
                        weigh(t, pr)
                        if ls is not None:
                            scores(t.next(), pr, 1, before, projected)
                        if pr in (1, 3) and lp == 1:
                            combine(z, t, lo, pr // 2)
                        if lr is not None and pr == (5 if lr == 0 else 6):
                            router_turn(y, lr)
                        if lr is not None and pr == (6 if lr == 0 else 7):
                            router_logits(y, lr)
                else:
                    for hp in range(8):
                        if ls is not None:
                            for a in range(TT):
                                scores(t.next(), hp, a, before, projected)
                        if hp == 1 and lp == 1:
                            for a in range(TT):
                                combine(z, t, lo, a)
                    if lr is not None:
                        router_turn(y, lr)
                        router_logits(y, lr)
                if la is not None:
                    if ls is None:
                        pe.wait_ge(a_bank, projected + 2)
                    else:
                        pe.wait_ge(v_bank, before + 15)
                    values(q, la)
                if lp == 1:
                    pe.wait_ge(v_comb, z.n - NB + 1)
                elif lr is not None:
                    pe.wait_ge(v_log, routed(lr, y.n) + 1)

            def router_turn(z, layer):
                k = routed(layer, z.n)
                if layer == 2:
                    pe.wait_ge(g_xr, k + 1 - NB)
                else:
                    pe.wait_ge(v_xr, k + 1)
                pe.wait_ge(v_res, z.n + 1)
                for ct in range(CT):
                    for a in range(TT):
                        ins = nc.tensor.transpose(PM[:, ct * T + a * P:ct * T + (a + 1) * P], XRS[:, a, ct * P:(ct + 1) * P], ident)
                ins.then_inc(p_rt, 1)

            def router_logits(z, layer):
                k = routed(layer, z.n)
                if isinstance(z.n, int) and z.n == 0:
                    pe.wait_ge(s_gate, 16)
                pe.wait_ge(a_xrt, k + 1)
                for a in range(TT):
                    for ct in range(CT):
                        ins = mm(PM[:, a * NE:(a + 1) * NE], XRT[:, ct, a * P:(a + 1) * P], GATE[:, layer // 2, ct, :],
                                 start=(ct == 0), stop=(ct == CT - 1))
                ins.then_inc(p_log, 1)

            def combine(z, t, lo, a):
                b = z.batch(1)
                if a == 0:
                    if isinstance(z.n, int) and z.n == NB:
                        pe.wait_ge(v_y, ST * NE)
                    if lo is not None:
                        pe.wait_ge(v_res, t.n)
                    pe.wait_ge(v_wct, z.n - NB + 1)
                for i in range(NE // 2):
                    ins = mm(PM[:, a * C:(a + 1) * C], WCT[z.par][:, i, a * P:(a + 1) * P], yall[:, b * (NE // 2) + i, :],
                             start=(i == 0), stop=(i == NE // 2 - 1))
                if a == TT - 1:
                    ins.then_inc(p_comb, 1)

            attention_rounds_0(pe, body)
            pe.wait_ge(v_topk, 5)
            for a in range(TT):
                ins = nc.tensor.transpose(PM[0:NB * NE, a * P:(a + 1) * P], PR[:, a].rearrange("p b e -> p (b e)"), ident)
            ins.then_inc(p_topk, 1)
            pe.wait_ge(v_topk, TOPK_STEPS)
            for a in range(TT):
                ins = nc.tensor.transpose(PM[:, a * NB * NE:(a + 1) * NB * NE], POS[:, a * P:(a + 1) * P], ident[0:NB * NE, 0:NB * NE])
            ins.then_inc(p_topk, 1)
            def gather(m, par):
                b = 2 * m + par
                pe.wait_ge(a_xst, b + 1)
                pe.wait_ge(v_gsel, TT * (b + 1))
                for c in range(CT):
                    wait(pe, a_xi if c == 0 else v_xi, b - 1)
                    for a in range(TT):
                        ins = mm(PTT[par][:, c, :], XST[par][:, a, c * P:(c + 1) * P], GSEL[par][:, a].rearrange("p e s -> p (e s)"),
                                 start=(a == 0), stop=(a == TT - 1))
                    ins.then_inc(p_disp, 1)

            gather_rounds(pe, gather)
            pe.wait_ge(a_xi, NB)
            pe.wait_ge(v_xi, NB)

            def turn_inputs(m, par):
                e = 2 * m + par
                pe.wait_ge(s_zs[par], 16 * (m - NE // 2 + 1))
                for c in range(CT):
                    j = (uses(1) * par + c) % 4
                    wait(pe, a_h, use0(1, e) + c - 3)
                    for st in range(ST):
                        ins = nc.tensor.transpose(PTT[j // 2][:, j % 2, st * P:(st + 1) * P], ZS[par][:, st, c * P:(c + 1) * P], ident)
                    ins.then_inc(p_h, 1)

            def hidden(m, par, layer):
                e = 2 * m + par
                pe.wait_ge(s_w1[par], 16 * (m + 1))
                if layer == 1:
                    pe.wait_ge(a_h, use0(1, e) + CT)
                for f in range(FT):
                    k = use0(layer, e) + uses(layer) - FT + f
                    j = (uses(layer) * par + uses(layer) - FT + f) % 4
                    wait(pe, a_h, k - 3)
                    for c in range(CT):
                        rhs = xint[:, c, bass.ts(e, SLOT)] if layer == 0 else ZT[par][:, c, :]
                        ins = mm(PTT[j // 2][:, j % 2, :], W1[par][:, c, f * P:(f + 1) * P], rhs, start=(c == 0), stop=(c == CT - 1))
                    ins.then_inc(p_h, 1)

            def outputs(m, par, layer, st):
                e = 2 * m + par
                if st == 0:
                    pe.wait_ge(a_h, use0(layer, e + 1))
                    pe.wait_ge(s_w2[par], 16 * (m + 1))
                bk = (PS[0], PS[1], PO, PM)[st]
                wait(pe, v_y, ST * e + st - 3)
                for f in range(FT):
                    ins = mm(bk[:, 0:C], ht[:, par, f, st * P:(st + 1) * P], W2[par][:, f, :], start=(f == 0), stop=(f == FT - 1))
                ins.then_inc(p_y, 1)

            def step(layer):
                def go(m, par, last):
                    q = Turn(m, par)
                    if not last:
                        hidden(q.next().m, q.next().par, layer)
                    for st in range(ST):
                        outputs(m, par, layer, st)
                        if st == 2 and layer == 1 and not last and not (isinstance(m, int) and m > NE // 2 and par == 0):
                            turn_inputs(q.next(2).m, q.next(2).par)
                return go

            expert_rounds(pe, lambda: hidden(0, 0, 0), step(0), 0)
            attention_rounds_12(pe, body)
            pe.wait_ge(v_rt, PICK_STEPS)
            picks = PICK.rearrange("p k i e -> p (k i e)")
            mm(PS[0][:, 0:2 * NT * NE], tri, picks, start=True, stop=True).then_inc(p_rte, 1)
            mm(PS[1][:, 0:2 * NT * NE], ONES[:, :], picks, start=True, stop=True).then_inc(p_rte, 1)

            def first():
                turn_inputs(NE // 2, 0)
                hidden(NE // 2, 0, 1)
                turn_inputs(NE // 2, 1)
            expert_rounds(pe, first, step(1), 1)


def layout(inputs):
    import numpy as np

    a = {k: np.asarray(v) for k, v in inputs.items()}
    f32 = np.float32

    def heads(w):
        return w.reshape(*w.shape[:-1], NH // 2, CT, HD).swapaxes(-3, -2).swapaxes(-2, -1).reshape(w.shape)

    w3, wo, bos, bqk, bv = [], [], [], [], []
    for wq, wk, wv, w_o, bq, bk, b_v, bo in (
        [a[f"L0_xattn_{n}"] for n in ("Wq", "Wk", "Wv", "Wo", "bq", "bk", "bv", "bo")],
        [a[f"L1_xattn_{n}"].T for n in ("wq", "wk", "wv", "wo", "bq", "bk", "bv", "bo")],
        [a[f"L1_ffn_{n}"] for n in ("wq", "wk", "wv", "wo", "bq", "bk", "bv", "bo")],
    ):
        w3.append(np.stack([heads(wq), heads(wk), wv]))
        wo.append(w_o.reshape(PAIRS, 2, 4, HD, C).transpose(2, 1, 3, 0, 4).reshape(P, PAIRS, C))
        bos.append(bo)
        bqk.append(np.stack([heads(bq).reshape(CT, P), heads(bk).reshape(CT, P)]).transpose(2, 0, 1))
        bv.append(b_v)

    cf = np.zeros((P, NCF), f32)
    p = np.arange(P)

    def put(name, value):
        cf[:, CF[name][0]:CF[name][1]] = value

    put("ident", np.eye(P))
    put("tri", p[:, None] <= p[None, :])
    put("iota", np.arange(CAP0)[None, :])
    put("slot", (p % CAP0)[:, None])
    put("rev", NE - np.arange(NE)[None, :])
    put("base", SLOT * np.arange(NE)[None, :])
    put("keep", (np.arange(2 * NE * NT) % NT != 0)[None, :])
    put("token", 1 + p[:, None] + P * np.arange(NT)[None, :])
    put("place", p[:, None] + P * np.arange(ST)[None, :])
    put("part", p[:, None] % NPART == np.arange(NPART)[None, :])
    place = np.arange(T) - P
    s = np.where(place < 0, -1, 1)
    cd = np.zeros((KDEC, 2, 2, T), f32)
    cd[:NPART, 1, 0] = s * place
    cd[:NPART, 0, 1] = 1
    cd[NPART:, 0, 0] = -s
    cd[NPART:, 1, 1] = place
    d = np.arange(P)[None, :] - np.arange(P)[:, None]
    corr = np.concatenate([abs(d) + d, abs(d) - d], 1)
    k = np.arange(T)
    dist = np.abs((k[:, None] - k[None, :]).reshape(TT, P, T)).transpose(1, 0, 2).reshape(P, TT * T)
    bf16 = lambda v: (v.astype(f32).view(np.uint32) >> 16).astype(np.uint16)
    cb = bf16(np.concatenate([np.eye(P), dist, corr], 1))
    mask = a["mask_Bx1xSxS2_bf1"].reshape(NB, T, T)
    mask = np.stack([mask, mask.swapaxes(1, 2)], 1).view(np.uint8)
    c = np.ascontiguousarray
    return {
        "x": c(a["x"]), "ctxT": c(a["ctx_1024"].swapaxes(1, 2)), "maskp": c(mask), "cf": cf, "cb": cb, "cd": bf16(cd),
        "wqkv": c(np.stack(w3)), "wo": c(np.stack(wo)), "bo": c(np.stack(bos)), "bqk": c(np.stack(bqk)), "bv": c(np.stack(bv)),
        "gates": c(np.stack([a["L0_ffn_gate_w"], a["L1_ffn_wr"]])), "td": c(a["L1_xattn_time_decay"].reshape(1)),
        "lnp": c(np.stack([a[f"L1_ffn_ln{i}_{n}"] for i in (1, 2) for n in "gb"])),
        "w1": c(np.stack([a["L0_ffn_w1"], a["L1_ffn_w1"]])), "b1": c(a["L1_ffn_b1"].reshape(NE, FT, P).swapaxes(1, 2)),
        "w2": c(np.stack([a["L0_ffn_w2"], a["L1_ffn_w2"]])), "b2": c(a["L1_ffn_b2"]),
    }


def kernel(**inputs):
    import concourse.bacc as bacc
    from concourse.bass_utils import run_bass_kernel_spmd

    arrays = layout(inputs)
    nc = bacc.Bacc("TRN2", target_bir_lowering=False, num_devices=1)
    args = [nc.dram_tensor(f"in_{n}", v.shape, mybir.dt.from_np(v.dtype), kind="ExternalInput").ap() for n, v in arrays.items()]
    args.append(nc.dram_tensor("out_0", (NB, T, C), F32, kind="ExternalOutput").ap())
    bass_two_layer_cross_attention_moe(nc, *args)
    got = run_bass_kernel_spmd(nc, [{f"in_{n}": v for n, v in arrays.items()}], core_ids=[0])
    return got.results[0]["out_0"]
```
